# Optimizing a Trainium2 kernel written in Bass

```python
import numpy as np
import jax
import jax.numpy as jnp

def _softmax(x, axis=-1):
    return jax.nn.softmax(x, axis=axis)

def _gelu(x):
    return jax.nn.gelu(x, approximate=True)

def _silu(x):
    return jax.nn.silu(x)

def _sigmoid(x):
    return jax.nn.sigmoid(x)

def _layernorm(x, axis=-1, eps=1e-05):
    m = jnp.mean(x, axis=axis, keepdims=True)
    v = jnp.var(x, axis=axis, keepdims=True)
    return (x - m) / jnp.sqrt(v + eps)

def _scatter_add(tgt, idx, src, axis=0):
    return tgt.at[idx].add(src)

def _segment_sum(src, seg, n):
    return jax.ops.segment_sum(src, seg, n)
kernel_name = 'mk_gnn_ffn_d4_gnn_r32_e4e3f5'

def setup_inputs(seed: int=0):
    np.random.seed(seed)
    _w = jnp.asarray

    def _rec_inputs():
        import jax
        import jax.numpy as jnp
        _gk = jax.random.key(seed)
        x = -0.000364 + 1 * jax.random.normal(jax.random.fold_in(_gk, 1), (625, 768), jnp.float32)
        src = jax.random.randint(jax.random.fold_in(_gk, 2), (20000,), 0, 625, jnp.int32)
        dst = jax.random.randint(jax.random.fold_in(_gk, 3), (20000,), 0, 625, jnp.int32)
        _o = jnp.argsort(dst, stable=True)
        src = src[_o]
        dst = dst[_o]
        edge_type_3 = jax.random.randint(jax.random.fold_in(_gk, 13), (20000,), 0, 3, jnp.int32)
        return (x, src, dst, edge_type_3)
    x, src, dst, edge_type_3 = _rec_inputs()

    def _L0_gnn_setup():
        import jax, jax.numpy as jnp
        import numpy as np
        N, E, DIM, HEADS = (625, 10000, 768, 8)
        HD = DIM // HEADS
        EPS = 1e-05

        def layer_norm(x, w, b):
            mu = jnp.mean(x, axis=-1, keepdims=True)
            var = jnp.var(x, axis=-1, keepdims=True)
            return (x - mu) * jax.lax.rsqrt(var + EPS) * w + b

        def gatv2(x, src, dst, Ws, bs, Wd, bd, attn):
            H, D = attn.shape
            fs = (x @ Ws + bs).reshape(-1, H, D)
            fd = (x @ Wd + bd).reshape(-1, H, D)
            e = jax.nn.leaky_relu(fs[src] + fd[dst], 0.2)
            logits = jnp.einsum('ehd,hd->eh', e, attn)
            m = jax.ops.segment_max(logits, dst, num_segments=N)
            ex = jnp.exp(logits - m[dst])
            denom = jax.ops.segment_sum(ex, dst, num_segments=N)
            alpha = ex / denom[dst]
            out = jax.ops.segment_sum(alpha[:, :, None] * fs[src], dst, num_segments=N)
            return jax.nn.elu(out)
        key = jax.random.key(seed)
        ks = jax.random.split(key, 10)
        s = 1.0 / np.sqrt(DIM)
        return {'x': jax.random.normal(ks[0], (N, DIM), jnp.float32), 'src': jax.random.randint(ks[1], (E,), 0, N, jnp.int32), 'dst': jax.random.randint(ks[2], (E,), 0, N, jnp.int32), 'W1s': jax.random.normal(ks[3], (DIM, DIM), jnp.float32) * s, 'b1s': jnp.zeros((DIM,), jnp.float32), 'W1d': jax.random.normal(ks[4], (DIM, DIM), jnp.float32) * s, 'b1d': jnp.zeros((DIM,), jnp.float32), 'attn1': jax.random.normal(ks[5], (HEADS, HD), jnp.float32) * s, 'ln1_w': jnp.ones((DIM,), jnp.float32), 'ln1_b': jnp.zeros((DIM,), jnp.float32), 'Wos': jax.random.normal(ks[6], (DIM, DIM), jnp.float32) * s, 'bos': jnp.zeros((DIM,), jnp.float32), 'Wod': jax.random.normal(ks[7], (DIM, DIM), jnp.float32) * s, 'bod': jnp.zeros((DIM,), jnp.float32), 'attno': jax.random.normal(ks[8], (1, DIM), jnp.float32) * s, 'lno_w': jnp.ones((DIM,), jnp.float32), 'lno_b': jnp.zeros((DIM,), jnp.float32)}
    _L0_gnn_all = _L0_gnn_setup()
    _L0_gnn_in = {k: v for k, v in _L0_gnn_all.items() if k in ('W1s', 'b1s', 'W1d', 'b1d', 'attn1', 'ln1_w', 'ln1_b', 'Wos', 'bos', 'Wod', 'bod', 'attno', 'lno_w', 'lno_b')}
    del _L0_gnn_all

    def _L0_ffn_setup():
        import jax, jax.numpy as jnp
        import numpy as np
        B, S, D, F, E = (8, 64, 768, 96, 16)
        CAP = 64
        EPS = 1e-06

        def _switch_moe_block(x, ln_w, w_router, wi, wo):
            var = jnp.mean(jnp.square(x.astype(jnp.float32)), axis=-1, keepdims=True)
            normed = (x * jax.lax.rsqrt(var + EPS)).astype(x.dtype) * ln_w
            logits = jnp.einsum('bsd,de->bse', normed.astype(jnp.float32), w_router.astype(jnp.float32))
            probs = jax.nn.softmax(logits, axis=-1)
            expert_idx = jnp.argmax(probs, axis=-1)
            onehot = jax.nn.one_hot(expert_idx, E, dtype=jnp.float32)
            priority = jnp.cumsum(onehot, axis=1)
            keep = onehot * (priority <= CAP)
            pos = (priority - 1.0).astype(jnp.int32)
            dispatch = keep[..., None] * jax.nn.one_hot(pos, CAP, dtype=jnp.float32)
            expert_in = jnp.einsum('bsec,bsd->becd', dispatch, normed)
            h = jax.nn.relu(jnp.einsum('becd,edf->becf', expert_in, wi))
            expert_out = jnp.einsum('becf,efd->becd', h, wo)
            combined = jnp.einsum('bsec,becd->bsd', dispatch, expert_out)
            routed = jnp.sum(dispatch, axis=(2, 3)) > 0
            next_states = jnp.where(routed[..., None], combined.astype(x.dtype), normed)
            router_prob = jnp.max(probs, axis=-1, keepdims=True).astype(x.dtype)
            return x + router_prob * next_states
        key = jax.random.key(seed)
        k_x, k_r, k_wi, k_wo = jax.random.split(key, 4)
        x = jax.random.normal(k_x, (B, S, D), dtype=jnp.float32)
        ln_w = jnp.ones((D,), dtype=jnp.float32)
        w_router = jax.random.normal(k_r, (D, E), dtype=jnp.float32) * 0.02
        wi = jax.random.normal(k_wi, (E, D, F), dtype=jnp.float32) * D ** (-0.5)
        wo = jax.random.normal(k_wo, (E, F, D), dtype=jnp.float32) * F ** (-0.5)
        return {'x': x, 'ln_w': ln_w, 'w_router': w_router, 'wi': wi, 'wo': wo}
    _L0_ffn_all = _L0_ffn_setup()
    _L0_ffn_in = {k: v for k, v in _L0_ffn_all.items() if k in ('ln_w', 'w_router', 'wi', 'wo')}
    del _L0_ffn_all

    def _L1_gnn_setup():
        import jax, jax.numpy as jnp
        import numpy as np
        N_NODES = 10000
        NEG_SLOPE = 0.2
        EPS = 1e-16

        def gat_layer(x, W, att_src, att_dst, bias, src, dst, heads, out_ch, concat):
            n = x.shape[0]
            h = (x @ W.T).reshape(n, heads, out_ch)
            a_src = jnp.einsum('nhc,hc->nh', h, att_src)
            a_dst = jnp.einsum('nhc,hc->nh', h, att_dst)
            e = a_src[src] + a_dst[dst]
            e = jax.nn.leaky_relu(e, NEG_SLOPE)
            m = jax.ops.segment_max(e, dst, num_segments=n)
            ex = jnp.exp(e - m[dst])
            denom = jax.ops.segment_sum(ex, dst, num_segments=n)
            alpha = ex / (denom[dst] + EPS)
            msg = alpha[:, :, None] * h[src]
            out = jax.ops.segment_sum(msg, dst, num_segments=n)
            if concat:
                out = out.reshape(n, heads * out_ch)
            else:
                out = out.mean(axis=1)
            return out + bias
        key = jax.random.key(seed)
        ks = jax.random.split(key, 12)
        x = jax.random.normal(ks[0], (N_NODES, 768), dtype=jnp.float32)
        edge_index = jax.random.randint(ks[1], (2, 5000), 0, N_NODES, dtype=jnp.int64)
        s1 = 1.0 / np.sqrt(768.0)
        W1 = jax.random.normal(ks[2], (8 * 128, 768), dtype=jnp.float32) * s1
        att_src1 = jax.random.normal(ks[3], (8, 128), dtype=jnp.float32) * (1.0 / np.sqrt(128.0))
        att_dst1 = jax.random.normal(ks[4], (8, 128), dtype=jnp.float32) * (1.0 / np.sqrt(128.0))
        b1 = jnp.zeros((8 * 128,), dtype=jnp.float32)
        s2 = 1.0 / np.sqrt(1024.0)
        W2 = jax.random.normal(ks[5], (1 * 768, 1024), dtype=jnp.float32) * s2
        att_src2 = jax.random.normal(ks[6], (1, 768), dtype=jnp.float32) * (1.0 / np.sqrt(768.0))
        att_dst2 = jax.random.normal(ks[7], (1, 768), dtype=jnp.float32) * (1.0 / np.sqrt(768.0))
        b2 = jnp.zeros((768,), dtype=jnp.float32)
        return {'x': x, 'edge_index': edge_index, 'W1': W1, 'att_src1': att_src1, 'att_dst1': att_dst1, 'b1': b1, 'W2': W2, 'att_src2': att_src2, 'att_dst2': att_dst2, 'b2': b2}
    _L1_gnn_all = _L1_gnn_setup()
    _L1_gnn_in = {k: v for k, v in _L1_gnn_all.items() if k in ('W1', 'att_src1', 'att_dst1', 'b1', 'W2', 'att_src2', 'att_dst2', 'b2')}
    del _L1_gnn_all

    def _L1_ffn_setup():
        import jax, jax.numpy as jnp
        import numpy as np
        QN, QP = (-8, 7)

        def round_pass(x):
            return x + jax.lax.stop_gradient(jnp.round(x) - x)

        def _quant_act(x, alpha_a):
            a = alpha_a.mean()
            return round_pass(jnp.clip(x / a, QN, QP))

        def _quant_w(w, alpha_w):
            return round_pass(jnp.clip(w / alpha_w[:, None], QN, QP))
        key = jax.random.key(seed)
        ks = jax.random.split(key, 9)
        B, S, D, H = (16, 1024, 768, 96)

        def unif(k, shape):
            return jax.random.uniform(k, shape, jnp.float32, 0.02, 0.1)
        return {'x0': jax.random.normal(ks[0], (B, S, D), jnp.float32), 'w1': jax.random.normal(ks[1], (H, D), jnp.float32) * 0.02, 'b1': jax.random.normal(ks[2], (H,), jnp.float32) * 0.02, 'alpha_w1': unif(ks[3], (H,)), 'alpha_a1': unif(ks[4], (D,)), 'w2': jax.random.normal(ks[5], (D, H), jnp.float32) * 0.02, 'b2': jax.random.normal(ks[6], (D,), jnp.float32) * 0.02, 'alpha_w2': unif(ks[7], (D,)), 'alpha_a2': unif(ks[8], (H,))}
    _L1_ffn_all = _L1_ffn_setup()
    _L1_ffn_in = {k: v for k, v in _L1_ffn_all.items() if k in ('w1', 'b1', 'alpha_w1', 'alpha_a1', 'w2', 'b2', 'alpha_w2', 'alpha_a2')}
    del _L1_ffn_all

    def _L2_gnn_setup():
        import jax, jax.numpy as jnp
        import numpy as np
        NEG_SLOPE = 0.2
        EPS = 1e-16
        N_NODES = 1024
        N_EDGES = 5000
        DIM = 768
        HEADS1 = 4
        OUT1 = DIM // HEADS1
        HEADS2 = 1
        OUT2 = DIM
        N_REL = 3

        def rgat_conv(x, W, q, k, b, src, dst, etype, heads, out_ch, n_nodes):
            xr = jnp.einsum('nd,rdf->rnf', x, W)
            oi = xr[etype, dst]
            oj = xr[etype, src]
            qi = oi @ q
            kj = oj @ k
            alpha = jax.nn.leaky_relu(qi + kj, NEG_SLOPE)
            m = jax.ops.segment_max(alpha, dst, num_segments=n_nodes)
            e = jnp.exp(alpha - m[dst])
            z = jax.ops.segment_sum(e, dst, num_segments=n_nodes)
            a = e / (z[dst] + EPS)
            msg = (a[:, :, None] * oj.reshape(-1, heads, out_ch)).reshape(-1, heads * out_ch)
            out = jax.ops.segment_sum(msg, dst, num_segments=n_nodes)
            return out + b
        key = jax.random.key(seed)
        ks = jax.random.split(key, 12)
        s = 0.02
        return {'x': jax.random.normal(ks[0], (N_NODES, DIM), dtype=jnp.float32), 'edge_index': jax.random.randint(ks[1], (2, N_EDGES), 0, N_NODES, dtype=jnp.int64), 'edge_type': jax.random.randint(ks[2], (N_EDGES,), 0, N_REL, dtype=jnp.int64), 'W1': jax.random.normal(ks[3], (N_REL, DIM, HEADS1 * OUT1), dtype=jnp.float32) * s, 'q1': jax.random.normal(ks[4], (HEADS1 * OUT1, HEADS1), dtype=jnp.float32) * s, 'k1': jax.random.normal(ks[5], (HEADS1 * OUT1, HEADS1), dtype=jnp.float32) * s, 'b1': jnp.zeros((HEADS1 * OUT1,), dtype=jnp.float32), 'W2': jax.random.normal(ks[6], (N_REL, DIM, HEADS2 * OUT2), dtype=jnp.float32) * s, 'q2': jax.random.normal(ks[7], (HEADS2 * OUT2, HEADS2), dtype=jnp.float32) * s, 'k2': jax.random.normal(ks[8], (HEADS2 * OUT2, HEADS2), dtype=jnp.float32) * s, 'b2': jnp.zeros((HEADS2 * OUT2,), dtype=jnp.float32)}
    _L2_gnn_all = _L2_gnn_setup()
    _L2_gnn_in = {k: v for k, v in _L2_gnn_all.items() if k in ('W1', 'q1', 'k1', 'b1', 'W2', 'q2', 'k2', 'b2')}
    del _L2_gnn_all

    def _L2_ffn_setup():
        import jax, jax.numpy as jnp
        import numpy as np
        E, TOPK = (32, 2)
        D, HID, BOT, OUT = (768, 64, 256, 768)
        B, S = (2, 128)
        key = jax.random.key(seed)
        ks = jax.random.split(key, 7)
        p = lambda k, shape: jax.random.normal(k, shape, dtype=jnp.float32) * 0.02
        return {'x': jax.random.normal(ks[0], (B, S, D), dtype=jnp.float32), 'gate_w': p(ks[1], (E, D)), 'W1': p(ks[2], (E, D, HID)), 'b1': jnp.zeros((E, HID), jnp.float32), 'W2': p(ks[3], (E, HID, HID)), 'b2': jnp.zeros((E, HID), jnp.float32), 'W3': p(ks[4], (E, HID, BOT)), 'b3': jnp.zeros((E, BOT), jnp.float32), 'Wl': p(ks[5], (E, BOT, OUT)), 'bl': jnp.zeros((E, OUT), jnp.float32)}
    _L2_ffn_all = _L2_ffn_setup()
    _L2_ffn_in = {k: v for k, v in _L2_ffn_all.items() if k in ('gate_w', 'W1', 'b1', 'W2', 'b2', 'W3', 'b3', 'Wl', 'bl')}
    del _L2_ffn_all

    def _L3_gnn_setup():
        import jax, jax.numpy as jnp
        import numpy as np
        N_NODES = 10000
        D = 768
        N_EDGES = 5000

        def gcn_conv(x, W, b, src, dst, n_nodes):
            h = x @ W
            deg = jax.ops.segment_sum(jnp.ones_like(dst, dtype=h.dtype), dst, num_segments=n_nodes)
            dinv = jnp.where(deg > 0, jax.lax.rsqrt(deg), 0.0)
            norm = dinv[src] * dinv[dst]
            msgs = h[src] * norm[:, None]
            out = jax.ops.segment_sum(msgs, dst, num_segments=n_nodes)
            return out + b

        def add_self_loops(edge_index, n_nodes):
            loop = jnp.arange(n_nodes, dtype=edge_index.dtype)
            src = jnp.concatenate([edge_index[0], loop])
            dst = jnp.concatenate([edge_index[1], loop])
            return (src, dst)
        key = jax.random.key(seed)
        k1, k2, k3, k4 = jax.random.split(key, 4)
        x = jax.random.normal(k1, (N_NODES, D), dtype=jnp.float32)
        edge_index = jax.random.randint(k2, (2, N_EDGES), 0, N_NODES, dtype=jnp.int32)
        glorot = float(np.sqrt(6.0 / (D + D)))
        W1 = jax.random.uniform(k3, (D, D), jnp.float32, -glorot, glorot)
        W2 = jax.random.uniform(k4, (D, D), jnp.float32, -glorot, glorot)
        b1 = jnp.zeros((D,), jnp.float32)
        b2 = jnp.zeros((D,), jnp.float32)
        return {'x': x, 'W1': W1, 'b1': b1, 'W2': W2, 'b2': b2, 'edge_index': edge_index}
    _L3_gnn_all = _L3_gnn_setup()
    _L3_gnn_in = {k: v for k, v in _L3_gnn_all.items() if k in ('W1', 'b1', 'W2', 'b2')}
    del _L3_gnn_all

    def _L3_ffn_setup():
        import jax, jax.numpy as jnp
        import numpy as np
        B, S, D = (4, 1024, 768)
        E = 8
        H = 768
        HS = 96
        TOPK_ROUTED = 2
        key = jax.random.key(seed)
        ks = jax.random.split(key, 10)
        w = lambda k, shape: jax.random.normal(k, shape, dtype=jnp.float32) * 0.02
        return {'x': jax.random.normal(ks[0], (B, S, D), dtype=jnp.float32), 'router_w': w(ks[1], (D, E)), 'w_gate': w(ks[2], (E, D, H)), 'w_up': w(ks[3], (E, D, H)), 'w_down': w(ks[4], (E, H, D)), 'ws_gate': w(ks[5], (D, HS)), 'ws_up': w(ks[6], (D, HS)), 'ws_down': w(ks[7], (HS, D)), 'sg_w': w(ks[8], (D, 1)), 'sg_b': jnp.zeros((1,), jnp.float32)}
    _L3_ffn_all = _L3_ffn_setup()
    _L3_ffn_in = {k: v for k, v in _L3_ffn_all.items() if k in ('router_w', 'w_gate', 'w_up', 'w_down', 'ws_gate', 'ws_up', 'ws_down', 'sg_w', 'sg_b')}
    del _L3_ffn_all
    return {'x': x, 'src': src, 'dst': dst, 'edge_type_3': edge_type_3, 'L0_gnn_W1s': _L0_gnn_in['W1s'], 'L0_gnn_b1s': _L0_gnn_in['b1s'], 'L0_gnn_W1d': _L0_gnn_in['W1d'], 'L0_gnn_b1d': _L0_gnn_in['b1d'], 'L0_gnn_attn1': _L0_gnn_in['attn1'], 'L0_gnn_ln1_w': _L0_gnn_in['ln1_w'], 'L0_gnn_ln1_b': _L0_gnn_in['ln1_b'], 'L0_gnn_Wos': _L0_gnn_in['Wos'], 'L0_gnn_bos': _L0_gnn_in['bos'], 'L0_gnn_Wod': _L0_gnn_in['Wod'], 'L0_gnn_bod': _L0_gnn_in['bod'], 'L0_gnn_attno': _L0_gnn_in['attno'], 'L0_gnn_lno_w': _L0_gnn_in['lno_w'], 'L0_gnn_lno_b': _L0_gnn_in['lno_b'], 'L0_ffn_ln_w': _L0_ffn_in['ln_w'], 'L0_ffn_w_router': _L0_ffn_in['w_router'], 'L0_ffn_wi': _L0_ffn_in['wi'], 'L0_ffn_wo': _L0_ffn_in['wo'], 'L1_gnn_W1': _L1_gnn_in['W1'], 'L1_gnn_att_src1': _L1_gnn_in['att_src1'], 'L1_gnn_att_dst1': _L1_gnn_in['att_dst1'], 'L1_gnn_b1': _L1_gnn_in['b1'], 'L1_gnn_W2': _L1_gnn_in['W2'], 'L1_gnn_att_src2': _L1_gnn_in['att_src2'], 'L1_gnn_att_dst2': _L1_gnn_in['att_dst2'], 'L1_gnn_b2': _L1_gnn_in['b2'], 'L1_ffn_w1': _L1_ffn_in['w1'], 'L1_ffn_b1': _L1_ffn_in['b1'], 'L1_ffn_alpha_w1': _L1_ffn_in['alpha_w1'], 'L1_ffn_alpha_a1': _L1_ffn_in['alpha_a1'], 'L1_ffn_w2': _L1_ffn_in['w2'], 'L1_ffn_b2': _L1_ffn_in['b2'], 'L1_ffn_alpha_w2': _L1_ffn_in['alpha_w2'], 'L1_ffn_alpha_a2': _L1_ffn_in['alpha_a2'], 'L2_gnn_W1': _L2_gnn_in['W1'], 'L2_gnn_q1': _L2_gnn_in['q1'], 'L2_gnn_k1': _L2_gnn_in['k1'], 'L2_gnn_b1': _L2_gnn_in['b1'], 'L2_gnn_W2': _L2_gnn_in['W2'], 'L2_gnn_q2': _L2_gnn_in['q2'], 'L2_gnn_k2': _L2_gnn_in['k2'], 'L2_gnn_b2': _L2_gnn_in['b2'], 'L2_ffn_gate_w': _L2_ffn_in['gate_w'], 'L2_ffn_W1': _L2_ffn_in['W1'], 'L2_ffn_b1': _L2_ffn_in['b1'], 'L2_ffn_W2': _L2_ffn_in['W2'], 'L2_ffn_b2': _L2_ffn_in['b2'], 'L2_ffn_W3': _L2_ffn_in['W3'], 'L2_ffn_b3': _L2_ffn_in['b3'], 'L2_ffn_Wl': _L2_ffn_in['Wl'], 'L2_ffn_bl': _L2_ffn_in['bl'], 'L3_gnn_W1': _L3_gnn_in['W1'], 'L3_gnn_b1': _L3_gnn_in['b1'], 'L3_gnn_W2': _L3_gnn_in['W2'], 'L3_gnn_b2': _L3_gnn_in['b2'], 'L3_ffn_router_w': _L3_ffn_in['router_w'], 'L3_ffn_w_gate': _L3_ffn_in['w_gate'], 'L3_ffn_w_up': _L3_ffn_in['w_up'], 'L3_ffn_w_down': _L3_ffn_in['w_down'], 'L3_ffn_ws_gate': _L3_ffn_in['ws_gate'], 'L3_ffn_ws_up': _L3_ffn_in['ws_up'], 'L3_ffn_ws_down': _L3_ffn_in['ws_down'], 'L3_ffn_sg_w': _L3_ffn_in['sg_w'], 'L3_ffn_sg_b': _L3_ffn_in['sg_b']}

def reference(x, src, dst, edge_type_3, L0_gnn_W1s, L0_gnn_b1s, L0_gnn_W1d, L0_gnn_b1d, L0_gnn_attn1, L0_gnn_ln1_w, L0_gnn_ln1_b, L0_gnn_Wos, L0_gnn_bos, L0_gnn_Wod, L0_gnn_bod, L0_gnn_attno, L0_gnn_lno_w, L0_gnn_lno_b, L0_ffn_ln_w, L0_ffn_w_router, L0_ffn_wi, L0_ffn_wo, L1_gnn_W1, L1_gnn_att_src1, L1_gnn_att_dst1, L1_gnn_b1, L1_gnn_W2, L1_gnn_att_src2, L1_gnn_att_dst2, L1_gnn_b2, L1_ffn_w1, L1_ffn_b1, L1_ffn_alpha_w1, L1_ffn_alpha_a1, L1_ffn_w2, L1_ffn_b2, L1_ffn_alpha_w2, L1_ffn_alpha_a2, L2_gnn_W1, L2_gnn_q1, L2_gnn_k1, L2_gnn_b1, L2_gnn_W2, L2_gnn_q2, L2_gnn_k2, L2_gnn_b2, L2_ffn_gate_w, L2_ffn_W1, L2_ffn_b1, L2_ffn_W2, L2_ffn_b2, L2_ffn_W3, L2_ffn_b3, L2_ffn_Wl, L2_ffn_bl, L3_gnn_W1, L3_gnn_b1, L3_gnn_W2, L3_gnn_b2, L3_ffn_router_w, L3_ffn_w_gate, L3_ffn_w_up, L3_ffn_w_down, L3_ffn_ws_gate, L3_ffn_ws_up, L3_ffn_ws_down, L3_ffn_sg_w, L3_ffn_sg_b):
    import jax
    import jax.numpy as jnp

    def _L0_gnn_ref(x, src, dst, W1s, b1s, W1d, b1d, attn1, ln1_w, ln1_b, Wos, bos, Wod, bod, attno, lno_w, lno_b):
        import jax, jax.numpy as jnp
        import numpy as np
        N, E, DIM, HEADS = (625, 10000, 768, 8)
        HD = DIM // HEADS
        EPS = 1e-05

        def layer_norm(x, w, b):
            mu = jnp.mean(x, axis=-1, keepdims=True)
            var = jnp.var(x, axis=-1, keepdims=True)
            return (x - mu) * jax.lax.rsqrt(var + EPS) * w + b

        def gatv2(x, src, dst, Ws, bs, Wd, bd, attn):
            H, D = attn.shape
            fs = (x @ Ws + bs).reshape(-1, H, D)
            fd = (x @ Wd + bd).reshape(-1, H, D)
            e = jax.nn.leaky_relu(fs[src] + fd[dst], 0.2)
            logits = jnp.einsum('ehd,hd->eh', e, attn)
            m = jax.ops.segment_max(logits, dst, num_segments=N)
            ex = jnp.exp(logits - m[dst])
            denom = jax.ops.segment_sum(ex, dst, num_segments=N)
            alpha = ex / denom[dst]
            out = jax.ops.segment_sum(alpha[:, :, None] * fs[src], dst, num_segments=N)
            return jax.nn.elu(out)
        h = gatv2(x, src, dst, W1s, b1s, W1d, b1d, attn1).reshape(N, DIM)
        h = layer_norm(h + x, ln1_w, ln1_b)
        out = gatv2(h, src, dst, Wos, bos, Wod, bod, attno).reshape(N, DIM)
        return layer_norm(out, lno_w, lno_b)

    def _L0_ffn_ref(x, ln_w, w_router, wi, wo):
        import jax, jax.numpy as jnp
        import numpy as np
        B, S, D, F, E = (8, 64, 768, 96, 16)
        CAP = 64
        EPS = 1e-06

        def _switch_moe_block(x, ln_w, w_router, wi, wo):
            var = jnp.mean(jnp.square(x.astype(jnp.float32)), axis=-1, keepdims=True)
            normed = (x * jax.lax.rsqrt(var + EPS)).astype(x.dtype) * ln_w
            logits = jnp.einsum('bsd,de->bse', normed.astype(jnp.float32), w_router.astype(jnp.float32))
            probs = jax.nn.softmax(logits, axis=-1)
            expert_idx = jnp.argmax(probs, axis=-1)
            onehot = jax.nn.one_hot(expert_idx, E, dtype=jnp.float32)
            priority = jnp.cumsum(onehot, axis=1)
            keep = onehot * (priority <= CAP)
            pos = (priority - 1.0).astype(jnp.int32)
            dispatch = keep[..., None] * jax.nn.one_hot(pos, CAP, dtype=jnp.float32)
            expert_in = jnp.einsum('bsec,bsd->becd', dispatch, normed)
            h = jax.nn.relu(jnp.einsum('becd,edf->becf', expert_in, wi))
            expert_out = jnp.einsum('becf,efd->becd', h, wo)
            combined = jnp.einsum('bsec,becd->bsd', dispatch, expert_out)
            routed = jnp.sum(dispatch, axis=(2, 3)) > 0
            next_states = jnp.where(routed[..., None], combined.astype(x.dtype), normed)
            router_prob = jnp.max(probs, axis=-1, keepdims=True).astype(x.dtype)
            return x + router_prob * next_states
        return _switch_moe_block(x, ln_w, w_router, wi, wo)

    def _L1_gnn_ref(x, edge_index, W1, att_src1, att_dst1, b1, W2, att_src2, att_dst2, b2):
        import jax, jax.numpy as jnp
        import numpy as np
        N_NODES = 10000
        NEG_SLOPE = 0.2
        EPS = 1e-16

        def gat_layer(x, W, att_src, att_dst, bias, src, dst, heads, out_ch, concat):
            n = x.shape[0]
            h = (x @ W.T).reshape(n, heads, out_ch)
            a_src = jnp.einsum('nhc,hc->nh', h, att_src)
            a_dst = jnp.einsum('nhc,hc->nh', h, att_dst)
            e = a_src[src] + a_dst[dst]
            e = jax.nn.leaky_relu(e, NEG_SLOPE)
            m = jax.ops.segment_max(e, dst, num_segments=n)
            ex = jnp.exp(e - m[dst])
            denom = jax.ops.segment_sum(ex, dst, num_segments=n)
            alpha = ex / (denom[dst] + EPS)
            msg = alpha[:, :, None] * h[src]
            out = jax.ops.segment_sum(msg, dst, num_segments=n)
            if concat:
                out = out.reshape(n, heads * out_ch)
            else:
                out = out.mean(axis=1)
            return out + bias
        src, dst = (edge_index[0], edge_index[1])
        h = gat_layer(x, W1, att_src1, att_dst1, b1, src, dst, heads=8, out_ch=128, concat=True)
        h = jax.nn.relu(h)
        out = gat_layer(h, W2, att_src2, att_dst2, b2, src, dst, heads=1, out_ch=768, concat=True)
        return out

    def _L1_ffn_ref(x0, w1, b1, alpha_w1, alpha_a1, w2, b2, alpha_w2, alpha_a2):
        import jax, jax.numpy as jnp
        import numpy as np
        QN, QP = (-8, 7)

        def round_pass(x):
            return x + jax.lax.stop_gradient(jnp.round(x) - x)

        def _quant_act(x, alpha_a):
            a = alpha_a.mean()
            return round_pass(jnp.clip(x / a, QN, QP))

        def _quant_w(w, alpha_w):
            return round_pass(jnp.clip(w / alpha_w[:, None], QN, QP))
        xq = _quant_act(x0, alpha_a1)
        wq1 = _quant_w(w1, alpha_w1)
        x1 = jnp.einsum('bsd,hd->bsh', xq, wq1)
        x1 = x1 * alpha_w1 * alpha_a1.mean() + b1
        x1 = jax.nn.gelu(x1, approximate=False)
        x1 = jnp.clip(x1, -10.0, 10.0)
        hq = _quant_act(x1, alpha_a2)
        wq2 = _quant_w(w2, alpha_w2)
        x2 = jnp.einsum('bsh,dh->bsd', hq, wq2)
        x2 = x2 * alpha_w2 * alpha_a2.mean() + b2
        return x2

    def _L2_gnn_ref(x, edge_index, edge_type, W1, q1, k1, b1, W2, q2, k2, b2):
        import jax, jax.numpy as jnp
        import numpy as np
        NEG_SLOPE = 0.2
        EPS = 1e-16
        N_NODES = 1024
        N_EDGES = 5000
        DIM = 768
        HEADS1 = 4
        OUT1 = DIM // HEADS1
        HEADS2 = 1
        OUT2 = DIM
        N_REL = 3

        def rgat_conv(x, W, q, k, b, src, dst, etype, heads, out_ch, n_nodes):
            xr = jnp.einsum('nd,rdf->rnf', x, W)
            oi = xr[etype, dst]
            oj = xr[etype, src]
            qi = oi @ q
            kj = oj @ k
            alpha = jax.nn.leaky_relu(qi + kj, NEG_SLOPE)
            m = jax.ops.segment_max(alpha, dst, num_segments=n_nodes)
            e = jnp.exp(alpha - m[dst])
            z = jax.ops.segment_sum(e, dst, num_segments=n_nodes)
            a = e / (z[dst] + EPS)
            msg = (a[:, :, None] * oj.reshape(-1, heads, out_ch)).reshape(-1, heads * out_ch)
            out = jax.ops.segment_sum(msg, dst, num_segments=n_nodes)
            return out + b
        src, dst = (edge_index[0], edge_index[1])
        n = x.shape[0]
        h = rgat_conv(x, W1, q1, k1, b1, src, dst, edge_type, HEADS1, OUT1, n)
        h = jax.nn.elu(h)
        out = rgat_conv(h, W2, q2, k2, b2, src, dst, edge_type, HEADS2, OUT2, n)
        return out

    def _L2_ffn_ref(x, gate_w, W1, b1, W2, b2, W3, b3, Wl, bl):
        import jax, jax.numpy as jnp
        import numpy as np
        E, TOPK = (32, 2)
        D, HID, BOT, OUT = (768, 64, 256, 768)
        B, S = (2, 128)
        Bz, Sl, d = x.shape
        xt = x.reshape(-1, d)
        scores = jax.nn.softmax(xt @ gate_w.T, axis=-1)
        topk_w, topk_idx = jax.lax.top_k(scores, TOPK)
        topk_w = topk_w / (topk_w.sum(-1, keepdims=True) + 1e-20)
        gelu = lambda v: jax.nn.gelu(v, approximate=False)
        h = gelu(jnp.einsum('nd,edh->enh', xt, W1) + b1[:, None, :])
        h = gelu(jnp.einsum('enh,ehg->eng', h, W2) + b2[:, None, :])
        z = jnp.einsum('eng,egb->enb', h, W3) + b3[:, None, :]
        out_all = jnp.einsum('enb,ebo->eno', z, Wl) + bl[:, None, :]
        sel = jnp.take_along_axis(out_all.transpose(1, 0, 2), topk_idx[:, :, None], axis=1)
        y = (sel * topk_w[:, :, None]).sum(axis=1)
        return y.reshape(Bz, Sl, OUT)

    def _L3_gnn_ref(x, W1, b1, W2, b2, edge_index):
        import jax, jax.numpy as jnp
        import numpy as np
        N_NODES = 10000
        D = 768
        N_EDGES = 5000

        def gcn_conv(x, W, b, src, dst, n_nodes):
            h = x @ W
            deg = jax.ops.segment_sum(jnp.ones_like(dst, dtype=h.dtype), dst, num_segments=n_nodes)
            dinv = jnp.where(deg > 0, jax.lax.rsqrt(deg), 0.0)
            norm = dinv[src] * dinv[dst]
            msgs = h[src] * norm[:, None]
            out = jax.ops.segment_sum(msgs, dst, num_segments=n_nodes)
            return out + b

        def add_self_loops(edge_index, n_nodes):
            loop = jnp.arange(n_nodes, dtype=edge_index.dtype)
            src = jnp.concatenate([edge_index[0], loop])
            dst = jnp.concatenate([edge_index[1], loop])
            return (src, dst)
        n = x.shape[0]
        src, dst = add_self_loops(edge_index, n)
        h = gcn_conv(x, W1, b1, src, dst, n)
        h = jax.nn.relu(h)
        out = gcn_conv(h, W2, b2, src, dst, n)
        return out

    def _L3_ffn_ref(x, router_w, w_gate, w_up, w_down, ws_gate, ws_up, ws_down, sg_w, sg_b):
        import jax, jax.numpy as jnp
        import numpy as np
        B, S, D = (4, 1024, 768)
        E = 8
        H = 768
        HS = 96
        TOPK_ROUTED = 2
        probs = jax.nn.softmax(x @ router_w, axis=-1)
        gates, idx = jax.lax.top_k(probs, TOPK_ROUTED)
        gates = gates / jnp.sum(gates, axis=-1, keepdims=True)
        n_exp = router_w.shape[1]
        dense_g = jnp.sum(jax.nn.one_hot(idx, n_exp, dtype=x.dtype) * gates[..., None], axis=-2)
        g = jax.nn.silu(jnp.einsum('bsd,edh->bseh', x, w_gate))
        u = jnp.einsum('bsd,edh->bseh', x, w_up)
        expert_out = jnp.einsum('bseh,ehd->bsed', g * u, w_down)
        routed = jnp.einsum('bse,bsed->bsd', dense_g, expert_out)
        shared = jax.nn.silu(x @ ws_gate) * (x @ ws_up) @ ws_down
        alpha = jax.nn.sigmoid(x @ sg_w + sg_b)
        return alpha * shared + (1.0 - alpha) * routed
    edge_index = jnp.stack([src, dst])
    x = x + _L0_gnn_ref(_layernorm(x, axis=-1), src, dst, L0_gnn_W1s, L0_gnn_b1s, L0_gnn_W1d, L0_gnn_b1d, L0_gnn_attn1, L0_gnn_ln1_w, L0_gnn_ln1_b, L0_gnn_Wos, L0_gnn_bos, L0_gnn_Wod, L0_gnn_bod, L0_gnn_attno, L0_gnn_lno_w, L0_gnn_lno_b)
    x = x + _L0_ffn_ref(_layernorm(x, axis=-1)[None], L0_ffn_ln_w, L0_ffn_w_router, L0_ffn_wi, L0_ffn_wo)[0]
    x = x + _L1_gnn_ref(_layernorm(x, axis=-1), edge_index, L1_gnn_W1, L1_gnn_att_src1, L1_gnn_att_dst1, L1_gnn_b1, L1_gnn_W2, L1_gnn_att_src2, L1_gnn_att_dst2, L1_gnn_b2)
    x = x + _L1_ffn_ref(_layernorm(x, axis=-1)[None], L1_ffn_w1, L1_ffn_b1, L1_ffn_alpha_w1, L1_ffn_alpha_a1, L1_ffn_w2, L1_ffn_b2, L1_ffn_alpha_w2, L1_ffn_alpha_a2)[0]
    x = x + _L2_gnn_ref(_layernorm(x, axis=-1), edge_index, edge_type_3, L2_gnn_W1, L2_gnn_q1, L2_gnn_k1, L2_gnn_b1, L2_gnn_W2, L2_gnn_q2, L2_gnn_k2, L2_gnn_b2)
    x = x + _L2_ffn_ref(_layernorm(x, axis=-1)[None], L2_ffn_gate_w, L2_ffn_W1, L2_ffn_b1, L2_ffn_W2, L2_ffn_b2, L2_ffn_W3, L2_ffn_b3, L2_ffn_Wl, L2_ffn_bl)[0]
    x = x + _L3_gnn_ref(_layernorm(x, axis=-1), L3_gnn_W1, L3_gnn_b1, L3_gnn_W2, L3_gnn_b2, edge_index)
    x = x + _L3_ffn_ref(_layernorm(x, axis=-1)[None], L3_ffn_router_w, L3_ffn_w_gate, L3_ffn_w_up, L3_ffn_w_down, L3_ffn_ws_gate, L3_ffn_ws_up, L3_ffn_ws_down, L3_ffn_sg_w, L3_ffn_sg_b)[0]
    return x

_drawn_inputs = setup_inputs


def setup_inputs(seed=0):
    import zlib

    import numpy as np

    out = dict(_drawn_inputs(seed))
    spreads = {'L0_gnn_b1s': (0.0, 0.1),
     'L0_gnn_b1d': (0.0, 0.8),
     'L0_gnn_ln1_w': (1.0, 0.2),
     'L0_gnn_ln1_b': (0.0, 0.1),
     'L0_gnn_bos': (0.0, 0.1),
     'L0_gnn_bod': (0.0, 0.409),
     'L0_gnn_lno_w': (1.0, 0.2),
     'L0_gnn_lno_b': (0.0, 0.1),
     'L0_ffn_ln_w': (1.0, 0.2),
     'L1_gnn_b1': (0.0, 0.312),
     'L1_gnn_b2': (0.0, 0.1),
     'L2_gnn_b1': (0.0, 0.635),
     'L2_gnn_b2': (0.0, 0.1),
     'L2_ffn_b1': (0.0, 0.8),
     'L2_ffn_b2': (0.0, 0.8),
     'L2_ffn_b3': (0.0, 0.8),
     'L2_ffn_bl': (0.0, 0.274),
     'L3_gnn_b1': (0.0, 0.316),
     'L3_gnn_b2': (0.0, 0.1)}
    factors = {'L0_gnn_W1d': 3.922,
     'L1_gnn_att_src1': 3.233,
     'L1_gnn_att_dst1': 8.0,
     'L1_gnn_att_src2': 8.0,
     'L1_gnn_att_dst2': 64.0,
     'L1_ffn_w1': 6.207,
     'L1_ffn_b1': 8.0,
     'L1_ffn_alpha_w1': 8.0,
     'L1_ffn_w2': 5.974,
     'L1_ffn_b2': 6.399,
     'L1_ffn_alpha_w2': 8.0,
     'L2_gnn_q1': 8.0,
     'L2_gnn_k1': 8.0,
     'L2_gnn_q2': 8.0,
     'L2_gnn_k2': 8.0,
     'L2_ffn_W1': 8.0,
     'L2_ffn_W2': 8.0,
     'L2_ffn_W3': 8.0,
     'L2_ffn_Wl': 6.09,
     'L3_ffn_router_w': 7.083,
     'L3_ffn_w_gate': 6.392,
     'L3_ffn_w_up': 6.215,
     'L3_ffn_w_down': 6.194,
     'L3_ffn_ws_gate': 6.859,
     'L3_ffn_ws_up': 6.6,
     'L3_ffn_ws_down': 6.738,
     'L3_ffn_sg_w': 8.0}
    for name, (base, spread) in spreads.items():
        noise = np.random.default_rng([zlib.crc32(name.encode()), seed]).standard_normal(out[name].shape)
        drawn = base * np.exp(spread * noise) if base else spread * noise
        out[name] = jnp.asarray(drawn.astype(out[name].dtype))
    for name, factor in factors.items():
        out[name] = (out[name] * factor).astype(out[name].dtype)
    return out
```

```python
from contextlib import ExitStack, contextmanager

import concourse.bass as bass
from concourse import mybir

ALU = mybir.AluOpType
ACT = mybir.ActivationFunctionType
F32 = mybir.dt.float32
F16 = mybir.dt.float16
BF16 = mybir.dt.bfloat16
I32 = mybir.dt.int32
U32 = mybir.dt.uint32
AX_X = mybir.AxisListType.X

P = 128
NODES = 625
T = (NODES + P - 1) // P
NP = T * P
LAST = NODES - (T - 1) * P
D = 768
KD = D // P
EDGES = 20000
ET = 160
HALF = NP // 2
MASK = -1e30
FLOOR = -1e20
CREDIT = 64


class Counter:

    def __init__(self, sem, credit=CREDIT):
        self.sem, self.base = sem, credit

    def at(self, n):
        return self.base + n

    def close(self, n):
        self.base += n


class Steps:

    def __init__(self, engine, counter):
        self.engine, self.counter, self.first, self.k = engine, counter, counter.base, 0

    def then(self, instruction):
        instruction.then_inc(self.counter.sem, 1)
        self.k += 1
        self.engine.wait_ge(self.counter.sem, self.first + self.k)

    def done(self):
        self.counter.base = self.first + self.k

    @contextmanager
    def loop(self, start, end, per):
        self.done()
        base = self.counter.base
        with self.engine.Fori(start, end) as i:
            self.first, self.k = base + (i - start) * per, 0
            yield i
            assert self.k == per, (self.k, per)
        self.first, self.k = base + (end - start) * per, 0


COUNTERS = [
    "dve_step", "act_step", "pool_step", "pe_step",
    "loaded", "constants", "params", "weights_a", "weights_b", "rows_loaded",
    "targets_ready", "sources_ready", "onehots_used", "distance_step", "counts_final", "counts_saved", "logs_ready", "logs_done", "stored",
    "variance_ready", "deviation_ready", "rows_ready", "transposed", "columns_ready",
    "product_ready", "product_saved", "weights_used",
    "score_ready", "waited", "copied",
    "grid_a", "grid_b", "grid_used", "sum_ready", "last_sum_ready", "sum_used", "max_ready", "probs_ready", "probs_used",
    "turned", "turned_saved", "mixed", "mixed_saved", "row_ready", "row_saved",
    "elu_ready", "elu_done", "streamed_a", "streamed_b", "stream_used",
    "hidden_ready", "hidden_done", "hidden_used", "second_ready", "second_done",
    "cleared",
]
POOL_DMA_COUNTERS = [f"pair_{j}" for j in range(8)] + ["scattered", "bias_out"]


class Memory:
    pass


def scratch(nc, m, ctx):
    m.stage += 1
    stage = m.stage
    return lambda name, shape, dt: ctx.enter_context(nc.sbuf_tensor(f"{name}_{stage}", shape, dt))


def setup(nc, m, x, src, dst, etype, one):
    m.ident = one("ident", [P, P], F32)
    m.after = one("after", [P, P], F32)
    m.iota16 = one("iota16", [P, NP], F16)
    m.X = one("X", [P, T, D], F32)
    m.H = one("H", [P, T, D], F32)
    m.HT = one("HT", [P, KD, NP], F32)
    m.eps5 = one("eps5", [P, 1], F32)
    m.eps6 = one("eps6", [P, 1], F32)
    m.from_row = one("from_row", [P, ET], U32)
    m.to_row = one("to_row", [P, ET], U32)
    m.cell = one("cell", [P, ET], U32)
    m.counted = one("counted", [P, 3, ET], F32)
    m.minus_to = one("minus_to", [P, ET], F32)
    m.ones = one("ones", [P, P], F32)
    m.rank = one("rank", [P, 32], F32)
    m.zero = one("zero", [P, 1], F32)
    with ExitStack() as ctx:
        sb = scratch(nc, m, ctx)
        iota = sb("iota", [P, NP], I32)
        part = sb("part", [P, 1], I32)
        iota_f = sb("iota_f", [P, NP], F32)
        part_f = sb("part_f", [P, 1], F32)
        ends = sb("ends", [P, 3, ET], I32)
        ends_f = sb("ends_f", [P, 3, ET], F32)
        zeros = sb("zeros", [P, 3200], F32)
        f0 = sb("f0", [P, ET], F32)
        f1 = sb("f1", [P, ET], F32)
        src_f, dst_f, type_f = (ends_f[:, k] for k in range(3))
        clear, loaded, const, stored = m.c["cleared"], m.c["loaded"], m.c["constants"], m.c["stored"]
        with nc.Block() as block:
            @block.sync
            def _(sp):
                for name in COUNTERS:
                    sp.sem_inc(m.c[name].sem, CREDIT)
                for k, end in enumerate((src, dst, etype)):
                    sp.dma_start(ends[:, k, :], end).then_inc(loaded.sem, 16)
                sp.dma_start(m.X[:, 0:T - 1, :], x[0:(T - 1) * P].rearrange("(t p) d -> p t d", p=P)).then_inc(loaded.sem, 16)
                sp.wait_ge(clear.sem, clear.at(2))
                sp.dma_start(m.X[0:LAST, T - 1, :], x[(T - 1) * P:NODES]).then_inc(loaded.sem, 16)
                grid = m.grid.rearrange("(p r) h -> p (r h)", p=P)
                for k in range(8):
                    sp.dma_start(grid[:, k * 3200:(k + 1) * 3200], zeros[:]).then_inc(stored.sem, 16)
                grid1 = m.grid1.rearrange("(p r) h -> p (r h)", p=P)
                sp.dma_start(grid1, zeros[:]).then_inc(stored.sem, 16)
                sp.wait_ge(stored.sem, stored.at(16 * 9))

            @block.gpsimd
            def _(pool):
                nc.gpsimd.memset(m.X[:, T - 1, :], 0.0).then_inc(clear.sem, 1)
                nc.gpsimd.memset(zeros[:], 0.0).then_inc(clear.sem, 1)
                nc.gpsimd.iota(iota[:], pattern=[[1, NP]], base=0, channel_multiplier=0).then_inc(const.sem, 1)
                nc.gpsimd.iota(part[:], pattern=[[0, 1]], base=0, channel_multiplier=1).then_inc(const.sem, 1)

            @block.vector
            def _(dve):
                steps = Steps(dve, m.c["dve_step"])
                nc.vector.memset(m.eps5[:], 1e-5)
                nc.vector.memset(m.eps6[:], 1e-6)
                nc.vector.memset(m.zero[:], 0.0)
                nc.vector.memset(m.ones[:], 1.0)
                dve.wait_ge(const.sem, const.at(2))
                nc.vector.tensor_copy(iota_f[:], iota[:])
                steps.then(nc.vector.tensor_copy(part_f[:], part[:]))
                nc.vector.tensor_copy(m.iota16[:], iota_f[:])
                nc.vector.tensor_copy(m.rank[:], iota_f[:, 0:32])
                nc.vector.tensor_scalar(m.ident[:], iota_f[:, 0:P], part_f[:], None, ALU.is_equal)
                nc.vector.tensor_scalar(m.after[:], iota_f[:, 0:P], part_f[:], None, ALU.is_ge)
                dve.wait_ge(loaded.sem, loaded.at(16 * 5))
                steps.then(nc.vector.tensor_copy(ends_f[:], ends[:]))
                nc.vector.tensor_scalar(m.from_row[:], src_f, 0.0, None, ALU.max)
                nc.vector.tensor_scalar(m.to_row[:], dst_f, 0.0, None, ALU.max)
                nc.vector.tensor_scalar(f0[:], src_f, 0.0, None, ALU.max)
                steps.then(nc.vector.tensor_scalar(f1[:], dst_f, 0.0, float(NP), ALU.max, ALU.mult))
                steps.then(nc.vector.tensor_tensor(m.cell[:], f0[:], f1[:], ALU.add))
                steps.then(nc.vector.tensor_scalar(f0[:], src_f, 1.0, None, ALU.add))
                nc.vector.tensor_copy(m.counted[:, 0], src_f)
                nc.vector.tensor_scalar(m.minus_to[:], dst_f, -1.0, None, ALU.mult)
                for r in range(2):
                    steps.then(nc.vector.scalar_tensor_tensor(m.counted[:, 1 + r], type_f, float(r), f0[:], ALU.is_equal, ALU.mult))
                    steps.then(nc.vector.tensor_scalar(m.counted[:, 1 + r], m.counted[:, 1 + r], -1.0, None, ALU.add))
                steps.done()
        clear.close(2), loaded.close(80), const.close(2), stored.close(16 * 9)


def log_counts(nc, m, relations):
    with ExitStack() as ctx:
        sb = scratch(nc, m, ctx)
        slots = min(2, len(relations))
        count = sb("count", [P, slots, T, NP], F32)
        mask = sb("mask", [P, slots, T, NP], F32)
        loads = (m.c["grid_a"], m.c["grid_b"])
        logs, logged, ready, stored = (m.c[k] for k in ("logs_ready", "logs_done", "rows_ready", "stored"))
        with nc.Block() as block:
            @block.sync
            def _(sp):
                for n, r in enumerate(relations):
                    if n >= 2:
                        sp.wait_ge(stored.sem, stored.at(16 * (n - 1)))
                    sp.dma_start(count[:, n % 2], m.counts[r].rearrange("(t p) s -> p t s", p=P)).then_inc(loads[n % 2].sem, 16)
                    if n:
                        sp.wait_ge(ready.sem, ready.at(n))
                        sp.dma_start(m.logs[relations[n - 1]].rearrange("(t p) s -> p t s", p=P), count[:, (n - 1) % 2]).then_inc(stored.sem, 16)
                n = len(relations)
                sp.wait_ge(ready.sem, ready.at(n))
                sp.dma_start(m.logs[relations[n - 1]].rearrange("(t p) s -> p t s", p=P), count[:, (n - 1) % 2]).then_inc(stored.sem, 16)
                sp.wait_ge(stored.sem, stored.at(16 * n))

            @block.vector
            def _(dve):
                steps = Steps(dve, m.c["dve_step"])
                for n in range(len(relations)):
                    s = n % 2
                    dve.wait_ge(loads[s].sem, loads[s].at(16 * (n // 2 + 1)))
                    nc.vector.tensor_scalar(mask[:, s], count[:, s], 0.0, MASK, ALU.is_equal, ALU.mult)
                    steps.then(nc.vector.tensor_scalar(count[:, s], count[:, s], 1.0, None, ALU.max))
                    dve.sem_inc(logs.sem, 1)
                    dve.wait_ge(logged.sem, logged.at(n + 1))
                    steps.then(nc.vector.tensor_tensor(count[:, s], count[:, s], mask[:, s], ALU.add))
                    dve.sem_inc(ready.sem, 1)
                steps.done()

            @block.scalar
            def _(act):
                for n in range(len(relations)):
                    act.wait_ge(logs.sem, logs.at(n + 1))
                    nc.scalar.activation(count[:, n % 2], count[:, n % 2], ACT.Ln, bias=m.zero[:]).then_inc(logged.sem, 1)
        n = len(relations)
        loads[0].close(16 * ((n + 1) // 2)), loads[1].close(16 * (n // 2))
        logs.close(n), logged.close(n), ready.close(n), stored.close(16 * n)


def normalise(nc, m, src, dst, eps, scale=None, shift=None, turned=None):
    with ExitStack() as ctx:
        sb = scratch(nc, m, ctx)
        stats = sb("stats", [P, T, 2, 6], F32)
        mean = sb("mean", [P, T, 2], F32)
        dev = sb("dev", [P, T], F32)
        rdev = sb("rdev", [P, T], F32)
        affine = sb("affine", [P, 2, D], F32)
        var_ready, dev_ready, ready, params = (m.c[k] for k in ("variance_ready", "deviation_ready", "rows_ready", "params"))
        with nc.Block() as block:
            if scale is not None:
                @block.sync
                def _(sp):
                    sp.dma_start(affine[:, 0], scale.partition_broadcast(P)).then_inc(params.sem, 16)
                    sp.dma_start(affine[:, 1], shift.partition_broadcast(P)).then_inc(params.sem, 16)

            @block.vector
            def _(dve):
                steps = Steps(dve, m.c["dve_step"])
                for t in range(T):
                    for h in range(2):
                        ins = nc.vector.bn_stats(stats[:, t, h], src[:, t, h * 384:(h + 1) * 384])
                steps.then(ins)
                for t in range(T):
                    ins = nc.vector.bn_aggr(mean[:, t], stats[:, t].rearrange("p a b -> p (a b)"))
                ins.then_inc(var_ready.sem, 1)
                dve.wait_ge(dev_ready.sem, dev_ready.at(1))
                steps.then(nc.vector.reciprocal(rdev[:], dev[:]))
                if scale is not None:
                    dve.wait_ge(params.sem, params.at(32))
                for t in range(T):
                    ins = nc.vector.tensor_scalar(dst[:, t], src[:, t], mean[:, t, 0:1], rdev[:, t:t + 1],
                                                  ALU.subtract, ALU.mult)
                    if scale is not None:
                        steps.then(ins)
                        steps.then(nc.vector.tensor_tensor(dst[:, t], dst[:, t], affine[:, 0], ALU.mult))
                        ins = nc.vector.tensor_tensor(dst[:, t], dst[:, t], affine[:, 1], ALU.add)
                    ins.then_inc(ready.sem, 1)
                steps.done()

            if turned is not None:
                @block.tensor
                def _(pe):
                    turn_rows(nc, m, pe, dst)

            @block.scalar
            def _(act):
                act.wait_ge(var_ready.sem, var_ready.at(1))
                nc.scalar.activation(dev[:], mean[:, :, 1], ACT.Sqrt, bias=eps[:]).then_inc(dev_ready.sem, 1)
                if turned is not None:
                    save_turned(nc, m, act, turned)
        close_turn(m, 1 if turned is not None else 0)
        var_ready.close(1), dev_ready.close(1), ready.close(T)
        if scale is not None:
            params.close(32)


def turn_rows(nc, m, pe, rows, ready_made=False):
    ready, turned, saved = m.c["rows_ready"], m.c["transposed"], m.c["columns_ready"]
    nk = rows.shape[2] // P
    for t in range(T):
        if not ready_made:
            pe.wait_ge(ready.sem, ready.at(t + 1))
        pe.wait_ge(saved.sem, saved.at(t - 1))
        for k in range(nk):
            b = 2 * (t % 2) + k // 4
            ins = nc.tensor.transpose(m.psum[:, b, (k % 4) * P:(k % 4 + 1) * P], rows[:, t, k * P:(k + 1) * P], m.ident[:])
        ins.then_inc(turned.sem, 1)


def save_turned(nc, m, act, columns):
    turned, saved = m.c["transposed"], m.c["columns_ready"]
    nk = columns.shape[1]
    for t in range(T):
        act.wait_ge(turned.sem, turned.at(t + 1))
        for k0 in range(0, nk, 4):
            n = min(4, nk - k0)
            src = m.psum[:, 2 * (t % 2) + k0 // 4, 0:n * P].rearrange("p (k c) -> p k c", k=n)
            ins = nc.scalar.activation(columns[:, k0:k0 + n, t * P:(t + 1) * P], src, ACT.Copy)
        ins.then_inc(saved.sem, 1)


def close_turn(m, n):
    m.c["transposed"].close(n * T), m.c["columns_ready"].close(n * T)


def project(nc, m, columns, jobs, after=None):
    kk = columns.shape[1]
    width = jobs[0][0].shape[-1]
    parts = (width + 511) // 512
    w = width // parts
    load = (m.c["weights_a"], m.c["weights_b"])
    used, ready, saved = m.c["weights_used"], m.c["product_ready"], m.c["product_saved"]
    with ExitStack() as ctx:
        sb = scratch(nc, m, ctx)
        slots = min(2, len(jobs))
        weights = sb("weights", [P, slots, kk, width], F32)
        bias = sb("bias", [P, slots, width], F32)
        with nc.Block() as block:
            @block.sync
            def _(sp):
                for j, (wsrc, bsrc, _, _) in enumerate(jobs):
                    if j >= 2:
                        sp.wait_ge(used.sem, used.at(j - 1))
                        sp.wait_ge(saved.sem, saved.at((j - 1) * T))
                    c = load[j % 2]
                    sp.dma_start(weights[:, j % 2], wsrc.rearrange("(k p) f -> p k f", p=P)).then_inc(c.sem, 16)
                    if bsrc is not None:
                        sp.dma_start(bias[:, j % 2], bsrc.partition_broadcast(P)).then_inc(c.sem, 16)

            seen = []
            n_load = [0, 0]
            for j, job in enumerate(jobs):
                n_load[j % 2] += 16 if job[1] is None else 32
                seen.append(n_load[j % 2])

            @block.tensor
            def _(pe):
                for j in range(len(jobs)):
                    pe.wait_ge(load[j % 2].sem, load[j % 2].at(seen[j]))
                    for t in range(T):
                        u = j * T + t
                        pe.wait_ge(saved.sem, saved.at(u - 1))
                        for c in range(parts):
                            for k in range(kk):
                                ins = nc.tensor.matmul(m.psum[:, 2 * (u % 2) + c, 0:w], columns[:, k, t * P:(t + 1) * P],
                                                       weights[:, j % 2, k, c * w:(c + 1) * w],
                                                       start=(k == 0), stop=(k == kk - 1))
                        ins.then_inc(ready.sem, 1)
                    pe.wait_ge(ready.sem, ready.at((j + 1) * T))
                    pe.sem_inc(used.sem, 1)

            @block.vector
            def _(dve):
                steps = Steps(dve, m.c["dve_step"])
                for j, (_, bsrc, rows, factor) in enumerate(jobs):
                    for t in range(T):
                        u = j * T + t
                        dve.wait_ge(ready.sem, ready.at(u + 1))
                        src = m.psum[:, 2 * (u % 2):2 * (u % 2) + parts, 0:w]
                        out = rows[:, t, 0:width].rearrange("p (c w) -> p c w", c=parts)
                        if bsrc is not None:
                            ins = nc.vector.tensor_tensor(out, src, bias[:, j % 2].rearrange("p (c w) -> p c w", c=parts), ALU.add)
                        elif factor is not None:
                            ins = nc.vector.tensor_scalar(out, src, factor[:, t:t + 1], None, ALU.mult)
                        else:
                            ins = nc.vector.tensor_copy(out, src)
                        ins.then_inc(saved.sem, 1)
                if after is not None:
                    dve.wait_ge(saved.sem, saved.at(len(jobs) * T))
                    after(steps)
                steps.done()
        for k in range(2):
            load[k].close(n_load[k])
        used.close(len(jobs)), ready.close(len(jobs) * T), saved.close(len(jobs) * T)


def edge_scores(nc, m, fs, fd, attn, heads, grid, passes, saves):
    W = D + heads
    U = 8
    from_dram = m.from_dram[heads]
    to_dram = m.to_dram[heads]
    with ExitStack() as ctx:
        sb = scratch(nc, m, ctx)
        coef = sb("coef", [P, D], F32)
        low = sb("low", [P, D], F32)
        high = sb("high", [P, D], F32)
        work = sb("work", [P, T, D], F32)
        params, ready, stored = m.c["params"], m.c["rows_ready"], m.c["stored"]
        with nc.Block() as block:
            @block.sync
            def _(sp):
                sp.dma_start(coef[:], attn.partition_broadcast(P)).then_inc(params.sem, 16)
                sp.wait_ge(ready.sem, ready.at(1))
                sp.dma_start(from_dram.rearrange("(t p) d -> p t d", p=P), fs[:]).then_inc(stored.sem, 16)
                sp.wait_ge(ready.sem, ready.at(2))
                sp.dma_start(to_dram.rearrange("(t p) d -> p t d", p=P), fd[:]).then_inc(stored.sem, 16)
                sp.wait_ge(stored.sem, stored.at(32))

            @block.vector
            def _(dve):
                steps = Steps(dve, m.c["dve_step"])
                dve.wait_ge(params.sem, params.at(16))
                nc.vector.tensor_scalar(low[:], coef[:], 0.8, None, ALU.mult)
                steps.then(nc.vector.tensor_scalar(high[:], coef[:], 0.2, None, ALU.mult))
                for k, rows in enumerate((fs, fd)):
                    for t in range(T):
                        ins = nc.vector.tensor_tensor(work[:, t], rows[:, t, 0:D], high[:], ALU.mult)
                    steps.then(ins)
                    for t in range(T):
                        ins = nc.vector.tensor_reduce(rows[:, t, D:W], work[:, t].rearrange("p (h c) -> p h c", h=heads),
                                                      AX_X, ALU.add)
                    steps.then(ins)
                    dve.sem_inc(ready.sem, 1)
                steps.done()
        params.close(16), ready.close(2), stored.close(32)

        rows_of = sb("rows_of", [P, 2, 3, U], U32)
        both = sb("both", [P, U, W], F32)
        score = sb("score", [P, U, heads], F32)
        part = sb("part", [P, 2, heads], F32)
        C = len(passes)
        HOTS = 4
        distance = sb("distance", [P, 2, NP], F16)
        to_hot = sb("to_hot", [P, HOTS, NP], BF16)
        from_hot = sb("from_hot", [P, HOTS, NP], BF16)
        counts = sb("counts", [P, T, NP], F32)
        counts2 = sb("counts2", [P, T, NP], F32) if C == 2 else None
        rest = sb("rest", [P, 2, T, NP], F32) if C == 1 else None
        far = m.c["distance_step"]
        landed = [m.c[f"pair_{j}"] for j in range(U)]
        scored, scattered = m.c["score_ready"], m.c["scattered"]
        waited, copied = m.c["waited"], m.c["copied"]
        to_ready, from_ready, hots_used, counted, emptied = (
            m.c[k] for k in ("targets_ready", "sources_ready", "onehots_used", "counts_final", "counts_saved"))
        TURNS = ET // U
        ADD, SCATTER = 2, 5

        def wide(t):
            return m.psum[:, t, :]

        def narrow(t):
            return m.psum[:, T + t // 4, (t % 4) * P:(t % 4 + 1) * P]

        with nc.Block() as block:
            @block.gpsimd
            def _(pool):
                def after(counter, n):
                    pool.wait_ge(counter.sem, n)
                    pool.sem_inc(waited.sem, 1)

                def turn(i, parity, first=False, last=False):
                    if not last:
                        cols = bass.ds(i * U, U)
                        nc.gpsimd.tensor_copy(rows_of[:, parity, 0], m.from_row[:, cols])
                        nc.gpsimd.tensor_copy(rows_of[:, parity, 1], m.to_row[:, cols])
                        nc.gpsimd.tensor_copy(rows_of[:, parity, 2], m.cell[:, cols]).then_inc(copied.sem, 1)
                        after(copied, copied.at(i + 1))
                    for j in range(U):
                        if not last:
                            nc.gpsimd.indirect_dma_start(
                                out=both[:, j], out_offset=None, in_=from_dram,
                                in_offset=bass.IndirectOffsetOnAxis(ap=rows_of[:, parity, 0, j:j + 1], axis=0)).then_inc(landed[j].sem, 16)
                        same = j >= ADD
                        if same and not last or not same and not first:
                            k, q, of = (j - ADD) % U, parity if same else 1 - parity, i if same else i - 1
                            after(landed[k], landed[k].at(32 * of + 16))
                            nc.gpsimd.indirect_dma_start(
                                out=both[:, k], out_offset=None, in_=to_dram,
                                in_offset=bass.IndirectOffsetOnAxis(ap=rows_of[:, q, 1, k:k + 1], axis=0),
                                compute_op=ALU.add).then_inc(landed[k].sem, 16)
                        same = j >= SCATTER
                        if same and not last or not same and not first:
                            k, q, n = (j - SCATTER) % U, parity if same else 1 - parity, i * U + j - SCATTER
                            after(scored, scored.at(n + 1))
                            after(scattered, scattered.at(16 * n))
                            nc.gpsimd.indirect_dma_start(
                                out=grid, out_offset=bass.IndirectOffsetOnAxis(ap=rows_of[:, q, 2, k:k + 1], axis=0),
                                in_=score[:, k], in_offset=None).then_inc(scattered.sem, 16)

                turn(0, 0, first=True)
                with pool.Fori(0, TURNS // 2 - 1) as i:
                    turn(2 * i + 1, 1)
                    turn(2 * i + 2, 0)
                turn(TURNS - 1, 1)
                turn(TURNS, 0, last=True)
                pool.wait_ge(scattered.sem, scattered.at(16 * ET))

            @block.vector
            def _(dve):
                steps = Steps(dve, m.c["dve_step"])

                def turns(start, end, n_pass):
                    with steps.loop(start, end, 2 * U) as i:
                        for j in range(U):
                            for c in range(C):
                                q = C * (U * i + j) + c
                                tile = q - n_pass * ET
                                dve.wait_ge(hots_used.sem, hots_used.at(q - HOTS + 1))
                                nc.vector.tensor_scalar(from_hot[:, (C * j + c) % HOTS], m.iota16[:], m.counted[:, passes[n_pass], bass.ds(tile, 1)],
                                                        None, ALU.is_equal).then_inc(from_ready.sem, 1)
                            dve.wait_ge(landed[j].sem, landed[j].at(32 * i + 32))
                            steps.then(nc.vector.scalar_tensor_tensor(work[:, j % 2], both[:, j, 0:D], 0.0, low[:], ALU.max, ALU.mult))
                            steps.then(nc.vector.tensor_reduce(part[:, j % 2], work[:, j % 2].rearrange("p (h c) -> p h c", h=heads),
                                                               AX_X, ALU.add))
                            nc.vector.tensor_tensor(score[:, j], part[:, j % 2], both[:, j, D:W], ALU.add).then_inc(scored.sem, 1)

                def save_counts(n_pass, to):
                    dve.wait_ge(counted.sem, counted.at(n_pass + 1))
                    nc.vector.tensor_copy(to[:, :, 0:512], m.psum[:, 0:T, :])
                    nc.vector.tensor_copy(to[:, 0:4, 512:NP], m.psum[:, T, :].rearrange("p (t c) -> p t c", t=4))
                    nc.vector.tensor_copy(to[:, 4, 512:NP], narrow(4)).then_inc(emptied.sem, 1)

                for k in range(C):
                    turns(k * TURNS // C, (k + 1) * TURNS // C, k)
                    save_counts(k, (counts, counts2)[k])
                if C == 1:
                    dve.wait_ge(params.sem, params.at(32))
                    dve.wait_ge(emptied.sem, emptied.at(1))
                    steps.then(nc.vector.tensor_tensor(rest[:, 0], rest[:, 0], rest[:, 1], ALU.subtract))
                    nc.vector.tensor_tensor(rest[:, 0], rest[:, 0], counts[:], ALU.subtract).then_inc(emptied.sem, 1)
                steps.done()

            @block.scalar
            def _(act):
                def turns(start, end, n_pass):
                    with act.Fori(start, end) as i:
                        for j in range(U * C):
                            q = C * U * i + j
                            tile = q - n_pass * ET
                            act.wait_ge(far.sem, far.at(2 * q - 2))
                            nc.scalar.activation(distance[:, j % 2], m.iota16[:], ACT.Abs, bias=m.minus_to[:, bass.ds(tile, 1)]).then_inc(far.sem, 1)
                            act.wait_ge(hots_used.sem, hots_used.at(q - HOTS + 1))
                            act.wait_ge(far.sem, far.at(2 * q + 1))
                            nc.scalar.activation(to_hot[:, j % HOTS], distance[:, j % 2], ACT.Relu, bias=m.ones[:, 0:1], scale=-1.0).then_inc(to_ready.sem, 1)
                            act.sem_inc(far.sem, 1)

                for k in range(C):
                    turns(k * TURNS // C, (k + 1) * TURNS // C, k)

            @block.tensor
            def _(pe):
                def product(q, slot, first=False, last=False):
                    pe.wait_ge(to_ready.sem, to_ready.at(q + 1))
                    pe.wait_ge(from_ready.sem, from_ready.at(q + 1))
                    for t in range(T):
                        rows = to_hot[:, slot, t * P:(t + 1) * P]
                        nc.tensor.matmul(wide(t), rows, from_hot[:, slot, 0:512], start=first, stop=last)
                        ins = nc.tensor.matmul(narrow(t), rows, from_hot[:, slot, 512:NP], start=first and t % 4 == 0,
                                               stop=last and t % 4 == 3 or last and t == T - 1, skip_group_check=True)
                    ins.then_inc(hots_used.sem, 1)

                for n_pass in range(C):
                    if n_pass:
                        pe.wait_ge(emptied.sem, emptied.at(n_pass))
                    q = n_pass * ET
                    for j in range(HOTS):
                        product(q + j, j, first=(j == 0))
                    with pe.Fori(1, ET // HOTS - 1) as i:
                        for j in range(HOTS):
                            product(q + HOTS * i + j, j)
                    for j in range(HOTS):
                        product(q + ET - HOTS + j, j, last=(j == HOTS - 1))
                    pe.wait_ge(hots_used.sem, hots_used.at(q + ET))
                    pe.sem_inc(counted.sem, 1)

            @block.sync
            def _(sp):
                rows = lambda k: m.counts[k].rearrange("(t p) s -> p t s", p=P)
                if C == 1:
                    sp.dma_start(rest[:, 0], rows(3)).then_inc(params.sem, 16)
                    sp.dma_start(rest[:, 1], rows(0)).then_inc(params.sem, 16)
                for k, to in enumerate(saves):
                    sp.wait_ge(emptied.sem, emptied.at(k + 1))
                    sp.dma_start(rows(to), (rest[:, 0] if C == 1 else counts2[:]) if k else counts[:]).then_inc(stored.sem, 16)
                sp.wait_ge(stored.sem, stored.at(16 * len(saves)))
        for c in landed:
            c.close(32 * TURNS)
        scored.close(ET), scattered.close(16 * ET), copied.close(TURNS), far.close(2 * C * ET)
        to_ready.close(C * ET), from_ready.close(C * ET), hots_used.close(C * ET), counted.close(C), emptied.close(2)
        stored.close(16 * len(saves))
        if C == 1:
            params.close(32)


def attend(nc, m, relations, heads, width, values, out, grid=None, broad=None, near=None, logs=()):
    R, Hn = relations, heads
    parts = (width + 511) // 512
    w = width // parts
    load = (m.c["grid_a"], m.c["grid_b"])
    names = ("grid_used", "sum_ready", "sum_used", "max_ready", "probs_ready", "probs_used", "turned", "turned_saved",
             "mixed", "mixed_saved")
    a_ready = m.c["last_sum_ready"]
    g_used, s_ready, s_used, x_ready, p_ready, p_used, t_ready, t_saved, o_ready, o_saved = (m.c[k] for k in names)
    n_load = 1 + (grid is not None)
    with ExitStack() as ctx:
        sb = scratch(nc, m, ctx)
        log = sb("log_t", [P, 2, R, NP], F32)
        cells = sb("cells", [P, 2, NP, Hn], F32) if grid is not None else None
        total = sb("sum_t", [P, 2, R, NP], F32)
        score = sb("score_t", [P, 2, R, NP], F32)
        top = sb("top", [P, 2, R + 2], F32)
        probs = sb("probs", [P, 2, R, NP], F32)
        mass = sb("mass", [P, 4, R], F32)
        share = sb("share", [P, 2, 2], F32)
        turned = sb("turned_t", [P, 2, R, NP], F32)
        with nc.Block() as block:
            @block.sync
            def _(sp):
                for t in range(T):
                    if t >= 2:
                        sp.wait_ge(g_used.sem, g_used.at(t - 1))
                    c = load[t % 2]
                    rows = slice(t * P, (t + 1) * P)
                    for r in range(R):
                        sp.dma_start(log[:, t % 2, r], m.logs[logs[r]][rows]).then_inc(c.sem, 16)
                    if grid is not None:
                        sp.dma_start(cells[:, t % 2], grid.rearrange("(d s) h -> d s h", s=NP)[rows]).then_inc(c.sem, 16)

            pool_part = R if R == 1 else R - 1
            if grid is None:
                @block.gpsimd
                def _(pool):
                    for t in range(T):
                        for h in range(Hn):
                            u = t * Hn + h
                            if u >= 2:
                                pool.wait_ge(s_used.sem, s_used.at(u - 1))
                            for r in range(pool_part):
                                ins = nc.gpsimd.tensor_scalar(total[:, u % 2, r], broad[:, r * Hn + h],
                                                              near[:, t, r * Hn + h:r * Hn + h + 1], None, ALU.add)
                            ins.then_inc(s_ready.sem, 1)

            @block.vector
            def _(dve):
                steps = Steps(dve, m.c["dve_step"])

                def scores(t, h):
                    u = t * Hn + h
                    s = u % 2
                    if h == 0:
                        n = (R + (grid is not None)) * 16 * (t // 2 + 1)
                        dve.wait_ge(load[t % 2].sem, load[t % 2].at(n))
                    if u >= 2:
                        dve.wait_ge(p_ready.sem, p_ready.at(u - 1))
                    if grid is None:
                        dve.wait_ge(s_ready.sem, s_ready.at(u + 1))
                        if pool_part < R:
                            dve.wait_ge(a_ready.sem, a_ready.at(u + 1))
                        for r in range(R):
                            ins = nc.vector.scalar_tensor_tensor(total[:, s, r], total[:, s, r], 0.2, total[:, s, r], ALU.mult, ALU.max)
                        steps.then(ins)
                    for r in range(R):
                        part = cells[:, t % 2, :, h] if grid is not None else total[:, s, r]
                        ins = nc.vector.tensor_tensor_reduce(out=score[:, s, r], in0=part, in1=log[:, t % 2, r], scale=1.0,
                                                             scalar=FLOOR, op0=ALU.add, op1=ALU.max,
                                                             accum_out=top[:, s, r:r + 1])
                    steps.then(ins)
                    if grid is None:
                        dve.sem_inc(s_used.sem, 1)
                    if h == Hn - 1:
                        dve.sem_inc(g_used.sem, 1)
                    if R > 1:
                        steps.then(nc.vector.tensor_reduce(top[:, s, R:R + 1], top[:, s, 0:R], AX_X, ALU.max))
                    last = top[:, s, R:R + 1] if R > 1 else top[:, s, 0:1]
                    nc.vector.tensor_scalar(top[:, s, R + 1:R + 2], last, -1.0, None, ALU.mult).then_inc(x_ready.sem, 1)

                def save(t, h):
                    u = t * Hn + h
                    s = u % 2
                    dve.wait_ge(p_ready.sem, p_ready.at(u + 1))
                    if R > 1:
                        steps.then(nc.vector.tensor_reduce(share[:, s, 0:1], mass[:, u % 4, :], AX_X, ALU.add))
                        steps.then(nc.vector.tensor_scalar(share[:, s, 0:1], share[:, s, 0:1], 1e-16, None, ALU.add))
                    else:
                        steps.then(nc.vector.tensor_scalar(share[:, s, 0:1], mass[:, u % 4, 0:1], 1e-16, None, ALU.add))
                    steps.then(nc.vector.reciprocal(share[:, s, 1:2], share[:, s, 0:1]))
                    dve.wait_ge(o_ready.sem, o_ready.at(u + 1))
                    if parts == 1:
                        src, dst = m.psum[:, 4 + 2 * s, 0:w], out[:, t, h * w:(h + 1) * w]
                    else:
                        src = m.psum[:, 4 + 2 * s:6 + 2 * s, 0:w]
                        dst = out[:, t, 0:width].rearrange("p (c w) -> p c w", c=parts)
                    nc.vector.tensor_scalar(dst, src, share[:, s, 1:2], None, ALU.mult).then_inc(o_saved.sem, 1)

                units = [(t, h) for t in range(T) for h in range(Hn)]
                LAG = 2
                for n, unit in enumerate(units):
                    scores(*unit)
                    if n >= LAG:
                        save(*units[n - LAG])
                for unit in units[-LAG:]:
                    save(*unit)
                steps.done()

            @block.scalar
            def _(act):
                def last_sum(u):
                    t, h = divmod(u, Hn)
                    if u >= 2:
                        act.wait_ge(s_used.sem, s_used.at(u - 1))
                    r = R - 1
                    nc.scalar.activation(total[:, u % 2, r], broad[:, r * Hn + h], ACT.Identity,
                                         bias=near[:, t, r * Hn + h:r * Hn + h + 1]).then_inc(a_ready.sem, 1)

                def exponents(u):
                    s = u % 2
                    act.wait_ge(x_ready.sem, x_ready.at(u + 1))
                    if u >= 2:
                        act.wait_ge(p_used.sem, p_used.at(u - 1))
                    if u >= 4:
                        act.wait_ge(o_saved.sem, o_saved.at(u - 3))
                    for r in range(R):
                        ins = nc.scalar.activation(probs[:, s, r], score[:, s, r], ACT.Exp, bias=top[:, s, R + 1:R + 2],
                                                   accum_out=mass[:, u % 4, r:r + 1])
                    ins.then_inc(p_ready.sem, 1)

                def save_turned_probs(u):
                    if u >= 2:
                        act.wait_ge(o_ready.sem, o_ready.at(u - 1))
                    for r in range(R):
                        v = u * R + r
                        act.wait_ge(t_ready.sem, t_ready.at(v + 1))
                        b = 2 * (v % 2)
                        nc.scalar.activation(turned[:, u % 2, r, 0:512], m.psum[:, b, :], ACT.Copy)
                        nc.scalar.activation(turned[:, u % 2, r, 512:NP], m.psum[:, b + 1, 0:P], ACT.Copy).then_inc(t_saved.sem, 1)

                lag = 1 if R == 1 else 0
                if pool_part < R:
                    last_sum(0)
                for u in range(T * Hn):
                    if pool_part < R and u + 1 < T * Hn:
                        last_sum(u + 1)
                    exponents(u)
                    if u >= lag:
                        save_turned_probs(u - lag)
                if lag:
                    save_turned_probs(T * Hn - 1)

            @block.tensor
            def _(pe):
                def turn(u):
                    pe.wait_ge(p_ready.sem, p_ready.at(u + 1))
                    for r in range(R):
                        v = u * R + r
                        if v >= 2:
                            pe.wait_ge(t_saved.sem, t_saved.at(v - 1))
                        for c in range(T):
                            b = 2 * (v % 2) + c // 4
                            ins = nc.tensor.transpose(m.psum[:, b, (c % 4) * P:(c % 4 + 1) * P], probs[:, u % 2, r, c * P:(c + 1) * P],
                                                      m.ident[:])
                        ins.then_inc(t_ready.sem, 1)
                    pe.wait_ge(t_ready.sem, t_ready.at((u + 1) * R))
                    pe.sem_inc(p_used.sem, 1)

                def mix(u):
                    h = u % Hn
                    if u >= 2:
                        pe.wait_ge(o_saved.sem, o_saved.at(u - 1))
                    pe.wait_ge(t_saved.sem, t_saved.at((u + 1) * R))
                    for c in range(parts):
                        for r in range(R):
                            for k in range(T):
                                ins = nc.tensor.matmul(m.psum[:, 4 + 2 * (u % 2) + c, 0:w], turned[:, u % 2, r, k * P:(k + 1) * P],
                                                       values[r][:, k, h * width + c * w:h * width + (c + 1) * w],
                                                       start=(r == 0 and k == 0), stop=(r == R - 1 and k == T - 1))
                    ins.then_inc(o_ready.sem, 1)

                for u in range(T * Hn):
                    turn(u)
                    if u:
                        mix(u - 1)
                mix(T * Hn - 1)
        U = T * Hn
        per = (R + (grid is not None)) * 16
        load[0].close(per * ((T + 1) // 2)), load[1].close(per * (T // 2))
        g_used.close(T), x_ready.close(U), p_ready.close(U), p_used.close(U), t_ready.close(U * R), t_saved.close(U * R)
        o_ready.close(U), o_saved.close(U)
        if grid is None:
            s_ready.close(U), s_used.close(U)
            if R > 1:
                a_ready.close(U)


def elu_rows(nc, m, rows, bias=None, plus=None):
    width = rows.shape[2]
    e_ready, e_done, params = m.c["elu_ready"], m.c["elu_done"], m.c["params"]
    with ExitStack() as ctx:
        sb = scratch(nc, m, ctx)
        low = sb("low_part", [P, T, D], F32)
        row = sb("row", [P, D], F32)
        with nc.Block() as block:
            if bias is not None:
                @block.sync
                def _(sp):
                    sp.dma_start(row[:], bias.partition_broadcast(P)).then_inc(params.sem, 16)

            @block.vector
            def _(dve):
                steps = Steps(dve, m.c["dve_step"])
                if bias is not None:
                    dve.wait_ge(params.sem, params.at(16))
                    for t in range(T):
                        ins = nc.vector.tensor_tensor(rows[:, t, 0:D], rows[:, t, 0:D], row[:], ALU.add)
                    steps.then(ins)
                for t in range(T):
                    nc.vector.tensor_scalar(low[:, t], rows[:, t, 0:D], 0.0, None, ALU.min).then_inc(e_ready.sem, 1)
                for t in range(T):
                    dve.wait_ge(e_done.sem, e_done.at(t + 1))
                    ins = nc.vector.scalar_tensor_tensor(rows[:, t, 0:D], low[:, t], -1.0, rows[:, t, 0:D], ALU.add, ALU.max)
                    if plus is not None:
                        steps.then(ins)
                        steps.then(nc.vector.tensor_tensor(rows[:, t, 0:D], rows[:, t, 0:D], plus[:, t], ALU.add))
                steps.done()

            @block.scalar
            def _(act):
                for t in range(T):
                    act.wait_ge(e_ready.sem, e_ready.at(t + 1))
                    nc.scalar.activation(low[:, t], low[:, t], ACT.Exp, bias=m.zero[:]).then_inc(e_done.sem, 1)
        e_ready.close(T), e_done.close(T)
        if bias is not None:
            params.close(16)


def add_rows(nc, m, out, a, b):
    with nc.Block() as block:
        @block.vector
        def _(dve):
            nc.vector.tensor_tensor(out, a, b, ALU.add)


def gat_v2_block(nc, m, g):
    normalise(nc, m, m.X, m.H, m.eps5, turned=m.HT)
    with ExitStack() as ctx:
        sb = scratch(nc, m, ctx)
        out = sb("out_rows", [P, T, D], F32)
        for layer, (heads, names) in enumerate(((8, ("W1s", "b1s", "W1d", "b1d", "attn1")), (1, ("Wos", "bos", "Wod", "bod", "attno")))):
            ws, bs, wd, bd, attn = (g["L0_gnn_" + k] for k in names)
            with ExitStack() as inner:
                fs = scratch(nc, m, inner)("fs", [P, T, D + heads], F32)
                with nc.sbuf_tensor(f"fd_{heads}", [P, T, D + heads], F32) as fd:
                    project(nc, m, m.HT, [(ws, bs, fs, None), (wd, bd, fd, None)])
                    grid = m.grid if heads == 8 else m.grid1
                    passes, saves = ((0, 1), (3, 0)) if layer == 0 else ((2,), (1, 2))
                    edge_scores(nc, m, fs, fd, attn.rearrange("h c -> (h c)"), heads, grid, passes, saves)
                log_counts(nc, m, [3] if layer == 0 else [0, 1, 2])
                attend(nc, m, 1, heads, D // heads, [fs], out, grid=grid, logs=(3,))
            if layer == 0:
                elu_rows(nc, m, out, plus=m.H)
                normalise(nc, m, out, m.H, m.eps5, g["L0_gnn_ln1_w"], g["L0_gnn_ln1_b"], turned=m.HT)
            else:
                elu_rows(nc, m, out)
                normalise(nc, m, out, m.H, m.eps5, g["L0_gnn_lno_w"], g["L0_gnn_lno_b"])
                add_rows(nc, m, m.X[:], m.X[:], m.H[:])


def first_largest(nc, steps, values, work, top, chosen, rank):
    n = values.shape[2]
    shape = [P, T, n]
    ranks = rank[:, 0:n].unsqueeze(1).to_broadcast(shape)
    steps.then(nc.vector.tensor_reduce(top[:, :, 0], values, AX_X, ALU.max))
    steps.then(nc.vector.tensor_tensor(work, values, top[:, :, 0:1].to_broadcast(shape), ALU.is_lt))
    steps.then(nc.vector.scalar_tensor_tensor(work, work, float(n), ranks, ALU.mult, ALU.add))
    steps.then(nc.vector.tensor_reduce(top[:, :, 1], work, AX_X, ALU.min))
    steps.then(nc.vector.tensor_tensor(chosen, ranks, top[:, :, 1:2].to_broadcast(shape), ALU.is_equal))


def switch_block(nc, m, g):
    E, F, CAP = 16, 96, 64
    normalise(nc, m, m.X, m.H, m.eps5)
    with ExitStack() as ctx:
        sb = scratch(nc, m, ctx)
        N = sb("normed", [P, T, D], F32)
        logits = sb("logits", [P, T, E], F32)
        chance = sb("chance", [P, T], F32)
        passed = sb("passed", [P, T], F32)
        kept = sb("kept", [P, T, E], F32)
        keptT = sb("keptT", [E, NP], F32)
        params, v_ready, d_ready, ready = (m.c[k] for k in ("params", "variance_ready", "deviation_ready", "rows_ready"))
        with ExitStack() as inner:
            sb2 = scratch(nc, m, inner)
            row = sb2("ln_w", [P, D], F32)
            square = sb2("square", [P, T], F32)
            dev = sb2("dev", [P, T], F32)
            junk = sb2("junk", [P, D], F32)
            with nc.Block() as block:
                @block.sync
                def _(sp):
                    sp.dma_start(row[:], g["L0_ffn_ln_w"].partition_broadcast(P)).then_inc(params.sem, 16)

                @block.vector
                def _(dve):
                    steps = Steps(dve, m.c["dve_step"])
                    for t in range(T):
                        steps.then(nc.vector.tensor_tensor_reduce(out=junk[:], in0=m.H[:, t], in1=m.H[:, t], scale=1.0, scalar=0.0,
                                                                  op0=ALU.mult, op1=ALU.add, accum_out=square[:, t:t + 1]))
                    dve.sem_inc(v_ready.sem, 1)
                    dve.wait_ge(d_ready.sem, d_ready.at(1))
                    steps.then(nc.vector.reciprocal(dev[:], dev[:]))
                    dve.wait_ge(params.sem, params.at(16))
                    for t in range(T):
                        nc.vector.scalar_tensor_tensor(N[:, t], m.H[:, t], dev[:, t:t + 1], row[:], ALU.mult, ALU.mult).then_inc(ready.sem, 1)
                    steps.done()

                @block.tensor
                def _(pe):
                    turn_rows(nc, m, pe, N)

                @block.scalar
                def _(act):
                    act.wait_ge(v_ready.sem, v_ready.at(1))
                    nc.scalar.activation(dev[:], square[:], ACT.Sqrt, bias=m.eps6[:], scale=1.0 / D).then_inc(d_ready.sem, 1)
                    save_turned(nc, m, act, m.HT)
            params.close(16), v_ready.close(1), d_ready.close(1), ready.close(T), close_turn(m, 1)
        project(nc, m, m.HT, [(g["L0_ffn_w_router"], None, logits, None)])
        with ExitStack() as inner:
            sb2 = scratch(nc, m, inner)
            work, chosen, power = (sb2(k, [P, T, E], F32) for k in ("work", "chosen", "power"))
            top = sb2("top", [P, T, 2], F32)
            e_ready, e_done = m.c["elu_ready"], m.c["elu_done"]
            t_ready, t_saved, o_ready, o_saved = (m.c[k] for k in ("turned", "turned_saved", "mixed", "mixed_saved"))
            with nc.Block() as block:
                @block.vector
                def _(dve):
                    steps = Steps(dve, m.c["dve_step"])
                    first_largest(nc, steps, logits[:], work[:], top, chosen[:], m.rank)
                    dve.sem_inc(ready.sem, 1)
                    steps.then(nc.vector.tensor_tensor(power[:], logits[:], top[:, :, 0:1].to_broadcast([P, T, E]), ALU.subtract))
                    dve.sem_inc(e_ready.sem, 1)
                    dve.wait_ge(o_ready.sem, o_ready.at(1))
                    places = m.psum[:, 0, 0:T * E].rearrange("p (t e) -> p t e", t=T)
                    steps.then(nc.vector.scalar_tensor_tensor(kept[:], places, float(CAP), chosen[:], ALU.is_le, ALU.mult))
                    dve.sem_inc(o_saved.sem, 1)
                    steps.then(nc.vector.tensor_reduce(passed[:], kept[:], AX_X, ALU.add))
                    steps.then(nc.vector.tensor_scalar(passed[:], passed[:], -1.0, 1.0, ALU.mult, ALU.add))
                    dve.wait_ge(e_done.sem, e_done.at(1))
                    steps.then(nc.vector.tensor_reduce(chance[:], power[:], AX_X, ALU.add))
                    steps.then(nc.vector.reciprocal(chance[:], chance[:]))
                    dve.wait_ge(t_ready.sem, t_ready.at(1))
                    nc.vector.tensor_copy(keptT[:, 0:512], m.psum[0:E, 1, :])
                    steps.then(nc.vector.tensor_copy(keptT[:, 512:NP], m.psum[0:E, 2, 0:P]))
                    steps.done()

                @block.scalar
                def _(act):
                    act.wait_ge(e_ready.sem, e_ready.at(1))
                    nc.scalar.activation(power[:], power[:], ACT.Exp, bias=m.zero[:]).then_inc(e_done.sem, 1)

                @block.tensor
                def _(pe):
                    pe.wait_ge(ready.sem, ready.at(1))
                    for t in range(T):
                        for k in range(t + 1):
                            ins = nc.tensor.matmul(m.psum[:, 0, t * E:(t + 1) * E], m.after[:] if k == t else m.ones[:],
                                                   chosen[:, k], start=(k == 0), stop=(k == t))
                    ins.then_inc(o_ready.sem, 1)
                    pe.wait_ge(o_saved.sem, o_saved.at(1))
                    for t in range(T):
                        ins = nc.tensor.transpose(m.psum[0:E, 1 + t // 4, (t % 4) * P:(t % 4 + 1) * P], kept[:, t], m.ident[:])
                    ins.then_inc(t_ready.sem, 1)
            ready.close(1), e_ready.close(1), e_done.close(1), o_ready.close(1), o_saved.close(1), t_ready.close(1)

        wi = sb("wi", [P, KD, E * F], F32)
        wo = sb("wo", [F, E, D], F32)
        hidden = sb("hidden", [F, E, NP], F32)
        pick = sb("pick", [E, E, F], F32)
        load, h_ready, h_done, used, s_ready, s_done = (
            m.c[k] for k in ("weights_a", "hidden_ready", "hidden_done", "hidden_used", "second_ready", "second_done"))
        with nc.Block() as block:
            @block.sync
            def _(sp):
                sp.dma_start(wi[:], g["L0_ffn_wi"].rearrange("(k p) f -> p k f", p=P)).then_inc(load.sem, 16)
                sp.dma_start(wo[:], g["L0_ffn_wo"].rearrange("e f d -> f e d")).then_inc(load.sem, 16)

            @block.tensor
            def _(pe):
                pe.wait_ge(load.sem, load.at(32))
                pe.wait_ge(ready.sem, ready.at(1))
                for e in range(E):
                    if e >= 1:
                        pe.wait_ge(used.sem, used.at(e))
                    for c in range(2):
                        cols = slice(c * HALF, (c + 1) * HALF)
                        for k in range(KD):
                            ins = nc.tensor.matmul(m.psum[0:F, c, 0:HALF], wi[:, k, e * F:(e + 1) * F], m.HT[:, k, cols],
                                                   start=(k == 0), stop=(k == KD - 1))
                        ins = nc.tensor.matmul(m.psum[0:F, 2 + c, 0:HALF], pick[:, e], keptT[:, cols], start=True, stop=True)
                    ins.then_inc(h_ready.sem, 1)
                pe.wait_ge(used.sem, used.at(E))
                for t in range(T):
                    if t >= 2:
                        pe.wait_ge(s_done.sem, s_done.at(t - 1))
                    for c in range(2):
                        for e in range(E):
                            ins = nc.tensor.matmul(m.psum[:, 4 + 2 * (t % 2) + c, 0:384], hidden[:, e, t * P:(t + 1) * P],
                                                   wo[:, e, c * 384:(c + 1) * 384], start=(e == 0), stop=(e == E - 1))
                    ins.then_inc(s_ready.sem, 1)

            @block.scalar
            def _(act):
                for e in range(E):
                    act.wait_ge(h_ready.sem, h_ready.at(e + 1))
                    nc.scalar.activation(hidden[:, e].rearrange("p (c n) -> p c n", c=2), m.psum[0:F, 0:2, 0:HALF],
                                         ACT.Relu).then_inc(h_done.sem, 1)

            @block.vector
            def _(dve):
                steps = Steps(dve, m.c["dve_step"])
                nc.vector.tensor_copy(pick[:], m.ident[0:E, 0:E].unsqueeze(2).to_broadcast([E, E, F])).then_inc(ready.sem, 1)
                for e in range(E):
                    dve.wait_ge(h_done.sem, h_done.at(e + 1))
                    own = hidden[:, e].rearrange("p (c n) -> p c n", c=2)
                    nc.vector.tensor_tensor(own, own, m.psum[0:F, 2:4, 0:HALF], ALU.mult).then_inc(used.sem, 1)
                for t in range(T):
                    dve.wait_ge(s_ready.sem, s_ready.at(t + 1))
                    two = lambda rows: rows[:, t].rearrange("p (c w) -> p c w", c=2)
                    steps.then(nc.vector.scalar_tensor_tensor(two(N), two(N), passed[:, t:t + 1], m.psum[:, 4 + 2 * (t % 2):6 + 2 * (t % 2), 0:384],
                                                              ALU.mult, ALU.add))
                    dve.sem_inc(s_done.sem, 1)
                    steps.then(nc.vector.scalar_tensor_tensor(m.H[:, t], N[:, t], chance[:, t:t + 1], m.H[:, t], ALU.mult, ALU.add))
                    steps.then(nc.vector.tensor_tensor(m.X[:, t], m.X[:, t], m.H[:, t], ALU.add))
                steps.done()
        load.close(32), ready.close(1), h_ready.close(E), h_done.close(E), used.close(E), s_ready.close(T), s_done.close(T)


def spread(nc, m, rows, n, broad):
    total = rows.shape[2]
    t_ready, t_saved, o_ready, o_saved, ready = (m.c[k] for k in ("turned", "turned_saved", "mixed", "mixed_saved", "rows_ready"))
    with ExitStack() as ctx:
        sb = scratch(nc, m, ctx)
        pick = sb("pick", [total, n, P], F32)
        turned = sb("turned_s", [total, NP], F32)
        with nc.Block() as block:
            @block.vector
            def _(dve):
                nc.vector.tensor_copy(pick[:], m.ident[0:total, 0:n].unsqueeze(2).to_broadcast([total, n, P])).then_inc(ready.sem, 1)

            @block.tensor
            def _(pe):
                for t in range(T):
                    ins = nc.tensor.transpose(m.psum[0:total, t // 4, (t % 4) * P:(t % 4 + 1) * P], rows[:, t], m.ident[:])
                ins.then_inc(t_ready.sem, 1)
                pe.wait_ge(ready.sem, ready.at(1))
                pe.wait_ge(t_saved.sem, t_saved.at(1))
                for j in range(n):
                    if j >= 2:
                        pe.wait_ge(o_saved.sem, o_saved.at(j - 1))
                    for c in range(2):
                        ins = nc.tensor.matmul(m.psum[:, 4 + 2 * (j % 2) + c, 0:HALF], pick[:, j], turned[:, c * HALF:(c + 1) * HALF],
                                               start=True, stop=True)
                    ins.then_inc(o_ready.sem, 1)

            @block.scalar
            def _(act):
                act.wait_ge(t_ready.sem, t_ready.at(1))
                nc.scalar.activation(turned[:, 0:512], m.psum[0:total, 0, :], ACT.Copy)
                nc.scalar.activation(turned[:, 512:NP], m.psum[0:total, 1, 0:P], ACT.Copy).then_inc(t_saved.sem, 1)
                for j in range(n):
                    act.wait_ge(o_ready.sem, o_ready.at(j + 1))
                    b = 4 + 2 * (j % 2)
                    nc.scalar.activation(broad[:, j].rearrange("p (c n) -> p c n", c=2), m.psum[:, b:b + 2, 0:HALF],
                                         ACT.Copy).then_inc(o_saved.sem, 1)
        ready.close(1), t_ready.close(1), t_saved.close(1), o_ready.close(n), o_saved.close(n)


def head_scores(nc, m, values, att_s, att_d, heads, scores):
    width = values.shape[2]
    params = m.c["params"]
    with ExitStack() as ctx:
        sb = scratch(nc, m, ctx)
        att = sb("att", [P, 2, width], F32)
        work = sb("work", [P, 2, width], F32)
        with nc.Block() as block:
            @block.sync
            def _(sp):
                for k, a in enumerate((att_s, att_d)):
                    sp.dma_start(att[:, k], a.rearrange("h c -> (h c)").partition_broadcast(P)).then_inc(params.sem, 16)

            @block.vector
            def _(dve):
                steps = Steps(dve, m.c["dve_step"])
                dve.wait_ge(params.sem, params.at(32))
                for t in range(T):
                    for k in range(2):
                        ins = nc.vector.tensor_tensor(work[:, k], values[:, t], att[:, k], ALU.mult)
                    steps.then(ins)
                    for k in range(2):
                        ins = nc.vector.tensor_reduce(scores[:, t, k * heads:(k + 1) * heads],
                                                      work[:, k].rearrange("p (h c) -> p h c", h=heads), AX_X, ALU.add)
                    steps.then(ins)
                steps.done()
        params.close(32)


def finish_rows(nc, m, rows, bias, turned=None, relu=False, onto=None):
    width = rows.shape[2]
    params, ready = m.c["params"], m.c["rows_ready"]
    with ExitStack() as ctx:
        sb = scratch(nc, m, ctx)
        row = sb("row", [P, width], F32)
        with nc.Block() as block:
            @block.sync
            def _(sp):
                sp.dma_start(row[:], bias.partition_broadcast(P)).then_inc(params.sem, 16)

            @block.vector
            def _(dve):
                steps = Steps(dve, m.c["dve_step"])
                dve.wait_ge(params.sem, params.at(16))
                for t in range(T):
                    ins = nc.vector.tensor_tensor(rows[:, t], rows[:, t], row[:], ALU.add)
                    if relu:
                        steps.then(ins)
                        ins = nc.vector.tensor_scalar(rows[:, t], rows[:, t], 0.0, None, ALU.max)
                    if onto is not None:
                        steps.then(ins)
                        ins = nc.vector.tensor_tensor(onto[:, t], onto[:, t], rows[:, t], ALU.add)
                    ins.then_inc(ready.sem, 1)
                steps.done()

            if turned is not None:
                @block.tensor
                def _(pe):
                    turn_rows(nc, m, pe, rows)

                @block.scalar
                def _(act):
                    save_turned(nc, m, act, turned)
        params.close(16), ready.close(T), close_turn(m, 1 if turned is not None else 0)


def gat_block(nc, m, g):
    normalise(nc, m, m.X, m.H, m.eps5, turned=m.HT)
    with ExitStack() as ctx:
        sb = scratch(nc, m, ctx)
        columns = sb("columns", [P, 8, NP], F32)
        with ExitStack() as inner:
            sb1 = scratch(nc, m, inner)
            values = sb1("values", [P, T, 1024], F32)
            scores = sb1("scores", [P, T, 16], F32)
            broad = sb1("broad", [P, 8, NP], F32)
            out = sb1("out", [P, T, 1024], F32)
            project(nc, m, m.HT, [(g["L1_gnn_W1"], None, values, None)])
            head_scores(nc, m, values, g["L1_gnn_att_src1"], g["L1_gnn_att_dst1"], 8, scores)
            spread(nc, m, scores, 8, broad)
            attend(nc, m, 1, 8, 128, [values], out, broad=broad, near=scores[:, :, 8:16], logs=(3,))
            finish_rows(nc, m, out, g["L1_gnn_b1"], turned=columns, relu=True)
        values = sb("values", [P, T, D], F32)
        scores = sb("scores", [P, T, 2], F32)
        broad = sb("broad", [P, 1, NP], F32)
        project(nc, m, columns, [(g["L1_gnn_W2"], None, values, None)])
        head_scores(nc, m, values, g["L1_gnn_att_src2"], g["L1_gnn_att_dst2"], 1, scores)
        spread(nc, m, scores, 1, broad)
        attend(nc, m, 1, 1, D, [values], m.H, broad=broad, near=scores[:, :, 1:2], logs=(3,))
        finish_rows(nc, m, m.H, g["L1_gnn_b2"], onto=m.X)


def quantise(nc, steps, out, src, factor):
    ROUND = 12582912.0
    steps.then(nc.vector.tensor_scalar(out[0], src, factor, -8.0, ALU.mult, ALU.max))
    steps.then(nc.vector.tensor_scalar(out[0], out[0], 7.0, ROUND, ALU.min, ALU.add))
    ins = nc.vector.tensor_scalar(out[1], out[0], -ROUND, None, ALU.add)
    return ins


def quant_block(nc, m, g):
    F = 96
    normalise(nc, m, m.X, m.H, m.eps5)
    with ExitStack() as ctx:
        sb = scratch(nc, m, ctx)
        a1 = sb("a1", [P, D], F32)
        a2 = sb("a2", [P, F], F32)
        aw2 = sb("aw2", [P, D], F32)
        b2 = sb("b2", [P, D], F32)
        aw1c = sb("aw1c", [F, 1], F32)
        b1c = sb("b1c", [F, 1], F32)
        aw2c = sb("aw2c", [P, KD], F32)
        w1 = sb("w1", [F, D], F32)
        w2 = sb("w2", [P, KD, F], F32)
        mean = sb("mean", [P, 4], F32)
        w1q = sb("w1q", [F, D], F32)
        w2q = sb("w2q", [P, KD, F], F32)
        w1T = sb("w1T", [P, KD, F], BF16)
        w2T = sb("w2T", [F, D], BF16)
        xT = sb("xT", [P, KD, NP], BF16)
        hid = sb("hid", [F, NP], F32)
        hq = sb("hq", [F, NP], BF16)
        rest = sb("rest", [P, T, D], F32)
        params, ready, turned, saved, h_ready, h_done, s_ready, s_done = (
            m.c[k] for k in ("params", "rows_ready", "transposed", "columns_ready", "hidden_ready", "hidden_done", "second_ready", "second_done"))
        q_ready = m.c["sum_ready"]
        w_turned, w_saved = m.c["turned"], m.c["turned_saved"]
        column = lambda a: a.rearrange("(h o) -> h o", o=1)
        with nc.Block() as block:
            @block.sync
            def _(sp):
                loads = [(a1[:], g["L1_ffn_alpha_a1"].partition_broadcast(P)), (a2[:], g["L1_ffn_alpha_a2"].partition_broadcast(P)),
                         (aw2[:], g["L1_ffn_alpha_w2"].partition_broadcast(P)), (b2[:], g["L1_ffn_b2"].partition_broadcast(P)),
                         (aw1c[:], column(g["L1_ffn_alpha_w1"])), (b1c[:], column(g["L1_ffn_b1"])),
                         (w1[:], g["L1_ffn_w1"]), (w2[:], g["L1_ffn_w2"].rearrange("(k p) h -> p k h", p=P))]
                for to, of in loads:
                    sp.dma_start(to, of).then_inc(params.sem, 16)
                with nc.allow_non_contiguous_dma("768 numbers"):
                    sp.dma_start(aw2c[:], g["L1_ffn_alpha_w2"].rearrange("(k p) -> p k", p=P)).then_inc(params.sem, 16)

            @block.vector
            def _(dve):
                steps = Steps(dve, m.c["dve_step"])
                dve.wait_ge(params.sem, params.at(16 * 9))
                nc.vector.tensor_reduce(mean[:, 0:1], a1[:], AX_X, ALU.add)
                steps.then(nc.vector.tensor_reduce(mean[:, 1:2], a2[:], AX_X, ALU.add))
                nc.vector.tensor_scalar(mean[:, 0:1], mean[:, 0:1], 1.0 / D, None, ALU.mult)
                steps.then(nc.vector.tensor_scalar(mean[:, 1:2], mean[:, 1:2], 1.0 / F, None, ALU.mult))
                nc.vector.reciprocal(mean[:, 2:4], mean[:, 0:2])
                nc.vector.reciprocal(aw2c[:], aw2c[:])
                steps.then(nc.vector.reciprocal(w1q[:, 0:1], aw1c[:]))
                steps.then(nc.vector.tensor_scalar(w1[:], w1[:], w1q[:, 0:1], None, ALU.mult))
                steps.then(nc.vector.tensor_tensor(w2[:], w2[:], aw2c[:].unsqueeze(2).to_broadcast([P, KD, F]), ALU.mult))
                steps.then(quantise(nc, steps, (w1q[:], w1q[:]), w1[:], 1.0))
                steps.then(quantise(nc, steps, (w2q[:], w2q[:]), w2[:], 1.0))
                dve.sem_inc(q_ready.sem, 1)
                for t in range(T):
                    quantise(nc, steps, (rest[:, t], rest[:, t]), m.H[:, t], mean[:, 2:3]).then_inc(ready.sem, 1)
                steps.then(nc.vector.tensor_tensor(aw1c[:], aw1c[:], mean[0:F, 0:1], ALU.mult))
                steps.then(nc.vector.tensor_scalar(aw2[:], aw2[:], mean[:, 1:2], None, ALU.mult))
                dve.sem_inc(q_ready.sem, 1)
                dve.wait_ge(h_done.sem, h_done.at(1))
                steps.then(nc.vector.tensor_scalar(hid[:], hid[:], -10.0, 10.0, ALU.max, ALU.min))
                quantise(nc, steps, (hid[:], hq[:]), hid[:], mean[0:F, 3:4]).then_inc(h_done.sem, 1)
                for t in range(T):
                    dve.wait_ge(s_ready.sem, s_ready.at(t + 1))
                    two = lambda r: r.rearrange("p (c w) -> p c w", c=2)
                    b = 4 + 2 * (t % 2)
                    steps.then(nc.vector.tensor_tensor(two(rest[:, t]), m.psum[:, b:b + 2, 0:384], two(aw2[:]), ALU.mult))
                    dve.sem_inc(s_done.sem, 1)
                    steps.then(nc.vector.tensor_tensor(rest[:, t], rest[:, t], b2[:], ALU.add))
                    steps.then(nc.vector.tensor_tensor(m.X[:, t], m.X[:, t], rest[:, t], ALU.add))
                steps.done()

            @block.tensor
            def _(pe):
                pe.wait_ge(q_ready.sem, q_ready.at(1))
                for k in range(KD):
                    nc.tensor.transpose(m.psum[:, 4, k * 96 % 480:k * 96 % 480 + 96] if k < 5 else m.psum[:, 5, 0:96],
                                        w1q[:, k * P:(k + 1) * P], m.ident[0:F, 0:F])
                for k in range(KD):
                    ins = nc.tensor.transpose(m.psum[0:F, 6 + k // 4, (k % 4) * P:(k % 4 + 1) * P], w2q[:, k], m.ident[:])
                ins.then_inc(w_turned.sem, 1)
                turn_rows(nc, m, pe, rest)
                pe.wait_ge(w_saved.sem, w_saved.at(1))
                pe.wait_ge(saved.sem, saved.at(T))
                for c in range(2):
                    for k in range(KD):
                        ins = nc.tensor.matmul(m.psum[0:F, c, 0:HALF], w1T[:, k], xT[:, k, c * HALF:(c + 1) * HALF],
                                               start=(k == 0), stop=(k == KD - 1))
                ins.then_inc(h_ready.sem, 1)
                pe.wait_ge(h_done.sem, h_done.at(2))
                for t in range(T):
                    if t >= 2:
                        pe.wait_ge(s_done.sem, s_done.at(t - 1))
                    for c in range(2):
                        ins = nc.tensor.matmul(m.psum[:, 4 + 2 * (t % 2) + c, 0:384], hq[:, t * P:(t + 1) * P],
                                               w2T[:, c * 384:(c + 1) * 384], start=True, stop=True)
                    ins.then_inc(s_ready.sem, 1)

            @block.scalar
            def _(act):
                act.wait_ge(w_turned.sem, w_turned.at(1))
                nc.scalar.activation(w1T[:, 0:5], m.psum[:, 4, 0:480].rearrange("p (k f) -> p k f", k=5), ACT.Copy)
                nc.scalar.activation(w1T[:, 5], m.psum[:, 5, 0:96], ACT.Copy)
                nc.scalar.activation(w2T[:, 0:512], m.psum[0:F, 6, :], ACT.Copy)
                nc.scalar.activation(w2T[:, 512:D], m.psum[0:F, 7, 0:256], ACT.Copy).then_inc(w_saved.sem, 1)
                save_turned(nc, m, act, xT)
                act.wait_ge(h_ready.sem, h_ready.at(1))
                act.wait_ge(q_ready.sem, q_ready.at(2))
                nc.scalar.activation(hid[:].rearrange("p (c n) -> p c n", c=2), m.psum[0:F, 0:2, 0:HALF], ACT.Gelu,
                                     bias=b1c[:], scale=aw1c[:]).then_inc(h_done.sem, 1)
        params.close(16 * 9), ready.close(T), q_ready.close(2), close_turn(m, 1), w_turned.close(1), w_saved.close(1)
        h_ready.close(1), h_done.close(2), s_ready.close(T), s_done.close(T)


def relation_scores(nc, m, values, q, k, heads, scores, R):
    params, turned, saved, o_ready, o_saved = (m.c[x] for x in ("params", "transposed", "columns_ready", "mixed", "mixed_saved"))
    for r in range(R):
        with ExitStack() as ctx:
            sb = scratch(nc, m, ctx)
            both = sb("both_qk", [P, KD, 2, heads], F32)
            with nc.Block() as block:
                @block.sync
                def _(sp):
                    with nc.allow_non_contiguous_dma("a few thousand numbers"):
                        for n, w in enumerate((k, q)):
                            sp.dma_start(both[:, :, n], w.rearrange("(k p) h -> p k h", p=P)).then_inc(params.sem, 16)

                @block.tensor
                def _(pe):
                    turn_rows(nc, m, pe, values[r], ready_made=True)
                    pe.wait_ge(params.sem, params.at(32))
                    pe.wait_ge(saved.sem, saved.at(T))
                    for t in range(T):
                        for c in range(KD):
                            ins = nc.tensor.matmul(m.psum[:, 4, t * 2 * heads:(t + 1) * 2 * heads], m.HT[:, c, t * P:(t + 1) * P],
                                                   both[:, c].rearrange("p n h -> p (n h)"), start=(c == 0), stop=(c == KD - 1))
                    ins.then_inc(o_ready.sem, 1)

                @block.scalar
                def _(act):
                    save_turned(nc, m, act, m.HT)

                @block.vector
                def _(dve):
                    dve.wait_ge(o_ready.sem, o_ready.at(1))
                    src = m.psum[:, 4, 0:T * 2 * heads].rearrange("p (t n h) -> p t n h", t=T, n=2)
                    for n in range(2):
                        nc.vector.tensor_copy(scores[:, :, n * R * heads + r * heads:n * R * heads + (r + 1) * heads], src[:, :, n])
            params.close(32), close_turn(m, 1), o_ready.close(1)


def rgat_block(nc, m, g):
    R = 3
    for layer, heads in ((1, 4), (2, 1)):
        if layer == 1:
            normalise(nc, m, m.X, m.H, m.eps5, turned=m.HT)
        W, q, k, b = (g[f"L2_gnn_{n}{layer}"] for n in ("W", "q", "k", "b"))
        with ExitStack() as ctx:
            sb = scratch(nc, m, ctx)
            values = [sb(f"values{r}", [P, T, D], F32) for r in range(R)]
            scores = sb("scores", [P, T, 2 * R * heads], F32)
            broad = sb("broad", [P, R * heads, NP], F32)
            project(nc, m, m.HT, [(W[r], None, values[r], None) for r in range(R)])
            relation_scores(nc, m, values, q, k, heads, scores, R)
            spread(nc, m, scores, R * heads, broad)
            attend(nc, m, R, heads, D // heads, values, m.H, broad=broad, near=scores[:, :, R * heads:], logs=(0, 1, 2))
        if layer == 1:
            elu_rows(nc, m, m.H, bias=b)
            with nc.Block() as block:
                @block.tensor
                def _(pe):
                    turn_rows(nc, m, pe, m.H, ready_made=True)

                @block.scalar
                def _(act):
                    save_turned(nc, m, act, m.HT)
            close_turn(m, 1)
        else:
            finish_rows(nc, m, m.H, b, onto=m.X)


def top_two(nc, m, logits, E, eps, gates_dram, mix=None):
    rows = E + (mix is not None)
    e_ready, e_done, ready, t_ready, t_saved, stored = (
        m.c[k] for k in ("elu_ready", "elu_done", "rows_ready", "turned", "turned_saved", "stored"))
    with ExitStack() as ctx:
        sb = scratch(nc, m, ctx)
        shape = [P, T, E]
        work, first, second, prob = (sb(k, shape, F32) for k in ("work", "first", "second", "prob"))
        gates = sb("gates", [P, T, rows], F32)
        gatesT = sb("gatesT", [rows, NP], F32)
        top = sb("top", [P, T, 2], F32)
        share = sb("share", [P, T, 2], F32)
        with nc.Block() as block:
            @block.vector
            def _(dve):
                steps = Steps(dve, m.c["dve_step"])
                steps.then(nc.vector.tensor_reduce(top[:, :, 0], logits[:, :, 0:E], AX_X, ALU.max))
                steps.then(nc.vector.tensor_tensor(prob[:], logits[:, :, 0:E], top[:, :, 0:1].to_broadcast(shape), ALU.subtract))
                dve.sem_inc(e_ready.sem, 1)
                dve.wait_ge(e_done.sem, e_done.at(1))
                steps.then(nc.vector.tensor_reduce(share[:, :, 0], prob[:], AX_X, ALU.add))
                steps.then(nc.vector.reciprocal(share[:, :, 1], share[:, :, 0]))
                steps.then(nc.vector.tensor_tensor(prob[:], prob[:], share[:, :, 1:2].to_broadcast(shape), ALU.mult))
                first_largest(nc, steps, prob[:], work[:], top, first[:], m.rank)
                steps.then(nc.vector.scalar_tensor_tensor(second[:], first[:], -2.0, prob[:], ALU.mult, ALU.add))
                first_largest(nc, steps, second[:], work[:], top, second[:], m.rank)
                steps.then(nc.vector.tensor_tensor(first[:], first[:], second[:], ALU.add))
                steps.then(nc.vector.tensor_tensor(prob[:], prob[:], first[:], ALU.mult))
                steps.then(nc.vector.tensor_reduce(share[:, :, 0], prob[:], AX_X, ALU.add))
                steps.then(nc.vector.tensor_scalar(share[:, :, 0], share[:, :, 0], eps, None, ALU.add))
                steps.then(nc.vector.reciprocal(share[:, :, 1], share[:, :, 0]))
                if mix is not None:
                    steps.then(nc.vector.tensor_scalar(share[:, :, 0], gates[:, :, E], -1.0, 1.0, ALU.mult, ALU.add))
                    steps.then(nc.vector.tensor_tensor(share[:, :, 1], share[:, :, 1], share[:, :, 0], ALU.mult))
                steps.then(nc.vector.tensor_tensor(gates[:, :, 0:E], prob[:], share[:, :, 1:2].to_broadcast(shape), ALU.mult))
                dve.sem_inc(ready.sem, 1)
                steps.done()

            @block.scalar
            def _(act):
                act.wait_ge(e_ready.sem, e_ready.at(1))
                ins = nc.scalar.activation(prob[:], prob[:], ACT.Exp, bias=m.zero[:])
                if mix is not None:
                    ins = nc.scalar.activation(gates[:, :, E], logits[:, :, E], ACT.Sigmoid, bias=mix[:])
                ins.then_inc(e_done.sem, 1)
                act.wait_ge(t_ready.sem, t_ready.at(1))
                nc.scalar.activation(gatesT[:, 0:512], m.psum[0:rows, 0, :], ACT.Copy)
                nc.scalar.activation(gatesT[:, 512:NP], m.psum[0:rows, 1, 0:P], ACT.Copy).then_inc(t_saved.sem, 1)

            @block.tensor
            def _(pe):
                pe.wait_ge(ready.sem, ready.at(1))
                for t in range(T):
                    ins = nc.tensor.transpose(m.psum[0:rows, t // 4, (t % 4) * P:(t % 4 + 1) * P], gates[:, t], m.ident[:])
                ins.then_inc(t_ready.sem, 1)

            @block.sync
            def _(sp):
                sp.wait_ge(t_saved.sem, t_saved.at(1))
                sp.dma_start(gates_dram, gatesT[:]).then_inc(stored.sem, 16)
                sp.wait_ge(stored.sem, stored.at(16))
        e_ready.close(1), e_done.close(1), ready.close(1), t_ready.close(1), t_saved.close(1), stored.close(16)


def deep_experts_block(nc, m, g):
    E, HID, BOT = 32, 64, 256
    PAIRS = E // 2
    normalise(nc, m, m.X, m.H, m.eps5, turned=m.HT)
    gates_dram = m.gates32
    with ExitStack() as ctx:
        logits = scratch(nc, m, ctx)("logits", [P, T, E], F32)
        project(nc, m, m.HT, [(g["L2_ffn_gate_w"], None, logits, None)])
        top_two(nc, m, logits, E, 1e-20, gates_dram)
    with ExitStack() as ctx:
        sb = scratch(nc, m, ctx)
        gated = sb("gated", [P, PAIRS, NP], F32)
        merged = sb("merged", [P, PAIRS, D], F32)
        bias = sb("bias", [E, D], F32)
        bl = sb("bl", [E, D], F32)
        gatesT = sb("gatesT", [E, NP], F32)
        params = m.c["params"]
        with ExitStack() as inner:
            sb1 = scratch(nc, m, inner)
            w1 = sb1("w1", [P, 2, KD, P], F32)
            w2 = sb1("w2", [P, 2, P], F32)
            w3 = sb1("w3", [P, 2, 2, 2, HID + 1], F32)
            wl = sb1("wl", [P, 2, 2, 2, D], F32)
            gate = sb1("gate", [P, 2, NP], F32)
            b1 = sb1("b1", [P, PAIRS], F32)
            b2 = sb1("b2", [P, PAIRS], F32)
            first = sb1("first", [P, 2, NP], F32)
            second = sb1("second", [P, 2, NP], F32)
            row = sb1("row", [HID + 1, 2, D], F32)
            load = (m.c["streamed_a"], m.c["streamed_b"])
            row_out = m.c["bias_out"]
            used, f_ready, f_done, s_ready, s_done, g_done, m_ready, m_done, cleared, c_used = (
                m.c[k] for k in ("stream_used", "hidden_ready", "hidden_done", "second_ready", "second_done", "hidden_used", "mixed",
                                 "mixed_saved", "cleared", "grid_used"))
            LOADS = 6
            with nc.Block() as block:
                @block.sync
                def _(sp):
                    sp.dma_start(b1[:], g["L2_ffn_b1"]).then_inc(params.sem, 16)
                    sp.dma_start(b2[:], g["L2_ffn_b2"]).then_inc(params.sem, 16)
                    sp.dma_start(bl[:], g["L2_ffn_bl"]).then_inc(params.sem, 16)
                    sp.dma_start(gatesT[:], gates_dram).then_inc(params.sem, 16)
                    sp.wait_ge(cleared.sem, cleared.at(1))
                    waited = m.c["waited"]
                    with sp.Fori(0, PAIRS // 2) as i:
                        for s in range(2):
                            p = 2 * i + s
                            sp.wait_ge(used.sem, used.at(p - 1))
                            sp.sem_inc(waited.sem, 1)
                            sp.wait_ge(g_done.sem, g_done.at(p - 1))
                            sp.sem_inc(waited.sem, 1)
                            one_ = bass.ds(p, 1)
                            sp.dma_start(w1[:, s].rearrange("p k f -> p (k f)"), g["L2_ffn_W1"][one_].rearrange("o p f -> (o p) f")).then_inc(load[s].sem, 16)
                            for h in range(2):
                                sp.dma_start(w2[h * HID:(h + 1) * HID, s, h * HID:(h + 1) * HID],
                                             g["L2_ffn_W2"][one_, h * HID:(h + 1) * HID].rearrange("o p f -> (o p) f")).then_inc(load[s].sem, 16)
                            sp.dma_start(w3[:, s].rearrange("p e k f -> p (e k f)"), g["L2_ffn_W3"][one_].rearrange("o p f -> (o p) f")).then_inc(load[s].sem, 16)
                            sp.dma_start(wl[:, s].rearrange("p e k f -> p (e k f)"), g["L2_ffn_Wl"][one_].rearrange("o p f -> (o p) f")).then_inc(load[s].sem, 16)
                            for h in range(2):
                                sp.dma_start(gate[h * HID:(h + 1) * HID, s], gates_dram[bass.ds(2 * p + h, 1)].to_broadcast([HID, NP])).then_inc(load[s].sem, 16)

                @block.tensor
                def _(pe):
                    with pe.Fori(0, PAIRS // 2) as i:
                        for s in range(2):
                            p = 2 * i + s
                            pe.wait_ge(load[s].sem, load[s].at(16 * (LOADS + 1) * (i + 1)))
                            for c in range(2):
                                for k in range(KD):
                                    ins = nc.tensor.matmul(m.psum[:, c, 0:HALF], w1[:, s, k], m.HT[:, k, c * HALF:(c + 1) * HALF],
                                                           start=(k == 0), stop=(k == KD - 1))
                            ins.then_inc(f_ready.sem, 1)
                            for e in range(2):
                                pe.wait_ge(m_done.sem, m_done.at(2 * p + e - 1))
                                for c in range(2):
                                    for k in range(2):
                                        ins = nc.tensor.matmul(m.psum[0:HID + 1, 4 + 2 * e + c, 0:384], w3[:, s, e, k],
                                                               wl[:, s, e, k, c * 384:(c + 1) * 384], start=(k == 0), stop=(k == 1))
                                ins.then_inc(m_ready.sem, 1)
                            pe.wait_ge(f_done.sem, f_done.at(p + 1))
                            pe.wait_ge(s_done.sem, s_done.at(p))
                            for c in range(2):
                                ins = nc.tensor.matmul(m.psum[:, 2 + c, 0:HALF], w2[:, s], first[:, s, c * HALF:(c + 1) * HALF], start=True, stop=True)
                            ins.then_inc(s_ready.sem, 1)
                            pe.wait_ge(s_ready.sem, s_ready.at(p + 1))
                            pe.sem_inc(used.sem, 1)

                @block.scalar
                def _(act):
                    two = lambda v: v.rearrange("p (c n) -> p c n", c=2)
                    act.wait_ge(params.sem, params.at(64))
                    with act.Fori(0, PAIRS // 2) as i:
                        for s in range(2):
                            p = 2 * i + s
                            act.wait_ge(f_ready.sem, f_ready.at(p + 1))
                            nc.scalar.activation(two(first[:, s]), m.psum[:, 0:2, 0:HALF], ACT.Gelu, bias=b1[:, bass.ds(p, 1)]).then_inc(f_done.sem, 1)
                            for e in range(2):
                                act.wait_ge(m_ready.sem, m_ready.at(2 * p + e + 1))
                                if e == 0:
                                    act.wait_ge(row_out.sem, row_out.at(32 * p))
                                nc.scalar.activation(row[HID:HID + 1, e].rearrange("p (c n) -> p c n", c=2), m.psum[HID:HID + 1, 4 + 2 * e:6 + 2 * e, 0:384], ACT.Copy)
                                nc.scalar.activation(merged[e * HID:(e + 1) * HID, bass.ds(p, 1)].rearrange("p o (c n) -> p (o c) n", c=2),
                                                     m.psum[0:HID, 4 + 2 * e:6 + 2 * e, 0:384], ACT.Copy).then_inc(m_done.sem, 1)
                            act.wait_ge(s_ready.sem, s_ready.at(p + 1))
                            act.wait_ge(g_done.sem, g_done.at(p - 1))
                            nc.scalar.activation(two(second[:, s]), m.psum[:, 2:4, 0:HALF], ACT.Gelu, bias=b2[:, bass.ds(p, 1)]).then_inc(s_done.sem, 1)

                @block.vector
                def _(dve):
                    nc.vector.memset(w2[:], 0.0).then_inc(cleared.sem, 1)
                    with dve.Fori(0, PAIRS // 2) as i:
                        for s in range(2):
                            p = 2 * i + s
                            dve.wait_ge(load[s].sem, load[s].at(16 * (LOADS + 1) * (i + 1)))
                            dve.wait_ge(s_done.sem, s_done.at(p + 1))
                            nc.vector.tensor_tensor(gated[:, bass.ds(p, 1)].rearrange("p o n -> p (o n)"), second[:, s], gate[:, s], ALU.mult).then_inc(g_done.sem, 1)

                @block.gpsimd
                def _(pool):
                    with pool.Fori(0, PAIRS // 2) as i:
                        for s in range(2):
                            p = 2 * i + s
                            pool.wait_ge(m_done.sem, m_done.at(2 * p + 2))
                            pool.sem_inc(m.c["waited"].sem, 1)
                            for e in range(2):
                                pool.dma_start(m.bias_rows[bass.ds(2 * p + e, 1)], row[HID:HID + 1, e]).then_inc(row_out.sem, 16)
                    pool.wait_ge(row_out.sem, row_out.at(32 * PAIRS))
            params.close(64), cleared.close(1), m.c["waited"].close(PAIRS)
            for s in range(2):
                load[s].close(16 * (LOADS + 1) * (PAIRS // 2))
            row_out.close(32 * PAIRS)
            used.close(PAIRS), f_ready.close(PAIRS), f_done.close(PAIRS), s_ready.close(PAIRS), s_done.close(PAIRS), g_done.close(PAIRS)
            m_ready.close(E), m_done.close(E)
        ready, o_ready, o_saved = (m.c[k] for k in ("rows_ready", "mixed", "mixed_saved"))
        with nc.Block() as block:
            @block.sync
            def _(sp):
                sp.dma_start(bias[:], m.bias_rows).then_inc(params.sem, 16)

            @block.vector
            def _(dve):
                steps = Steps(dve, m.c["dve_step"])
                dve.wait_ge(params.sem, params.at(16))
                nc.vector.tensor_tensor(bias[:], bias[:], bl[:], ALU.add).then_inc(ready.sem, 1)
                for t in range(T):
                    dve.wait_ge(o_ready.sem, o_ready.at(t + 1))
                    two = m.X[:, t].rearrange("p (c w) -> p c w", c=2)
                    nc.vector.tensor_tensor(two, two, m.psum[:, 2 * (t % 2):2 * (t % 2) + 2, 0:384], ALU.add).then_inc(o_saved.sem, 1)
                steps.done()

            @block.tensor
            def _(pe):
                for t in range(T):
                    if t >= 2:
                        pe.wait_ge(o_saved.sem, o_saved.at(t - 1))
                    cols = slice(t * P, (t + 1) * P)
                    for c in range(2):
                        out, of = m.psum[:, 2 * (t % 2) + c, 0:384], slice(c * 384, (c + 1) * 384)
                        for p in range(PAIRS):
                            nc.tensor.matmul(out, gated[:, p, cols], merged[:, p, of], start=(p == 0), stop=False)
                        if t == 0 and c == 0:
                            pe.wait_ge(ready.sem, ready.at(1))
                        ins = nc.tensor.matmul(out, gatesT[:, cols], bias[:, of], start=False, stop=True)
                    ins.then_inc(o_ready.sem, 1)
        params.close(16), ready.close(1), o_ready.close(T), o_saved.close(T)


def gcn_block(nc, m, g):
    normalise(nc, m, m.X, m.H, m.eps5, turned=m.HT)
    with ExitStack() as ctx:
        sb = scratch(nc, m, ctx)
        count = sb("count", [P, T, NP], F32)
        countT = sb("countT", [P, T, NP], F32)
        root = sb("root", [P, T], F32)
        values = sb("values", [P, T, D], F32)
        row = sb("row", [P, 2, D], F32)
        params, ready, turned, saved, v_ready, d_ready = (
            m.c[k] for k in ("params", "rows_ready", "transposed", "columns_ready", "variance_ready", "deviation_ready"))
        with nc.Block() as block:
            @block.sync
            def _(sp):
                sp.dma_start(count[:], m.counts[3].rearrange("(t p) s -> p t s", p=P)).then_inc(params.sem, 16)
                for k in range(2):
                    sp.dma_start(row[:, k], g[f"L3_gnn_b{k + 1}"].partition_broadcast(P)).then_inc(params.sem, 16)

            @block.vector
            def _(dve):
                steps = Steps(dve, m.c["dve_step"])
                dve.wait_ge(params.sem, params.at(48))
                for t in range(T):
                    own = count[:, t, t * P:(t + 1) * P]
                    ins = nc.vector.tensor_tensor(own, own, m.ident[:], ALU.add)
                    ins.then_inc(ready.sem, 1)
                dve.wait_ge(ready.sem, ready.at(T))
                steps.then(nc.vector.tensor_reduce(root[:], count[:], AX_X, ALU.add))
                dve.sem_inc(v_ready.sem, 1)
                dve.wait_ge(d_ready.sem, d_ready.at(1))
                steps.then(nc.vector.reciprocal(root[:], root[:]))
                steps.done()

            @block.tensor
            def _(pe):
                turn_rows(nc, m, pe, count)

            @block.scalar
            def _(act):
                save_turned(nc, m, act, countT)
                act.wait_ge(v_ready.sem, v_ready.at(1))
                nc.scalar.activation(root[:], root[:], ACT.Sqrt, bias=m.zero[:]).then_inc(d_ready.sem, 1)
        params.close(48), ready.close(T), close_turn(m, 1), v_ready.close(1), d_ready.close(1)
        o_ready, o_saved = m.c["mixed"], m.c["mixed_saved"]
        for layer in (1, 2):
            project(nc, m, m.HT, [(g[f"L3_gnn_W{layer}"], None, values, root)])
            with nc.Block() as block:
                @block.tensor
                def _(pe):
                    for t in range(T):
                        if t >= 2:
                            pe.wait_ge(o_saved.sem, o_saved.at(t - 1))
                        for c in range(2):
                            for k in range(T):
                                ins = nc.tensor.matmul(m.psum[:, 4 + 2 * (t % 2) + c, 0:384], countT[:, k, t * P:(t + 1) * P],
                                                       values[:, k, c * 384:(c + 1) * 384], start=(k == 0), stop=(k == T - 1))
                        ins.then_inc(o_ready.sem, 1)
                    if layer == 1:
                        turn_rows(nc, m, pe, m.H)

                @block.vector
                def _(dve):
                    steps = Steps(dve, m.c["dve_step"])
                    for t in range(T):
                        dve.wait_ge(o_ready.sem, o_ready.at(t + 1))
                        two = lambda r: r.rearrange("p (c w) -> p c w", c=2)
                        b = 4 + 2 * (t % 2)
                        steps.then(nc.vector.scalar_tensor_tensor(two(m.H[:, t]), m.psum[:, b:b + 2, 0:384], root[:, t:t + 1],
                                                                  two(row[:, layer - 1]), ALU.mult, ALU.add))
                        dve.sem_inc(o_saved.sem, 1)
                        if layer == 1:
                            nc.vector.tensor_scalar(m.H[:, t], m.H[:, t], 0.0, None, ALU.max).then_inc(ready.sem, 1)
                        else:
                            nc.vector.tensor_tensor(m.X[:, t], m.X[:, t], m.H[:, t], ALU.add)
                    steps.done()

                if layer == 1:
                    @block.scalar
                    def _(act):
                        save_turned(nc, m, act, m.HT)
            o_ready.close(T), o_saved.close(T)
            if layer == 1:
                ready.close(T), close_turn(m, 1)


def gated_experts_block(nc, m, g):
    E, HS = 8, 96
    normalise(nc, m, m.X, m.H, m.eps5, turned=m.HT)
    gates_dram = m.gates9
    params = m.c["params"]
    with ExitStack() as ctx:
        sb = scratch(nc, m, ctx)
        logits = sb("logits", [P, T, E + 1], F32)
        sg_b = sb("sg_b", [P, 1], F32)
        with nc.Block() as block:
            @block.sync
            def _(sp):
                sp.dma_start(sg_b[:], g["L3_ffn_sg_b"].partition_broadcast(P)).then_inc(params.sem, 16)
                sp.wait_ge(params.sem, params.at(16))
        params.close(16)
        project(nc, m, m.HT, [(g["L3_ffn_router_w"], None, logits, None)])
        top_two(nc, m, logits, E, 0.0, gates_dram, mix=sg_b)
    silu_ready, product_ready, gate_up_ready, down_ready, down_done = (
        m.c[k] for k in ("hidden_done", "hidden_used", "hidden_ready", "second_ready", "second_done"))
    with ExitStack() as ctx:
        sb = scratch(nc, m, ctx)
        SLOTS = 3
        gu = sb("gate_up", [P, SLOTS, 2, KD, P], F32)
        down = sb("down", [P, 2, KD, D], F32)
        gate = sb("gate", [P, 2, NP], F32)
        act_rows = sb("silu", [P, 2, HALF], F32)
        hidden = sb("hidden", [P, KD, NP], F32)
        shared_gu = sb("shared_gu", [P, 2, KD, HS], F32)
        shared_down = sb("shared_down", [HS, D], F32)
        tile_in = (m.c["grid_a"], m.c["grid_b"], m.c["weights_a"])
        down_in = (m.c["streamed_a"], m.c["streamed_b"])
        tile_used, down_used = m.c["stream_used"], m.c["weights_used"]
        UN = 2 * KD
        G = E + 1

        def banks_of(v):
            return 2 * (v % 2), 2 * (v % 2) + 1

        with nc.Block() as block:
            @block.sync
            def _(sp):
                waited = m.c["waited"]
                with sp.Fori(0, E // 2) as i:
                    for s in range(2):
                        e = 2 * i + s
                        sp.wait_ge(down_used.sem, down_used.at(e - 1))
                        sp.sem_inc(waited.sem, 1)
                        sp.wait_ge(product_ready.sem, product_ready.at(UN * (e - 1)))
                        sp.sem_inc(waited.sem, 1)
                        sp.dma_start(gate[:, s], gates_dram[bass.ds(e, 1)].to_broadcast([P, NP])).then_inc(down_in[s].sem, 16)
                        for f in range(KD):
                            n = e * KD + f
                            sp.wait_ge(tile_used.sem, tile_used.at(n - SLOTS + 1))
                            sp.sem_inc(waited.sem, 1)
                            sp.dma_start(gu[:, f % SLOTS].rearrange("p a k c -> p (a k c)"),
                                         g["L3_ffn_gate_up"][bass.ds(n, 1)].rearrange("o p f -> (o p) f")).then_inc(tile_in[f % SLOTS].sem, 16)
                            if f == 2:
                                sp.dma_start(down[:, s], g["L3_ffn_w_down"][bass.ds(e, 1)].rearrange("o (k p) d -> p (o k) d", p=P)).then_inc(down_in[s].sem, 16)
                sp.dma_start(shared_gu[:, 0], g["L3_ffn_ws_gate"].rearrange("(k p) f -> p k f", p=P)).then_inc(params.sem, 16)
                sp.dma_start(shared_gu[:, 1], g["L3_ffn_ws_up"].rearrange("(k p) f -> p k f", p=P)).then_inc(params.sem, 16)
                sp.dma_start(shared_down[:], g["L3_ffn_ws_down"]).then_inc(params.sem, 16)
                sp.wait_ge(product_ready.sem, product_ready.at(UN * (E - 1)))
                sp.dma_start(gate[:, 0], gates_dram[E:E + 1].to_broadcast([P, NP])).then_inc(params.sem, 16)

            @block.tensor
            def _(pe):
                def gate_up(v, j, weights, width):
                    pe.wait_ge(product_ready.sem, product_ready.at(v - 1))
                    c = j % 2
                    for a, b in enumerate(banks_of(j)):
                        for k in range(KD):
                            ins = nc.tensor.matmul(m.psum[0:width, b, 0:HALF], weights[:, a, k], m.HT[:, k, c * HALF:(c + 1) * HALF],
                                                   start=(k == 0), stop=(k == KD - 1))
                    ins.then_inc(gate_up_ready.sem, 1)

                def down_rows(w, t, parts, weights):
                    pe.wait_ge(down_done.sem, down_done.at(w - 1))
                    for c in range(2):
                        for k in range(parts):
                            rows = hidden[:, k, t * P:(t + 1) * P] if parts > 1 else hidden[0:HS, 0, t * P:(t + 1) * P]
                            ins = nc.tensor.matmul(m.psum[:, 4 + 2 * (t % 2) + c, 0:384], rows, weights(k, c), start=(k == 0), stop=(k == parts - 1))
                    ins.then_inc(down_ready.sem, 1)

                with pe.Fori(0, E // 2) as i:
                    for s in range(2):
                        e = 2 * i + s
                        for f in range(KD):
                            pe.wait_ge(tile_in[f % SLOTS].sem, tile_in[f % SLOTS].at(16 * (2 * e + f // SLOTS + 1)))
                            if f == 0:
                                pe.wait_ge(down_ready.sem, down_ready.at(T * e))
                            for c in range(2):
                                gate_up(UN * e + 2 * f + c, 2 * f + c, gu[:, f % SLOTS], P)
                            pe.wait_ge(gate_up_ready.sem, gate_up_ready.at(UN * e + 2 * f + 2))
                            pe.sem_inc(tile_used.sem, 1)
                        pe.wait_ge(down_in[s].sem, down_in[s].at(32 * (i + 1)))
                        pe.wait_ge(product_ready.sem, product_ready.at(UN * (e + 1)))
                        for t in range(T):
                            down_rows(e * T + t, t, KD, lambda k, c: down[:, s, k, c * 384:(c + 1) * 384])
                        pe.wait_ge(down_ready.sem, down_ready.at(T * (e + 1)))
                        pe.sem_inc(down_used.sem, 1)
                pe.wait_ge(params.sem, params.at(64))
                for c in range(2):
                    gate_up(UN * E + c, c, shared_gu, HS)
                pe.wait_ge(product_ready.sem, product_ready.at(UN * E + 2))
                for t in range(T):
                    down_rows(E * T + t, t, 1, lambda k, c: shared_down[:, c * 384:(c + 1) * 384])

            @block.scalar
            def _(act):
                def silu(v, j, width):
                    act.wait_ge(gate_up_ready.sem, gate_up_ready.at(v + 1))
                    act.wait_ge(product_ready.sem, product_ready.at(v - 1))
                    nc.scalar.activation(act_rows[0:width, j % 2], m.psum[0:width, banks_of(j)[0], 0:HALF], ACT.Silu).then_inc(silu_ready.sem, 1)

                with act.Fori(0, E) as e:
                    for j in range(UN):
                        silu(UN * e + j, j, P)
                for j in range(2):
                    silu(UN * E + j, j, HS)

            @block.vector
            def _(dve):
                steps = Steps(dve, m.c["dve_step"])

                def product(v, j, width, s):
                    c = j % 2
                    dve.wait_ge(silu_ready.sem, silu_ready.at(v + 1))
                    out = hidden[0:width, j // 2, c * HALF:(c + 1) * HALF]
                    steps.then(nc.vector.tensor_tensor(out, act_rows[0:width, c], m.psum[0:width, banks_of(j)[1], 0:HALF], ALU.mult))
                    nc.vector.tensor_tensor(out, out, gate[0:width, s, c * HALF:(c + 1) * HALF], ALU.mult).then_inc(product_ready.sem, 1)

                def add_down(w, t):
                    dve.wait_ge(down_ready.sem, down_ready.at(w + 1))
                    two = m.X[:, t].rearrange("p (c w) -> p c w", c=2)
                    nc.vector.tensor_tensor(two, two, m.psum[:, 4 + 2 * (t % 2):6 + 2 * (t % 2), 0:384], ALU.add).then_inc(down_done.sem, 1)

                with steps.loop(0, E // 2, 2 * UN) as i:
                    for s in range(2):
                        e = 2 * i + s
                        dve.wait_ge(down_in[s].sem, down_in[s].at(32 * (i + 1)))
                        dve.wait_ge(down_ready.sem, down_ready.at(T * e))
                        for j in range(UN):
                            product(UN * e + j, j, P, s)
                        for t in range(T):
                            add_down(e * T + t, t)
                dve.wait_ge(params.sem, params.at(64))
                for j in range(2):
                    product(UN * E + j, j, HS, 0)
                for t in range(T):
                    add_down(E * T + t, t)
                steps.done()
        for s in range(SLOTS):
            tile_in[s].close(16 * 2 * E)
        for s in range(2):
            down_in[s].close(32 * (E // 2))
        params.close(64), tile_used.close(KD * E), down_used.close(E)
        n = UN * E + 2
        gate_up_ready.close(n), silu_ready.close(n), product_ready.close(n), down_ready.close(T * G), down_done.close(T * G)


def finish(nc, m, out):
    stored = m.c["stored"]
    with nc.Block() as block:
        @block.sync
        def _(sp):
            sp.dma_start(out[0:(T - 1) * P].rearrange("(t p) d -> p t d", p=P), m.X[:, 0:T - 1, :]).then_inc(stored.sem, 16)
            sp.dma_start(out[(T - 1) * P:NODES], m.X[0:LAST, T - 1, :]).then_inc(stored.sem, 16)
            sp.wait_ge(stored.sem, stored.at(32))
    stored.close(32)


def gnn_ffn_kernel(nc, g, out, until=(0, 8)):
    m = Memory()
    m.stage = 0
    with ExitStack() as ctx:
        m.c = {name: Counter(ctx.enter_context(nc.semaphore(name))) for name in COUNTERS}
        m.c |= {name: Counter(ctx.enter_context(nc.semaphore(name)), 0) for name in POOL_DMA_COUNTERS}
        m.psum = ctx.enter_context(nc.psum_tensor("psum", [P, 8, 512], F32))
        one = lambda name, shape, dt: ctx.enter_context(nc.sbuf_tensor(name, shape, dt))
        m.grid = nc.dram_tensor("grid", (NP * NP, 8), F32).ap()
        m.grid1 = nc.dram_tensor("grid1", (NP * NP, 1), F32).ap()
        m.logs = nc.dram_tensor("log_counts", (4, NP, NP), F32).ap()
        m.counts = nc.dram_tensor("counts", (4, NP, NP), F32).ap()
        m.from_dram = {h: nc.dram_tensor(f"from_rows_{h}", (NP, D + h), F32).ap() for h in (8, 1)}
        m.to_dram = {h: nc.dram_tensor(f"to_rows_{h}", (NP, D + h), F32).ap() for h in (8, 1)}
        m.gates32 = nc.dram_tensor("gates_32", (32, NP), F32).ap()
        m.gates9 = nc.dram_tensor("gates_9", (9, NP), F32).ap()
        m.bias_rows = nc.dram_tensor("bias_rows", (32, D), F32).ap()
        setup(nc, m, g["x"], g["src"], g["dst"], g["edge_type_3"], one)
        blocks = [gat_v2_block, switch_block, gat_block, quant_block, rgat_block, deep_experts_block, gcn_block,
                  gated_experts_block]
        for b in blocks[until[0]:until[1]]:
            b(nc, m, g)
        finish(nc, m, out)


def host_layout(inputs):
    import numpy as np
    laid = {name: np.asarray(a) for name, a in inputs.items()}
    for name in ("src", "dst", "edge_type_3"):
        padded = np.full((ET * P,), -1, dtype=laid[name].dtype)
        padded[:EDGES] = laid[name]
        laid[name] = padded.reshape(P, ET)
    for name in ("L1_gnn_W1", "L1_gnn_W2", "L2_ffn_gate_w"):
        laid[name] = laid[name].T
    laid["L0_ffn_wi"] = laid["L0_ffn_wi"].transpose(1, 0, 2).reshape(D, -1)
    laid["L2_ffn_W1"] = laid["L2_ffn_W1"].reshape(16, 2, KD, P, 64).transpose(0, 3, 2, 1, 4).reshape(16, P, -1)
    laid["L2_ffn_W2"] = laid["L2_ffn_W2"].reshape(16, P, 64)
    w3 = np.concatenate([laid["L2_ffn_W3"].transpose(0, 2, 1), laid.pop("L2_ffn_b3")[:, :, None]], axis=2)
    laid["L2_ffn_W3"] = w3.reshape(16, 2, 2, P, 65).transpose(0, 3, 1, 2, 4).reshape(16, P, -1)
    laid["L2_ffn_Wl"] = laid["L2_ffn_Wl"].reshape(16, 2, 2, P, D).transpose(0, 3, 1, 2, 4).reshape(16, P, -1)
    for name in ("L2_ffn_b1", "L2_ffn_b2"):
        laid[name] = laid[name].reshape(16, P).T
    laid["L3_ffn_router_w"] = np.concatenate([laid["L3_ffn_router_w"], laid.pop("L3_ffn_sg_w")], axis=1)
    tiles = [laid.pop(f"L3_ffn_w_{k}").reshape(8, KD, P, KD, P).transpose(0, 3, 2, 1, 4) for k in ("gate", "up")]
    laid["L3_ffn_gate_up"] = np.stack(tiles, axis=3).reshape(8 * KD, P, -1)
    laid = {name: np.ascontiguousarray(a) for name, a in laid.items()}
    return laid


def kernel(**inputs):
    import concourse.bacc as _bacc
    from concourse.bass_utils import run_bass_kernel_spmd as _run

    nc = _bacc.Bacc("TRN2", target_bir_lowering=False, num_devices=1)
    arrays, g = {}, {}
    for name, a in host_layout(inputs).items():
        arrays[f"in_{name}"] = a
        g[name] = nc.dram_tensor(f"in_{name}", a.shape, mybir.dt.from_np(a.dtype), kind="ExternalInput").ap()
    out = nc.dram_tensor("out_x", (NODES, D), F32, kind="ExternalOutput").ap()
    gnn_ffn_kernel(nc, g, out)
    r = _run(nc, [arrays], core_ids=[0])
    return r.results[0]["out_x"]
```

```python
from contextlib import ExitStack, contextmanager

import concourse.bass as bass
from concourse import mybir

ALU = mybir.AluOpType
ACT = mybir.ActivationFunctionType
F32 = mybir.dt.float32
F16 = mybir.dt.float16
BF16 = mybir.dt.bfloat16
I32 = mybir.dt.int32
U32 = mybir.dt.uint32
AX_X = mybir.AxisListType.X

P = 128
NODES = 625
T = (NODES + P - 1) // P
NP = T * P
LAST = NODES - (T - 1) * P
D = 768
KD = D // P
EDGES = 20000
ET = 160
HALF = NP // 2
MASK = -1e30
FLOOR = -1e20
CREDIT = 64


class Counter:

    def __init__(self, sem, credit=CREDIT):
        self.sem, self.base = sem, credit

    def at(self, n):
        return self.base + n

    def close(self, n):
        self.base += n


class Steps:

    def __init__(self, engine, counter):
        self.engine, self.counter, self.first, self.k = engine, counter, counter.base, 0

    def then(self, instruction):
        instruction.then_inc(self.counter.sem, 1)
        self.k += 1
        self.engine.wait_ge(self.counter.sem, self.first + self.k)

    def done(self):
        self.counter.base = self.first + self.k

    @contextmanager
    def loop(self, start, end, per):
        self.done()
        base = self.counter.base
        with self.engine.Fori(start, end) as i:
            self.first, self.k = base + (i - start) * per, 0
            yield i
            assert self.k == per, (self.k, per)
        self.first, self.k = base + (end - start) * per, 0


COUNTERS = [
    "dve_step", "act_step", "pool_step", "pe_step",
    "loaded", "constants", "params", "weights_a", "weights_b", "rows_loaded",
    "targets_ready", "sources_ready", "onehots_used", "distance_step", "counts_final", "counts_saved", "logs_ready", "logs_done", "stored",
    "variance_ready", "deviation_ready", "rows_ready", "transposed", "columns_ready",
    "product_ready", "product_saved", "weights_used",
    "score_ready", "waited", "copied",
    "grid_a", "grid_b", "grid_used", "sum_ready", "last_sum_ready", "sum_used", "max_ready", "probs_ready", "probs_used",
    "turned", "turned_saved", "mixed", "mixed_saved", "row_ready", "row_saved",
    "elu_ready", "elu_done", "streamed_a", "streamed_b", "stream_used",
    "hidden_ready", "hidden_done", "hidden_used", "second_ready", "second_done",
    "cleared", "hidden_turned", "hidden_saved", "gate_ready", "up_ready", "silu_ready", "down_ready", "made_ready",
]
POOL_DMA_COUNTERS = [f"pair_{j}" for j in range(8)] + ["scattered", "bias_out", "sent", "fetched", "made_out"]


class Memory:
    pass


def scratch(nc, m, ctx):
    m.stage += 1
    stage = m.stage
    return lambda name, shape, dt: ctx.enter_context(nc.sbuf_tensor(f"{name}_{stage}", shape, dt))


def setup(nc, m, x, src, dst, etype, one):
    m.ident = one("ident", [P, P], F32)
    m.after = one("after", [P, P], F32)
    m.iota16 = one("iota16", [P, NP], F16)
    m.X = one("X", [P, T, D], F32)
    m.H = one("H", [P, T, D], F32)
    m.HT = one("HT", [P, KD, NP], F32)
    m.eps5 = one("eps5", [P, 1], F32)
    m.eps6 = one("eps6", [P, 1], F32)
    m.from_row = one("from_row", [P, ET], U32)
    m.to_row = one("to_row", [P, ET], U32)
    m.cell = one("cell", [P, ET], U32)
    m.counted = one("counted", [P, 3, ET], F32)
    m.minus_to = one("minus_to", [P, ET], F32)
    m.ones = one("ones", [P, P], F32)
    m.rank = one("rank", [P, 32], F32)
    m.zero = one("zero", [P, 1], F32)
    m.part = one("part", [P, 1], F32)
    with ExitStack() as ctx:
        sb = scratch(nc, m, ctx)
        iota = sb("iota", [P, NP], I32)
        part = sb("part", [P, 1], I32)
        iota_f = sb("iota_f", [P, NP], F32)
        part_f = sb("part_f", [P, 1], F32)
        ends = sb("ends", [P, 3, ET], I32)
        ends_f = sb("ends_f", [P, 3, ET], F32)
        zeros = sb("zeros", [P, 3200], F32)
        f0 = sb("f0", [P, ET], F32)
        f1 = sb("f1", [P, ET], F32)
        src_f, dst_f, type_f = (ends_f[:, k] for k in range(3))
        token_stores = (m.tokens.shape[0] * D // P + 3199) // 3200
        clear, loaded, const, stored = m.c["cleared"], m.c["loaded"], m.c["constants"], m.c["stored"]
        with nc.Block() as block:
            @block.sync
            def _(sp):
                for name in COUNTERS:
                    sp.sem_inc(m.c[name].sem, CREDIT)
                for k, end in enumerate((src, dst, etype)):
                    sp.dma_start(ends[:, k, :], end).then_inc(loaded.sem, 16)
                sp.dma_start(m.X[:, 0:T - 1, :], x[0:(T - 1) * P].rearrange("(t p) d -> p t d", p=P)).then_inc(loaded.sem, 16)
                sp.wait_ge(clear.sem, clear.at(2))
                sp.dma_start(m.X[0:LAST, T - 1, :], x[(T - 1) * P:NODES]).then_inc(loaded.sem, 16)
                grid = m.grid.rearrange("(p r) h -> p (r h)", p=P)
                for k in range(8):
                    sp.dma_start(grid[:, k * 3200:(k + 1) * 3200], zeros[:]).then_inc(stored.sem, 16)
                grid1 = m.grid1.rearrange("(p r) h -> p (r h)", p=P)
                sp.dma_start(grid1, zeros[:]).then_inc(stored.sem, 16)
                tokens = m.tokens.rearrange("(p r) d -> p (r d)", p=P)
                for k in range(0, tokens.shape[1], 3200):
                    n = min(3200, tokens.shape[1] - k)
                    sp.dma_start(tokens[:, k:k + n], zeros[:, 0:n]).then_inc(stored.sem, 16)
                sp.wait_ge(stored.sem, stored.at(16 * (9 + token_stores)))

            @block.gpsimd
            def _(pool):
                nc.gpsimd.memset(m.X[:, T - 1, :], 0.0).then_inc(clear.sem, 1)
                nc.gpsimd.memset(zeros[:], 0.0).then_inc(clear.sem, 1)
                nc.gpsimd.iota(iota[:], pattern=[[1, NP]], base=0, channel_multiplier=0).then_inc(const.sem, 1)
                nc.gpsimd.iota(part[:], pattern=[[0, 1]], base=0, channel_multiplier=1).then_inc(const.sem, 1)

            @block.vector
            def _(dve):
                steps = Steps(dve, m.c["dve_step"])
                nc.vector.memset(m.eps5[:], 1e-5)
                nc.vector.memset(m.eps6[:], 1e-6)
                nc.vector.memset(m.zero[:], 0.0)
                nc.vector.memset(m.ones[:], 1.0)
                dve.wait_ge(const.sem, const.at(2))
                nc.vector.tensor_copy(iota_f[:], iota[:])
                steps.then(nc.vector.tensor_copy(part_f[:], part[:]))
                nc.vector.tensor_copy(m.iota16[:], iota_f[:])
                nc.vector.tensor_copy(m.rank[:], iota_f[:, 0:32])
                nc.vector.tensor_copy(m.part[:], part_f[:])
                nc.vector.tensor_scalar(m.ident[:], iota_f[:, 0:P], part_f[:], None, ALU.is_equal)
                nc.vector.tensor_scalar(m.after[:], iota_f[:, 0:P], part_f[:], None, ALU.is_ge)
                dve.wait_ge(loaded.sem, loaded.at(16 * 5))
                steps.then(nc.vector.tensor_copy(ends_f[:], ends[:]))
                nc.vector.tensor_scalar(m.from_row[:], src_f, 0.0, None, ALU.max)
                nc.vector.tensor_scalar(m.to_row[:], dst_f, 0.0, None, ALU.max)
                nc.vector.tensor_scalar(f0[:], src_f, 0.0, None, ALU.max)
                steps.then(nc.vector.tensor_scalar(f1[:], dst_f, 0.0, float(NP), ALU.max, ALU.mult))
                steps.then(nc.vector.tensor_tensor(m.cell[:], f0[:], f1[:], ALU.add))
                steps.then(nc.vector.tensor_scalar(f0[:], src_f, 1.0, None, ALU.add))
                nc.vector.tensor_copy(m.counted[:, 0], src_f)
                nc.vector.tensor_scalar(m.minus_to[:], dst_f, -1.0, None, ALU.mult)
                for r in range(2):
                    steps.then(nc.vector.scalar_tensor_tensor(m.counted[:, 1 + r], type_f, float(r), f0[:], ALU.is_equal, ALU.mult))
                    steps.then(nc.vector.tensor_scalar(m.counted[:, 1 + r], m.counted[:, 1 + r], -1.0, None, ALU.add))
                steps.done()
        clear.close(2), loaded.close(80), const.close(2), stored.close(16 * (9 + token_stores))


def log_counts(nc, m, relations):
    with ExitStack() as ctx:
        sb = scratch(nc, m, ctx)
        slots = min(2, len(relations))
        count = sb("count", [P, slots, T, NP], F32)
        mask = sb("mask", [P, slots, T, NP], F32)
        loads = (m.c["grid_a"], m.c["grid_b"])
        logs, logged, ready, stored = (m.c[k] for k in ("logs_ready", "logs_done", "rows_ready", "stored"))
        with nc.Block() as block:
            @block.sync
            def _(sp):
                for n, r in enumerate(relations):
                    if n >= 2:
                        sp.wait_ge(stored.sem, stored.at(16 * (n - 1)))
                    sp.dma_start(count[:, n % 2], m.counts[r].rearrange("(t p) s -> p t s", p=P)).then_inc(loads[n % 2].sem, 16)
                    if n:
                        sp.wait_ge(ready.sem, ready.at(n))
                        sp.dma_start(m.logs[relations[n - 1]].rearrange("(t p) s -> p t s", p=P), count[:, (n - 1) % 2]).then_inc(stored.sem, 16)
                n = len(relations)
                sp.wait_ge(ready.sem, ready.at(n))
                sp.dma_start(m.logs[relations[n - 1]].rearrange("(t p) s -> p t s", p=P), count[:, (n - 1) % 2]).then_inc(stored.sem, 16)
                sp.wait_ge(stored.sem, stored.at(16 * n))

            @block.vector
            def _(dve):
                steps = Steps(dve, m.c["dve_step"])
                for n in range(len(relations)):
                    s = n % 2
                    dve.wait_ge(loads[s].sem, loads[s].at(16 * (n // 2 + 1)))
                    nc.vector.tensor_scalar(mask[:, s], count[:, s], 0.0, MASK, ALU.is_equal, ALU.mult)
                    steps.then(nc.vector.tensor_scalar(count[:, s], count[:, s], 1.0, None, ALU.max))
                    dve.sem_inc(logs.sem, 1)
                    dve.wait_ge(logged.sem, logged.at(n + 1))
                    steps.then(nc.vector.tensor_tensor(count[:, s], count[:, s], mask[:, s], ALU.add))
                    dve.sem_inc(ready.sem, 1)
                steps.done()

            @block.scalar
            def _(act):
                for n in range(len(relations)):
                    act.wait_ge(logs.sem, logs.at(n + 1))
                    nc.scalar.activation(count[:, n % 2], count[:, n % 2], ACT.Ln, bias=m.zero[:]).then_inc(logged.sem, 1)
        n = len(relations)
        loads[0].close(16 * ((n + 1) // 2)), loads[1].close(16 * (n // 2))
        logs.close(n), logged.close(n), ready.close(n), stored.close(16 * n)


def normalise(nc, m, src, dst, eps, scale=None, shift=None, turned=None):
    with ExitStack() as ctx:
        sb = scratch(nc, m, ctx)
        stats = sb("stats", [P, T, 2, 6], F32)
        mean = sb("mean", [P, T, 2], F32)
        dev = sb("dev", [P, T], F32)
        rdev = sb("rdev", [P, T], F32)
        affine = sb("affine", [P, 2, D], F32)
        var_ready, dev_ready, ready, params = (m.c[k] for k in ("variance_ready", "deviation_ready", "rows_ready", "params"))
        with nc.Block() as block:
            if scale is not None:
                @block.sync
                def _(sp):
                    sp.dma_start(affine[:, 0], scale.partition_broadcast(P)).then_inc(params.sem, 16)
                    sp.dma_start(affine[:, 1], shift.partition_broadcast(P)).then_inc(params.sem, 16)

            @block.vector
            def _(dve):
                steps = Steps(dve, m.c["dve_step"])
                for t in range(T):
                    for h in range(2):
                        ins = nc.vector.bn_stats(stats[:, t, h], src[:, t, h * 384:(h + 1) * 384])
                steps.then(ins)
                for t in range(T):
                    ins = nc.vector.bn_aggr(mean[:, t], stats[:, t].rearrange("p a b -> p (a b)"))
                ins.then_inc(var_ready.sem, 1)
                dve.wait_ge(dev_ready.sem, dev_ready.at(1))
                steps.then(nc.vector.reciprocal(rdev[:], dev[:]))
                if scale is not None:
                    dve.wait_ge(params.sem, params.at(32))
                for t in range(T):
                    ins = nc.vector.tensor_scalar(dst[:, t], src[:, t], mean[:, t, 0:1], rdev[:, t:t + 1],
                                                  ALU.subtract, ALU.mult)
                    if scale is not None:
                        steps.then(ins)
                        steps.then(nc.vector.tensor_tensor(dst[:, t], dst[:, t], affine[:, 0], ALU.mult))
                        ins = nc.vector.tensor_tensor(dst[:, t], dst[:, t], affine[:, 1], ALU.add)
                    ins.then_inc(ready.sem, 1)
                steps.done()

            if turned is not None:
                @block.tensor
                def _(pe):
                    turn_rows(nc, m, pe, dst)

            @block.scalar
            def _(act):
                act.wait_ge(var_ready.sem, var_ready.at(1))
                nc.scalar.activation(dev[:], mean[:, :, 1], ACT.Sqrt, bias=eps[:]).then_inc(dev_ready.sem, 1)
                if turned is not None:
                    save_turned(nc, m, act, turned)
        close_turn(m, 1 if turned is not None else 0)
        var_ready.close(1), dev_ready.close(1), ready.close(T)
        if scale is not None:
            params.close(32)


def turn_rows(nc, m, pe, rows, ready_made=False):
    ready, turned, saved = m.c["rows_ready"], m.c["transposed"], m.c["columns_ready"]
    nk = rows.shape[2] // P
    for t in range(T):
        if not ready_made:
            pe.wait_ge(ready.sem, ready.at(t + 1))
        pe.wait_ge(saved.sem, saved.at(t - 1))
        for k in range(nk):
            b = 2 * (t % 2) + k // 4
            ins = nc.tensor.transpose(m.psum[:, b, (k % 4) * P:(k % 4 + 1) * P], rows[:, t, k * P:(k + 1) * P], m.ident[:])
        ins.then_inc(turned.sem, 1)


def save_turned(nc, m, act, columns):
    turned, saved = m.c["transposed"], m.c["columns_ready"]
    nk = columns.shape[1]
    for t in range(T):
        act.wait_ge(turned.sem, turned.at(t + 1))
        for k0 in range(0, nk, 4):
            n = min(4, nk - k0)
            src = m.psum[:, 2 * (t % 2) + k0 // 4, 0:n * P].rearrange("p (k c) -> p k c", k=n)
            ins = nc.scalar.activation(columns[:, k0:k0 + n, t * P:(t + 1) * P], src, ACT.Copy)
        ins.then_inc(saved.sem, 1)


def close_turn(m, n):
    m.c["transposed"].close(n * T), m.c["columns_ready"].close(n * T)


def project(nc, m, columns, jobs, after=None):
    kk = columns.shape[1]
    width = jobs[0][0].shape[-1]
    parts = (width + 511) // 512
    w = width // parts
    load = (m.c["weights_a"], m.c["weights_b"])
    used, ready, saved = m.c["weights_used"], m.c["product_ready"], m.c["product_saved"]
    with ExitStack() as ctx:
        sb = scratch(nc, m, ctx)
        slots = min(2, len(jobs))
        weights = sb("weights", [P, slots, kk, width], F32)
        bias = sb("bias", [P, slots, width], F32)
        with nc.Block() as block:
            @block.sync
            def _(sp):
                for j, (wsrc, bsrc, _, _) in enumerate(jobs):
                    if j >= 2:
                        sp.wait_ge(used.sem, used.at(j - 1))
                        sp.wait_ge(saved.sem, saved.at((j - 1) * T))
                    c = load[j % 2]
                    sp.dma_start(weights[:, j % 2], wsrc.rearrange("(k p) f -> p k f", p=P)).then_inc(c.sem, 16)
                    if bsrc is not None:
                        sp.dma_start(bias[:, j % 2], bsrc.partition_broadcast(P)).then_inc(c.sem, 16)

            seen = []
            n_load = [0, 0]
            for j, job in enumerate(jobs):
                n_load[j % 2] += 16 if job[1] is None else 32
                seen.append(n_load[j % 2])

            @block.tensor
            def _(pe):
                for j in range(len(jobs)):
                    pe.wait_ge(load[j % 2].sem, load[j % 2].at(seen[j]))
                    for t in range(T):
                        u = j * T + t
                        pe.wait_ge(saved.sem, saved.at(u - 1))
                        for c in range(parts):
                            for k in range(kk):
                                ins = nc.tensor.matmul(m.psum[:, 2 * (u % 2) + c, 0:w], columns[:, k, t * P:(t + 1) * P],
                                                       weights[:, j % 2, k, c * w:(c + 1) * w],
                                                       start=(k == 0), stop=(k == kk - 1))
                        ins.then_inc(ready.sem, 1)
                    pe.wait_ge(ready.sem, ready.at((j + 1) * T))
                    pe.sem_inc(used.sem, 1)

            @block.vector
            def _(dve):
                steps = Steps(dve, m.c["dve_step"])
                for j, (_, bsrc, rows, factor) in enumerate(jobs):
                    for t in range(T):
                        u = j * T + t
                        dve.wait_ge(ready.sem, ready.at(u + 1))
                        src = m.psum[:, 2 * (u % 2):2 * (u % 2) + parts, 0:w]
                        out = rows[:, t, 0:width].rearrange("p (c w) -> p c w", c=parts)
                        if bsrc is not None:
                            ins = nc.vector.tensor_tensor(out, src, bias[:, j % 2].rearrange("p (c w) -> p c w", c=parts), ALU.add)
                        elif factor is not None:
                            ins = nc.vector.tensor_scalar(out, src, factor[:, t:t + 1], None, ALU.mult)
                        else:
                            ins = nc.vector.tensor_copy(out, src)
                        ins.then_inc(saved.sem, 1)
                if after is not None:
                    dve.wait_ge(saved.sem, saved.at(len(jobs) * T))
                    after(steps)
                steps.done()
        for k in range(2):
            load[k].close(n_load[k])
        used.close(len(jobs)), ready.close(len(jobs) * T), saved.close(len(jobs) * T)


def edge_scores(nc, m, fs, fd, attn, heads, grid, passes, saves):
    W = D + heads
    U = 8
    from_dram = m.from_dram[heads]
    to_dram = m.to_dram[heads]
    with ExitStack() as ctx:
        sb = scratch(nc, m, ctx)
        coef = sb("coef", [P, D], F32)
        low = sb("low", [P, D], F32)
        high = sb("high", [P, D], F32)
        work = sb("work", [P, T, D], F32)
        params, ready, stored = m.c["params"], m.c["rows_ready"], m.c["stored"]
        with nc.Block() as block:
            @block.sync
            def _(sp):
                sp.dma_start(coef[:], attn.partition_broadcast(P)).then_inc(params.sem, 16)
                sp.wait_ge(ready.sem, ready.at(1))
                sp.dma_start(from_dram.rearrange("(t p) d -> p t d", p=P), fs[:]).then_inc(stored.sem, 16)
                sp.wait_ge(ready.sem, ready.at(2))
                sp.dma_start(to_dram.rearrange("(t p) d -> p t d", p=P), fd[:]).then_inc(stored.sem, 16)
                sp.wait_ge(stored.sem, stored.at(32))

            @block.vector
            def _(dve):
                steps = Steps(dve, m.c["dve_step"])
                dve.wait_ge(params.sem, params.at(16))
                nc.vector.tensor_scalar(low[:], coef[:], 0.8, None, ALU.mult)
                steps.then(nc.vector.tensor_scalar(high[:], coef[:], 0.2, None, ALU.mult))
                for k, rows in enumerate((fs, fd)):
                    for t in range(T):
                        ins = nc.vector.tensor_tensor(work[:, t], rows[:, t, 0:D], high[:], ALU.mult)
                    steps.then(ins)
                    for t in range(T):
                        ins = nc.vector.tensor_reduce(rows[:, t, D:W], work[:, t].rearrange("p (h c) -> p h c", h=heads),
                                                      AX_X, ALU.add)
                    steps.then(ins)
                    dve.sem_inc(ready.sem, 1)
                steps.done()
        params.close(16), ready.close(2), stored.close(32)

        rows_of = sb("rows_of", [P, 2, 3, U], U32)
        both = sb("both", [P, U, W], F32)
        score = sb("score", [P, U, heads], F32)
        part = sb("part", [P, 2, heads], F32)
        C = len(passes)
        HOTS = 4
        distance = sb("distance", [P, 2, NP], F16)
        to_hot = sb("to_hot", [P, HOTS, NP], BF16)
        from_hot = sb("from_hot", [P, HOTS, NP], BF16)
        counts = sb("counts", [P, T, NP], F32)
        counts2 = sb("counts2", [P, T, NP], F32) if C == 2 else None
        rest = sb("rest", [P, 2, T, NP], F32) if C == 1 else None
        far = m.c["distance_step"]
        landed = [m.c[f"pair_{j}"] for j in range(U)]
        scored, scattered = m.c["score_ready"], m.c["scattered"]
        waited, copied = m.c["waited"], m.c["copied"]
        to_ready, from_ready, hots_used, counted, emptied = (
            m.c[k] for k in ("targets_ready", "sources_ready", "onehots_used", "counts_final", "counts_saved"))
        TURNS = ET // U
        ADD, SCATTER = 2, 5

        def wide(t):
            return m.psum[:, t, :]

        def narrow(t):
            return m.psum[:, T + t // 4, (t % 4) * P:(t % 4 + 1) * P]

        with nc.Block() as block:
            @block.gpsimd
            def _(pool):
                def after(counter, n):
                    pool.wait_ge(counter.sem, n)
                    pool.sem_inc(waited.sem, 1)

                def turn(i, parity, first=False, last=False):
                    if not last:
                        cols = bass.ds(i * U, U)
                        nc.gpsimd.tensor_copy(rows_of[:, parity, 0], m.from_row[:, cols])
                        nc.gpsimd.tensor_copy(rows_of[:, parity, 1], m.to_row[:, cols])
                        nc.gpsimd.tensor_copy(rows_of[:, parity, 2], m.cell[:, cols]).then_inc(copied.sem, 1)
                        after(copied, copied.at(i + 1))
                    for j in range(U):
                        if not last:
                            nc.gpsimd.indirect_dma_start(
                                out=both[:, j], out_offset=None, in_=from_dram,
                                in_offset=bass.IndirectOffsetOnAxis(ap=rows_of[:, parity, 0, j:j + 1], axis=0)).then_inc(landed[j].sem, 16)
                        same = j >= ADD
                        if same and not last or not same and not first:
                            k, q, of = (j - ADD) % U, parity if same else 1 - parity, i if same else i - 1
                            after(landed[k], landed[k].at(32 * of + 16))
                            nc.gpsimd.indirect_dma_start(
                                out=both[:, k], out_offset=None, in_=to_dram,
                                in_offset=bass.IndirectOffsetOnAxis(ap=rows_of[:, q, 1, k:k + 1], axis=0),
                                compute_op=ALU.add).then_inc(landed[k].sem, 16)
                        same = j >= SCATTER
                        if same and not last or not same and not first:
                            k, q, n = (j - SCATTER) % U, parity if same else 1 - parity, i * U + j - SCATTER
                            after(scored, scored.at(n + 1))
                            after(scattered, scattered.at(16 * n))
                            nc.gpsimd.indirect_dma_start(
                                out=grid, out_offset=bass.IndirectOffsetOnAxis(ap=rows_of[:, q, 2, k:k + 1], axis=0),
                                in_=score[:, k], in_offset=None).then_inc(scattered.sem, 16)

                turn(0, 0, first=True)
                with pool.Fori(0, TURNS // 2 - 1) as i:
                    turn(2 * i + 1, 1)
                    turn(2 * i + 2, 0)
                turn(TURNS - 1, 1)
                turn(TURNS, 0, last=True)
                pool.wait_ge(scattered.sem, scattered.at(16 * ET))

            @block.vector
            def _(dve):
                steps = Steps(dve, m.c["dve_step"])

                def turns(start, end, n_pass):
                    with steps.loop(start, end, 2 * U) as i:
                        for j in range(U):
                            for c in range(C):
                                q = C * (U * i + j) + c
                                tile = q - n_pass * ET
                                dve.wait_ge(hots_used.sem, hots_used.at(q - HOTS + 1))
                                nc.vector.tensor_scalar(from_hot[:, (C * j + c) % HOTS], m.iota16[:], m.counted[:, passes[n_pass], bass.ds(tile, 1)],
                                                        None, ALU.is_equal).then_inc(from_ready.sem, 1)
                            dve.wait_ge(landed[j].sem, landed[j].at(32 * i + 32))
                            steps.then(nc.vector.scalar_tensor_tensor(work[:, j % 2], both[:, j, 0:D], 0.0, low[:], ALU.max, ALU.mult))
                            steps.then(nc.vector.tensor_reduce(part[:, j % 2], work[:, j % 2].rearrange("p (h c) -> p h c", h=heads),
                                                               AX_X, ALU.add))
                            nc.vector.tensor_tensor(score[:, j], part[:, j % 2], both[:, j, D:W], ALU.add).then_inc(scored.sem, 1)

                def save_counts(n_pass, to):
                    dve.wait_ge(counted.sem, counted.at(n_pass + 1))
                    nc.vector.tensor_copy(to[:, :, 0:512], m.psum[:, 0:T, :])
                    nc.vector.tensor_copy(to[:, 0:4, 512:NP], m.psum[:, T, :].rearrange("p (t c) -> p t c", t=4))
                    nc.vector.tensor_copy(to[:, 4, 512:NP], narrow(4)).then_inc(emptied.sem, 1)

                for k in range(C):
                    turns(k * TURNS // C, (k + 1) * TURNS // C, k)
                    save_counts(k, (counts, counts2)[k])
                if C == 1:
                    dve.wait_ge(params.sem, params.at(32))
                    dve.wait_ge(emptied.sem, emptied.at(1))
                    steps.then(nc.vector.tensor_tensor(rest[:, 0], rest[:, 0], rest[:, 1], ALU.subtract))
                    nc.vector.tensor_tensor(rest[:, 0], rest[:, 0], counts[:], ALU.subtract).then_inc(emptied.sem, 1)
                steps.done()

            @block.scalar
            def _(act):
                def turns(start, end, n_pass):
                    with act.Fori(start, end) as i:
                        for j in range(U * C):
                            q = C * U * i + j
                            tile = q - n_pass * ET
                            act.wait_ge(far.sem, far.at(2 * q - 2))
                            nc.scalar.activation(distance[:, j % 2], m.iota16[:], ACT.Abs, bias=m.minus_to[:, bass.ds(tile, 1)]).then_inc(far.sem, 1)
                            act.wait_ge(hots_used.sem, hots_used.at(q - HOTS + 1))
                            act.wait_ge(far.sem, far.at(2 * q + 1))
                            nc.scalar.activation(to_hot[:, j % HOTS], distance[:, j % 2], ACT.Relu, bias=m.ones[:, 0:1], scale=-1.0).then_inc(to_ready.sem, 1)
                            act.sem_inc(far.sem, 1)

                for k in range(C):
                    turns(k * TURNS // C, (k + 1) * TURNS // C, k)

            @block.tensor
            def _(pe):
                def product(q, slot, first=False, last=False):
                    pe.wait_ge(to_ready.sem, to_ready.at(q + 1))
                    pe.wait_ge(from_ready.sem, from_ready.at(q + 1))
                    for t in range(T):
                        rows = to_hot[:, slot, t * P:(t + 1) * P]
                        nc.tensor.matmul(wide(t), rows, from_hot[:, slot, 0:512], start=first, stop=last)
                        ins = nc.tensor.matmul(narrow(t), rows, from_hot[:, slot, 512:NP], start=first and t % 4 == 0,
                                               stop=last and t % 4 == 3 or last and t == T - 1, skip_group_check=True)
                    ins.then_inc(hots_used.sem, 1)

                for n_pass in range(C):
                    if n_pass:
                        pe.wait_ge(emptied.sem, emptied.at(n_pass))
                    q = n_pass * ET
                    for j in range(HOTS):
                        product(q + j, j, first=(j == 0))
                    with pe.Fori(1, ET // HOTS - 1) as i:
                        for j in range(HOTS):
                            product(q + HOTS * i + j, j)
                    for j in range(HOTS):
                        product(q + ET - HOTS + j, j, last=(j == HOTS - 1))
                    pe.wait_ge(hots_used.sem, hots_used.at(q + ET))
                    pe.sem_inc(counted.sem, 1)

            @block.sync
            def _(sp):
                rows = lambda k: m.counts[k].rearrange("(t p) s -> p t s", p=P)
                if C == 1:
                    sp.dma_start(rest[:, 0], rows(3)).then_inc(params.sem, 16)
                    sp.dma_start(rest[:, 1], rows(0)).then_inc(params.sem, 16)
                for k, to in enumerate(saves):
                    sp.wait_ge(emptied.sem, emptied.at(k + 1))
                    sp.dma_start(rows(to), (rest[:, 0] if C == 1 else counts2[:]) if k else counts[:]).then_inc(stored.sem, 16)
                sp.wait_ge(stored.sem, stored.at(16 * len(saves)))
        for c in landed:
            c.close(32 * TURNS)
        scored.close(ET), scattered.close(16 * ET), copied.close(TURNS), far.close(2 * C * ET)
        to_ready.close(C * ET), from_ready.close(C * ET), hots_used.close(C * ET), counted.close(C), emptied.close(2)
        stored.close(16 * len(saves))
        if C == 1:
            params.close(32)


def attend(nc, m, relations, heads, width, values, out, grid=None, broad=None, near=None, logs=()):
    R, Hn = relations, heads
    parts = (width + 511) // 512
    w = width // parts
    load = (m.c["grid_a"], m.c["grid_b"])
    names = ("grid_used", "sum_ready", "sum_used", "max_ready", "probs_ready", "probs_used", "turned", "turned_saved",
             "mixed", "mixed_saved")
    a_ready = m.c["last_sum_ready"]
    g_used, s_ready, s_used, x_ready, p_ready, p_used, t_ready, t_saved, o_ready, o_saved = (m.c[k] for k in names)
    n_load = 1 + (grid is not None)
    with ExitStack() as ctx:
        sb = scratch(nc, m, ctx)
        log = sb("log_t", [P, 2, R, NP], F32)
        cells = sb("cells", [P, 2, NP, Hn], F32) if grid is not None else None
        total = sb("sum_t", [P, 2, R, NP], F32)
        score = sb("score_t", [P, 2, R, NP], F32)
        top = sb("top", [P, 2, R + 2], F32)
        probs = sb("probs", [P, 2, R, NP], F32)
        mass = sb("mass", [P, 4, R], F32)
        share = sb("share", [P, 2, 2], F32)
        turned = sb("turned_t", [P, 2, R, NP], F32)
        with nc.Block() as block:
            @block.sync
            def _(sp):
                for t in range(T):
                    if t >= 2:
                        sp.wait_ge(g_used.sem, g_used.at(t - 1))
                    c = load[t % 2]
                    rows = slice(t * P, (t + 1) * P)
                    for r in range(R):
                        sp.dma_start(log[:, t % 2, r], m.logs[logs[r]][rows]).then_inc(c.sem, 16)
                    if grid is not None:
                        sp.dma_start(cells[:, t % 2], grid.rearrange("(d s) h -> d s h", s=NP)[rows]).then_inc(c.sem, 16)

            pool_part = R if R == 1 else R - 1
            if grid is None:
                @block.gpsimd
                def _(pool):
                    for t in range(T):
                        for h in range(Hn):
                            u = t * Hn + h
                            if u >= 2:
                                pool.wait_ge(s_used.sem, s_used.at(u - 1))
                            for r in range(pool_part):
                                ins = nc.gpsimd.tensor_scalar(total[:, u % 2, r], broad[:, r * Hn + h],
                                                              near[:, t, r * Hn + h:r * Hn + h + 1], None, ALU.add)
                            ins.then_inc(s_ready.sem, 1)

            @block.vector
            def _(dve):
                steps = Steps(dve, m.c["dve_step"])

                def scores(t, h):
                    u = t * Hn + h
                    s = u % 2
                    if h == 0:
                        n = (R + (grid is not None)) * 16 * (t // 2 + 1)
                        dve.wait_ge(load[t % 2].sem, load[t % 2].at(n))
                    if u >= 2:
                        dve.wait_ge(p_ready.sem, p_ready.at(u - 1))
                    if grid is None:
                        dve.wait_ge(s_ready.sem, s_ready.at(u + 1))
                        if pool_part < R:
                            dve.wait_ge(a_ready.sem, a_ready.at(u + 1))
                        for r in range(R):
                            ins = nc.vector.scalar_tensor_tensor(total[:, s, r], total[:, s, r], 0.2, total[:, s, r], ALU.mult, ALU.max)
                        steps.then(ins)
                    for r in range(R):
                        part = cells[:, t % 2, :, h] if grid is not None else total[:, s, r]
                        ins = nc.vector.tensor_tensor_reduce(out=score[:, s, r], in0=part, in1=log[:, t % 2, r], scale=1.0,
                                                             scalar=FLOOR, op0=ALU.add, op1=ALU.max,
                                                             accum_out=top[:, s, r:r + 1])
                    steps.then(ins)
                    if grid is None:
                        dve.sem_inc(s_used.sem, 1)
                    if h == Hn - 1:
                        dve.sem_inc(g_used.sem, 1)
                    if R > 1:
                        steps.then(nc.vector.tensor_reduce(top[:, s, R:R + 1], top[:, s, 0:R], AX_X, ALU.max))
                    last = top[:, s, R:R + 1] if R > 1 else top[:, s, 0:1]
                    nc.vector.tensor_scalar(top[:, s, R + 1:R + 2], last, -1.0, None, ALU.mult).then_inc(x_ready.sem, 1)

                def save(t, h):
                    u = t * Hn + h
                    s = u % 2
                    dve.wait_ge(p_ready.sem, p_ready.at(u + 1))
                    if R > 1:
                        steps.then(nc.vector.tensor_reduce(share[:, s, 0:1], mass[:, u % 4, :], AX_X, ALU.add))
                        steps.then(nc.vector.tensor_scalar(share[:, s, 0:1], share[:, s, 0:1], 1e-16, None, ALU.add))
                    else:
                        steps.then(nc.vector.tensor_scalar(share[:, s, 0:1], mass[:, u % 4, 0:1], 1e-16, None, ALU.add))
                    steps.then(nc.vector.reciprocal(share[:, s, 1:2], share[:, s, 0:1]))
                    dve.wait_ge(o_ready.sem, o_ready.at(u + 1))
                    if parts == 1:
                        src, dst = m.psum[:, 4 + 2 * s, 0:w], out[:, t, h * w:(h + 1) * w]
                    else:
                        src = m.psum[:, 4 + 2 * s:6 + 2 * s, 0:w]
                        dst = out[:, t, 0:width].rearrange("p (c w) -> p c w", c=parts)
                    nc.vector.tensor_scalar(dst, src, share[:, s, 1:2], None, ALU.mult).then_inc(o_saved.sem, 1)

                units = [(t, h) for t in range(T) for h in range(Hn)]
                LAG = 2
                for n, unit in enumerate(units):
                    scores(*unit)
                    if n >= LAG:
                        save(*units[n - LAG])
                for unit in units[-LAG:]:
                    save(*unit)
                steps.done()

            @block.scalar
            def _(act):
                def last_sum(u):
                    t, h = divmod(u, Hn)
                    if u >= 2:
                        act.wait_ge(s_used.sem, s_used.at(u - 1))
                    r = R - 1
                    nc.scalar.activation(total[:, u % 2, r], broad[:, r * Hn + h], ACT.Identity,
                                         bias=near[:, t, r * Hn + h:r * Hn + h + 1]).then_inc(a_ready.sem, 1)

                def exponents(u):
                    s = u % 2
                    act.wait_ge(x_ready.sem, x_ready.at(u + 1))
                    if u >= 2:
                        act.wait_ge(p_used.sem, p_used.at(u - 1))
                    if u >= 4:
                        act.wait_ge(o_saved.sem, o_saved.at(u - 3))
                    for r in range(R):
                        ins = nc.scalar.activation(probs[:, s, r], score[:, s, r], ACT.Exp, bias=top[:, s, R + 1:R + 2],
                                                   accum_out=mass[:, u % 4, r:r + 1])
                    ins.then_inc(p_ready.sem, 1)

                def save_turned_probs(u):
                    if u >= 2:
                        act.wait_ge(o_ready.sem, o_ready.at(u - 1))
                    for r in range(R):
                        v = u * R + r
                        act.wait_ge(t_ready.sem, t_ready.at(v + 1))
                        b = 2 * (v % 2)
                        nc.scalar.activation(turned[:, u % 2, r, 0:512], m.psum[:, b, :], ACT.Copy)
                        nc.scalar.activation(turned[:, u % 2, r, 512:NP], m.psum[:, b + 1, 0:P], ACT.Copy).then_inc(t_saved.sem, 1)

                lag = 1 if R == 1 else 0
                if pool_part < R:
                    last_sum(0)
                for u in range(T * Hn):
                    if pool_part < R and u + 1 < T * Hn:
                        last_sum(u + 1)
                    exponents(u)
                    if u >= lag:
                        save_turned_probs(u - lag)
                if lag:
                    save_turned_probs(T * Hn - 1)

            @block.tensor
            def _(pe):
                def turn(u):
                    pe.wait_ge(p_ready.sem, p_ready.at(u + 1))
                    for r in range(R):
                        v = u * R + r
                        if v >= 2:
                            pe.wait_ge(t_saved.sem, t_saved.at(v - 1))
                        for c in range(T):
                            b = 2 * (v % 2) + c // 4
                            ins = nc.tensor.transpose(m.psum[:, b, (c % 4) * P:(c % 4 + 1) * P], probs[:, u % 2, r, c * P:(c + 1) * P],
                                                      m.ident[:])
                        ins.then_inc(t_ready.sem, 1)
                    pe.wait_ge(t_ready.sem, t_ready.at((u + 1) * R))
                    pe.sem_inc(p_used.sem, 1)

                def mix(u):
                    h = u % Hn
                    if u >= 2:
                        pe.wait_ge(o_saved.sem, o_saved.at(u - 1))
                    pe.wait_ge(t_saved.sem, t_saved.at((u + 1) * R))
                    for c in range(parts):
                        for r in range(R):
                            for k in range(T):
                                ins = nc.tensor.matmul(m.psum[:, 4 + 2 * (u % 2) + c, 0:w], turned[:, u % 2, r, k * P:(k + 1) * P],
                                                       values[r][:, k, h * width + c * w:h * width + (c + 1) * w],
                                                       start=(r == 0 and k == 0), stop=(r == R - 1 and k == T - 1))
                    ins.then_inc(o_ready.sem, 1)

                for u in range(T * Hn):
                    turn(u)
                    if u:
                        mix(u - 1)
                mix(T * Hn - 1)
        U = T * Hn
        per = (R + (grid is not None)) * 16
        load[0].close(per * ((T + 1) // 2)), load[1].close(per * (T // 2))
        g_used.close(T), x_ready.close(U), p_ready.close(U), p_used.close(U), t_ready.close(U * R), t_saved.close(U * R)
        o_ready.close(U), o_saved.close(U)
        if grid is None:
            s_ready.close(U), s_used.close(U)
            if R > 1:
                a_ready.close(U)


def elu_rows(nc, m, rows, bias=None, plus=None):
    width = rows.shape[2]
    e_ready, e_done, params = m.c["elu_ready"], m.c["elu_done"], m.c["params"]
    with ExitStack() as ctx:
        sb = scratch(nc, m, ctx)
        low = sb("low_part", [P, T, D], F32)
        row = sb("row", [P, D], F32)
        with nc.Block() as block:
            if bias is not None:
                @block.sync
                def _(sp):
                    sp.dma_start(row[:], bias.partition_broadcast(P)).then_inc(params.sem, 16)

            @block.vector
            def _(dve):
                steps = Steps(dve, m.c["dve_step"])
                if bias is not None:
                    dve.wait_ge(params.sem, params.at(16))
                    for t in range(T):
                        ins = nc.vector.tensor_tensor(rows[:, t, 0:D], rows[:, t, 0:D], row[:], ALU.add)
                    steps.then(ins)
                for t in range(T):
                    nc.vector.tensor_scalar(low[:, t], rows[:, t, 0:D], 0.0, None, ALU.min).then_inc(e_ready.sem, 1)
                for t in range(T):
                    dve.wait_ge(e_done.sem, e_done.at(t + 1))
                    ins = nc.vector.scalar_tensor_tensor(rows[:, t, 0:D], low[:, t], -1.0, rows[:, t, 0:D], ALU.add, ALU.max)
                    if plus is not None:
                        steps.then(ins)
                        steps.then(nc.vector.tensor_tensor(rows[:, t, 0:D], rows[:, t, 0:D], plus[:, t], ALU.add))
                steps.done()

            @block.scalar
            def _(act):
                for t in range(T):
                    act.wait_ge(e_ready.sem, e_ready.at(t + 1))
                    nc.scalar.activation(low[:, t], low[:, t], ACT.Exp, bias=m.zero[:]).then_inc(e_done.sem, 1)
        e_ready.close(T), e_done.close(T)
        if bias is not None:
            params.close(16)


def add_rows(nc, m, out, a, b):
    with nc.Block() as block:
        @block.vector
        def _(dve):
            nc.vector.tensor_tensor(out, a, b, ALU.add)


def gat_v2_block(nc, m, g):
    normalise(nc, m, m.X, m.H, m.eps5, turned=m.HT)
    with ExitStack() as ctx:
        sb = scratch(nc, m, ctx)
        out = sb("out_rows", [P, T, D], F32)
        for layer, (heads, names) in enumerate(((8, ("W1s", "b1s", "W1d", "b1d", "attn1")), (1, ("Wos", "bos", "Wod", "bod", "attno")))):
            ws, bs, wd, bd, attn = (g["L0_gnn_" + k] for k in names)
            with ExitStack() as inner:
                fs = scratch(nc, m, inner)("fs", [P, T, D + heads], F32)
                with nc.sbuf_tensor(f"fd_{heads}", [P, T, D + heads], F32) as fd:
                    project(nc, m, m.HT, [(ws, bs, fs, None), (wd, bd, fd, None)])
                    grid = m.grid if heads == 8 else m.grid1
                    passes, saves = ((0, 1), (3, 0)) if layer == 0 else ((2,), (1, 2))
                    edge_scores(nc, m, fs, fd, attn.rearrange("h c -> (h c)"), heads, grid, passes, saves)
                log_counts(nc, m, [3] if layer == 0 else [0, 1, 2])
                attend(nc, m, 1, heads, D // heads, [fs], out, grid=grid, logs=(3,))
            if layer == 0:
                elu_rows(nc, m, out, plus=m.H)
                normalise(nc, m, out, m.H, m.eps5, g["L0_gnn_ln1_w"], g["L0_gnn_ln1_b"], turned=m.HT)
            else:
                elu_rows(nc, m, out)
                normalise(nc, m, out, m.H, m.eps5, g["L0_gnn_lno_w"], g["L0_gnn_lno_b"])
                add_rows(nc, m, m.X[:], m.X[:], m.H[:])


def first_largest(nc, steps, values, work, top, chosen, rank):
    n = values.shape[2]
    shape = [P, T, n]
    ranks = rank[:, 0:n].unsqueeze(1).to_broadcast(shape)
    steps.then(nc.vector.tensor_reduce(top[:, :, 0], values, AX_X, ALU.max))
    steps.then(nc.vector.tensor_tensor(work, values, top[:, :, 0:1].to_broadcast(shape), ALU.is_lt))
    steps.then(nc.vector.scalar_tensor_tensor(work, work, float(n), ranks, ALU.mult, ALU.add))
    steps.then(nc.vector.tensor_reduce(top[:, :, 1], work, AX_X, ALU.min))
    steps.then(nc.vector.tensor_tensor(chosen, ranks, top[:, :, 1:2].to_broadcast(shape), ALU.is_equal))


def switch_block(nc, m, g):
    E, F, CAP = 16, 96, 64
    normalise(nc, m, m.X, m.H, m.eps5)
    with ExitStack() as ctx:
        sb = scratch(nc, m, ctx)
        N = sb("normed", [P, T, D], F32)
        logits = sb("logits", [P, T, E], F32)
        chance = sb("chance", [P, T], F32)
        passed = sb("passed", [P, T], F32)
        kept = sb("kept", [P, T, E], F32)
        keptT = sb("keptT", [E, NP], F32)
        params, v_ready, d_ready, ready = (m.c[k] for k in ("params", "variance_ready", "deviation_ready", "rows_ready"))
        with ExitStack() as inner:
            sb2 = scratch(nc, m, inner)
            row = sb2("ln_w", [P, D], F32)
            square = sb2("square", [P, T], F32)
            dev = sb2("dev", [P, T], F32)
            junk = sb2("junk", [P, D], F32)
            with nc.Block() as block:
                @block.sync
                def _(sp):
                    sp.dma_start(row[:], g["L0_ffn_ln_w"].partition_broadcast(P)).then_inc(params.sem, 16)

                @block.vector
                def _(dve):
                    steps = Steps(dve, m.c["dve_step"])
                    for t in range(T):
                        steps.then(nc.vector.tensor_tensor_reduce(out=junk[:], in0=m.H[:, t], in1=m.H[:, t], scale=1.0, scalar=0.0,
                                                                  op0=ALU.mult, op1=ALU.add, accum_out=square[:, t:t + 1]))
                    dve.sem_inc(v_ready.sem, 1)
                    dve.wait_ge(d_ready.sem, d_ready.at(1))
                    steps.then(nc.vector.reciprocal(dev[:], dev[:]))
                    dve.wait_ge(params.sem, params.at(16))
                    for t in range(T):
                        nc.vector.scalar_tensor_tensor(N[:, t], m.H[:, t], dev[:, t:t + 1], row[:], ALU.mult, ALU.mult).then_inc(ready.sem, 1)
                    steps.done()

                @block.tensor
                def _(pe):
                    turn_rows(nc, m, pe, N)

                @block.scalar
                def _(act):
                    act.wait_ge(v_ready.sem, v_ready.at(1))
                    nc.scalar.activation(dev[:], square[:], ACT.Sqrt, bias=m.eps6[:], scale=1.0 / D).then_inc(d_ready.sem, 1)
                    save_turned(nc, m, act, m.HT)
            params.close(16), v_ready.close(1), d_ready.close(1), ready.close(T), close_turn(m, 1)
        project(nc, m, m.HT, [(g["L0_ffn_w_router"], None, logits, None)])
        with ExitStack() as inner:
            sb2 = scratch(nc, m, inner)
            work, chosen, power = (sb2(k, [P, T, E], F32) for k in ("work", "chosen", "power"))
            top = sb2("top", [P, T, 2], F32)
            e_ready, e_done = m.c["elu_ready"], m.c["elu_done"]
            t_ready, t_saved, o_ready, o_saved = (m.c[k] for k in ("turned", "turned_saved", "mixed", "mixed_saved"))
            with nc.Block() as block:
                @block.vector
                def _(dve):
                    steps = Steps(dve, m.c["dve_step"])
                    first_largest(nc, steps, logits[:], work[:], top, chosen[:], m.rank)
                    dve.sem_inc(ready.sem, 1)
                    steps.then(nc.vector.tensor_tensor(power[:], logits[:], top[:, :, 0:1].to_broadcast([P, T, E]), ALU.subtract))
                    dve.sem_inc(e_ready.sem, 1)
                    dve.wait_ge(o_ready.sem, o_ready.at(1))
                    places = m.psum[:, 0, 0:T * E].rearrange("p (t e) -> p t e", t=T)
                    steps.then(nc.vector.scalar_tensor_tensor(kept[:], places, float(CAP), chosen[:], ALU.is_le, ALU.mult))
                    dve.sem_inc(o_saved.sem, 1)
                    steps.then(nc.vector.tensor_reduce(passed[:], kept[:], AX_X, ALU.add))
                    steps.then(nc.vector.tensor_scalar(passed[:], passed[:], -1.0, 1.0, ALU.mult, ALU.add))
                    dve.wait_ge(e_done.sem, e_done.at(1))
                    steps.then(nc.vector.tensor_reduce(chance[:], power[:], AX_X, ALU.add))
                    steps.then(nc.vector.reciprocal(chance[:], chance[:]))
                    dve.wait_ge(t_ready.sem, t_ready.at(1))
                    nc.vector.tensor_copy(keptT[:, 0:512], m.psum[0:E, 1, :])
                    steps.then(nc.vector.tensor_copy(keptT[:, 512:NP], m.psum[0:E, 2, 0:P]))
                    steps.done()

                @block.scalar
                def _(act):
                    act.wait_ge(e_ready.sem, e_ready.at(1))
                    nc.scalar.activation(power[:], power[:], ACT.Exp, bias=m.zero[:]).then_inc(e_done.sem, 1)

                @block.tensor
                def _(pe):
                    pe.wait_ge(ready.sem, ready.at(1))
                    for t in range(T):
                        for k in range(t + 1):
                            ins = nc.tensor.matmul(m.psum[:, 0, t * E:(t + 1) * E], m.after[:] if k == t else m.ones[:],
                                                   chosen[:, k], start=(k == 0), stop=(k == t))
                    ins.then_inc(o_ready.sem, 1)
                    pe.wait_ge(o_saved.sem, o_saved.at(1))
                    for t in range(T):
                        ins = nc.tensor.transpose(m.psum[0:E, 1 + t // 4, (t % 4) * P:(t % 4 + 1) * P], kept[:, t], m.ident[:])
                    ins.then_inc(t_ready.sem, 1)
            ready.close(1), e_ready.close(1), e_done.close(1), o_ready.close(1), o_saved.close(1), t_ready.close(1)

        wi = sb("wi", [P, KD, E * F], F32)
        wo = sb("wo", [F, E, D], F32)
        hidden = sb("hidden", [F, E, NP], F32)
        pick = sb("pick", [E, E, F], F32)
        load, h_ready, h_done, used, s_ready, s_done = (
            m.c[k] for k in ("weights_a", "hidden_ready", "hidden_done", "hidden_used", "second_ready", "second_done"))
        with nc.Block() as block:
            @block.sync
            def _(sp):
                sp.dma_start(wi[:], g["L0_ffn_wi"].rearrange("(k p) f -> p k f", p=P)).then_inc(load.sem, 16)
                sp.dma_start(wo[:], g["L0_ffn_wo"].rearrange("e f d -> f e d")).then_inc(load.sem, 16)

            @block.tensor
            def _(pe):
                pe.wait_ge(load.sem, load.at(32))
                pe.wait_ge(ready.sem, ready.at(1))
                for e in range(E):
                    if e >= 1:
                        pe.wait_ge(used.sem, used.at(e))
                    for c in range(2):
                        cols = slice(c * HALF, (c + 1) * HALF)
                        for k in range(KD):
                            ins = nc.tensor.matmul(m.psum[0:F, c, 0:HALF], wi[:, k, e * F:(e + 1) * F], m.HT[:, k, cols],
                                                   start=(k == 0), stop=(k == KD - 1))
                        ins = nc.tensor.matmul(m.psum[0:F, 2 + c, 0:HALF], pick[:, e], keptT[:, cols], start=True, stop=True)
                    ins.then_inc(h_ready.sem, 1)
                pe.wait_ge(used.sem, used.at(E))
                for t in range(T):
                    if t >= 2:
                        pe.wait_ge(s_done.sem, s_done.at(t - 1))
                    for c in range(2):
                        for e in range(E):
                            ins = nc.tensor.matmul(m.psum[:, 4 + 2 * (t % 2) + c, 0:384], hidden[:, e, t * P:(t + 1) * P],
                                                   wo[:, e, c * 384:(c + 1) * 384], start=(e == 0), stop=(e == E - 1))
                    ins.then_inc(s_ready.sem, 1)

            @block.scalar
            def _(act):
                for e in range(E):
                    act.wait_ge(h_ready.sem, h_ready.at(e + 1))
                    nc.scalar.activation(hidden[:, e].rearrange("p (c n) -> p c n", c=2), m.psum[0:F, 0:2, 0:HALF],
                                         ACT.Relu).then_inc(h_done.sem, 1)

            @block.vector
            def _(dve):
                steps = Steps(dve, m.c["dve_step"])
                nc.vector.tensor_copy(pick[:], m.ident[0:E, 0:E].unsqueeze(2).to_broadcast([E, E, F])).then_inc(ready.sem, 1)
                for e in range(E):
                    dve.wait_ge(h_done.sem, h_done.at(e + 1))
                    own = hidden[:, e].rearrange("p (c n) -> p c n", c=2)
                    nc.vector.tensor_tensor(own, own, m.psum[0:F, 2:4, 0:HALF], ALU.mult).then_inc(used.sem, 1)
                for t in range(T):
                    dve.wait_ge(s_ready.sem, s_ready.at(t + 1))
                    two = lambda rows: rows[:, t].rearrange("p (c w) -> p c w", c=2)
                    steps.then(nc.vector.scalar_tensor_tensor(two(N), two(N), passed[:, t:t + 1], m.psum[:, 4 + 2 * (t % 2):6 + 2 * (t % 2), 0:384],
                                                              ALU.mult, ALU.add))
                    dve.sem_inc(s_done.sem, 1)
                    steps.then(nc.vector.scalar_tensor_tensor(m.H[:, t], N[:, t], chance[:, t:t + 1], m.H[:, t], ALU.mult, ALU.add))
                    steps.then(nc.vector.tensor_tensor(m.X[:, t], m.X[:, t], m.H[:, t], ALU.add))
                steps.done()
        load.close(32), ready.close(1), h_ready.close(E), h_done.close(E), used.close(E), s_ready.close(T), s_done.close(T)


def spread(nc, m, rows, n, broad):
    total = rows.shape[2]
    t_ready, t_saved, o_ready, o_saved, ready = (m.c[k] for k in ("turned", "turned_saved", "mixed", "mixed_saved", "rows_ready"))
    with ExitStack() as ctx:
        sb = scratch(nc, m, ctx)
        pick = sb("pick", [total, n, P], F32)
        turned = sb("turned_s", [total, NP], F32)
        with nc.Block() as block:
            @block.vector
            def _(dve):
                nc.vector.tensor_copy(pick[:], m.ident[0:total, 0:n].unsqueeze(2).to_broadcast([total, n, P])).then_inc(ready.sem, 1)

            @block.tensor
            def _(pe):
                for t in range(T):
                    ins = nc.tensor.transpose(m.psum[0:total, t // 4, (t % 4) * P:(t % 4 + 1) * P], rows[:, t], m.ident[:])
                ins.then_inc(t_ready.sem, 1)
                pe.wait_ge(ready.sem, ready.at(1))
                pe.wait_ge(t_saved.sem, t_saved.at(1))
                for j in range(n):
                    if j >= 2:
                        pe.wait_ge(o_saved.sem, o_saved.at(j - 1))
                    for c in range(2):
                        ins = nc.tensor.matmul(m.psum[:, 4 + 2 * (j % 2) + c, 0:HALF], pick[:, j], turned[:, c * HALF:(c + 1) * HALF],
                                               start=True, stop=True)
                    ins.then_inc(o_ready.sem, 1)

            @block.scalar
            def _(act):
                act.wait_ge(t_ready.sem, t_ready.at(1))
                nc.scalar.activation(turned[:, 0:512], m.psum[0:total, 0, :], ACT.Copy)
                nc.scalar.activation(turned[:, 512:NP], m.psum[0:total, 1, 0:P], ACT.Copy).then_inc(t_saved.sem, 1)
                for j in range(n):
                    act.wait_ge(o_ready.sem, o_ready.at(j + 1))
                    b = 4 + 2 * (j % 2)
                    nc.scalar.activation(broad[:, j].rearrange("p (c n) -> p c n", c=2), m.psum[:, b:b + 2, 0:HALF],
                                         ACT.Copy).then_inc(o_saved.sem, 1)
        ready.close(1), t_ready.close(1), t_saved.close(1), o_ready.close(n), o_saved.close(n)


def head_scores(nc, m, values, att_s, att_d, heads, scores):
    width = values.shape[2]
    params = m.c["params"]
    with ExitStack() as ctx:
        sb = scratch(nc, m, ctx)
        att = sb("att", [P, 2, width], F32)
        work = sb("work", [P, 2, width], F32)
        with nc.Block() as block:
            @block.sync
            def _(sp):
                for k, a in enumerate((att_s, att_d)):
                    sp.dma_start(att[:, k], a.rearrange("h c -> (h c)").partition_broadcast(P)).then_inc(params.sem, 16)

            @block.vector
            def _(dve):
                steps = Steps(dve, m.c["dve_step"])
                dve.wait_ge(params.sem, params.at(32))
                for t in range(T):
                    for k in range(2):
                        ins = nc.vector.tensor_tensor(work[:, k], values[:, t], att[:, k], ALU.mult)
                    steps.then(ins)
                    for k in range(2):
                        ins = nc.vector.tensor_reduce(scores[:, t, k * heads:(k + 1) * heads],
                                                      work[:, k].rearrange("p (h c) -> p h c", h=heads), AX_X, ALU.add)
                    steps.then(ins)
                steps.done()
        params.close(32)


def finish_rows(nc, m, rows, bias, turned=None, relu=False, onto=None):
    width = rows.shape[2]
    params, ready = m.c["params"], m.c["rows_ready"]
    with ExitStack() as ctx:
        sb = scratch(nc, m, ctx)
        row = sb("row", [P, width], F32)
        with nc.Block() as block:
            @block.sync
            def _(sp):
                sp.dma_start(row[:], bias.partition_broadcast(P)).then_inc(params.sem, 16)

            @block.vector
            def _(dve):
                steps = Steps(dve, m.c["dve_step"])
                dve.wait_ge(params.sem, params.at(16))
                for t in range(T):
                    ins = nc.vector.tensor_tensor(rows[:, t], rows[:, t], row[:], ALU.add)
                    if relu:
                        steps.then(ins)
                        ins = nc.vector.tensor_scalar(rows[:, t], rows[:, t], 0.0, None, ALU.max)
                    if onto is not None:
                        steps.then(ins)
                        ins = nc.vector.tensor_tensor(onto[:, t], onto[:, t], rows[:, t], ALU.add)
                    ins.then_inc(ready.sem, 1)
                steps.done()

            if turned is not None:
                @block.tensor
                def _(pe):
                    turn_rows(nc, m, pe, rows)

                @block.scalar
                def _(act):
                    save_turned(nc, m, act, turned)
        params.close(16), ready.close(T), close_turn(m, 1 if turned is not None else 0)


def gat_block(nc, m, g):
    normalise(nc, m, m.X, m.H, m.eps5, turned=m.HT)
    with ExitStack() as ctx:
        sb = scratch(nc, m, ctx)
        columns = sb("columns", [P, 8, NP], F32)
        with ExitStack() as inner:
            sb1 = scratch(nc, m, inner)
            values = sb1("values", [P, T, 1024], F32)
            scores = sb1("scores", [P, T, 16], F32)
            broad = sb1("broad", [P, 8, NP], F32)
            out = sb1("out", [P, T, 1024], F32)
            project(nc, m, m.HT, [(g["L1_gnn_W1"], None, values, None)])
            head_scores(nc, m, values, g["L1_gnn_att_src1"], g["L1_gnn_att_dst1"], 8, scores)
            spread(nc, m, scores, 8, broad)
            attend(nc, m, 1, 8, 128, [values], out, broad=broad, near=scores[:, :, 8:16], logs=(3,))
            finish_rows(nc, m, out, g["L1_gnn_b1"], turned=columns, relu=True)
        values = sb("values", [P, T, D], F32)
        scores = sb("scores", [P, T, 2], F32)
        broad = sb("broad", [P, 1, NP], F32)
        project(nc, m, columns, [(g["L1_gnn_W2"], None, values, None)])
        head_scores(nc, m, values, g["L1_gnn_att_src2"], g["L1_gnn_att_dst2"], 1, scores)
        spread(nc, m, scores, 1, broad)
        attend(nc, m, 1, 1, D, [values], m.H, broad=broad, near=scores[:, :, 1:2], logs=(3,))
        finish_rows(nc, m, m.H, g["L1_gnn_b2"], onto=m.X)


def quantise(nc, steps, out, src, factor):
    steps.then(nc.vector.tensor_scalar(out[0], src, factor, -8.0, ALU.mult, ALU.max))
    steps.then(nc.vector.tensor_scalar(out[0], out[0], 7.0, ROUND, ALU.min, ALU.add))
    ins = nc.vector.tensor_scalar(out[1], out[0], -ROUND, None, ALU.add)
    return ins


def quant_block(nc, m, g):
    F = 96
    normalise(nc, m, m.X, m.H, m.eps5)
    with ExitStack() as ctx:
        sb = scratch(nc, m, ctx)
        a1 = sb("a1", [P, D], F32)
        a2 = sb("a2", [P, F], F32)
        aw2 = sb("aw2", [P, D], F32)
        b2 = sb("b2", [P, D], F32)
        aw1c = sb("aw1c", [F, 1], F32)
        b1c = sb("b1c", [F, 1], F32)
        aw2c = sb("aw2c", [P, KD], F32)
        w1 = sb("w1", [F, D], F32)
        w2 = sb("w2", [P, KD, F], F32)
        mean = sb("mean", [P, 4], F32)
        w1q = sb("w1q", [F, D], F32)
        w2q = sb("w2q", [P, KD, F], F32)
        w1T = sb("w1T", [P, KD, F], BF16)
        w2T = sb("w2T", [F, D], BF16)
        xT = sb("xT", [P, KD, NP], BF16)
        hid = sb("hid", [F, NP], F32)
        hq = sb("hq", [F, NP], BF16)
        rest = sb("rest", [P, T, D], F32)
        params, ready, turned, saved, h_ready, h_done, s_ready, s_done = (
            m.c[k] for k in ("params", "rows_ready", "transposed", "columns_ready", "hidden_ready", "hidden_done", "second_ready", "second_done"))
        q_ready = m.c["sum_ready"]
        w_turned, w_saved = m.c["turned"], m.c["turned_saved"]
        column = lambda a: a.rearrange("(h o) -> h o", o=1)
        with nc.Block() as block:
            @block.sync
            def _(sp):
                loads = [(a1[:], g["L1_ffn_alpha_a1"].partition_broadcast(P)), (a2[:], g["L1_ffn_alpha_a2"].partition_broadcast(P)),
                         (aw2[:], g["L1_ffn_alpha_w2"].partition_broadcast(P)), (b2[:], g["L1_ffn_b2"].partition_broadcast(P)),
                         (aw1c[:], column(g["L1_ffn_alpha_w1"])), (b1c[:], column(g["L1_ffn_b1"])),
                         (w1[:], g["L1_ffn_w1"]), (w2[:], g["L1_ffn_w2"].rearrange("(k p) h -> p k h", p=P))]
                for to, of in loads:
                    sp.dma_start(to, of).then_inc(params.sem, 16)
                with nc.allow_non_contiguous_dma("768 numbers"):
                    sp.dma_start(aw2c[:], g["L1_ffn_alpha_w2"].rearrange("(k p) -> p k", p=P)).then_inc(params.sem, 16)

            @block.vector
            def _(dve):
                steps = Steps(dve, m.c["dve_step"])
                dve.wait_ge(params.sem, params.at(16 * 9))
                nc.vector.tensor_reduce(mean[:, 0:1], a1[:], AX_X, ALU.add)
                steps.then(nc.vector.tensor_reduce(mean[:, 1:2], a2[:], AX_X, ALU.add))
                nc.vector.tensor_scalar(mean[:, 0:1], mean[:, 0:1], 1.0 / D, None, ALU.mult)
                steps.then(nc.vector.tensor_scalar(mean[:, 1:2], mean[:, 1:2], 1.0 / F, None, ALU.mult))
                nc.vector.reciprocal(mean[:, 2:4], mean[:, 0:2])
                nc.vector.reciprocal(aw2c[:], aw2c[:])
                steps.then(nc.vector.reciprocal(w1q[:, 0:1], aw1c[:]))
                steps.then(nc.vector.tensor_scalar(w1[:], w1[:], w1q[:, 0:1], None, ALU.mult))
                steps.then(nc.vector.tensor_tensor(w2[:], w2[:], aw2c[:].unsqueeze(2).to_broadcast([P, KD, F]), ALU.mult))
                steps.then(quantise(nc, steps, (w1q[:], w1q[:]), w1[:], 1.0))
                steps.then(quantise(nc, steps, (w2q[:], w2q[:]), w2[:], 1.0))
                dve.sem_inc(q_ready.sem, 1)
                for t in range(T):
                    quantise(nc, steps, (rest[:, t], rest[:, t]), m.H[:, t], mean[:, 2:3]).then_inc(ready.sem, 1)
                steps.then(nc.vector.tensor_tensor(aw1c[:], aw1c[:], mean[0:F, 0:1], ALU.mult))
                steps.then(nc.vector.tensor_scalar(aw2[:], aw2[:], mean[:, 1:2], None, ALU.mult))
                dve.sem_inc(q_ready.sem, 1)
                dve.wait_ge(h_done.sem, h_done.at(1))
                steps.then(nc.vector.tensor_scalar(hid[:], hid[:], -10.0, 10.0, ALU.max, ALU.min))
                quantise(nc, steps, (hid[:], hq[:]), hid[:], mean[0:F, 3:4]).then_inc(h_done.sem, 1)
                for t in range(T):
                    dve.wait_ge(s_ready.sem, s_ready.at(t + 1))
                    two = lambda r: r.rearrange("p (c w) -> p c w", c=2)
                    b = 4 + 2 * (t % 2)
                    steps.then(nc.vector.tensor_tensor(two(rest[:, t]), m.psum[:, b:b + 2, 0:384], two(aw2[:]), ALU.mult))
                    dve.sem_inc(s_done.sem, 1)
                    steps.then(nc.vector.tensor_tensor(rest[:, t], rest[:, t], b2[:], ALU.add))
                    steps.then(nc.vector.tensor_tensor(m.X[:, t], m.X[:, t], rest[:, t], ALU.add))
                steps.done()

            @block.tensor
            def _(pe):
                pe.wait_ge(q_ready.sem, q_ready.at(1))
                for k in range(KD):
                    nc.tensor.transpose(m.psum[:, 4, k * 96 % 480:k * 96 % 480 + 96] if k < 5 else m.psum[:, 5, 0:96],
                                        w1q[:, k * P:(k + 1) * P], m.ident[0:F, 0:F])
                for k in range(KD):
                    ins = nc.tensor.transpose(m.psum[0:F, 6 + k // 4, (k % 4) * P:(k % 4 + 1) * P], w2q[:, k], m.ident[:])
                ins.then_inc(w_turned.sem, 1)
                turn_rows(nc, m, pe, rest)
                pe.wait_ge(w_saved.sem, w_saved.at(1))
                pe.wait_ge(saved.sem, saved.at(T))
                for c in range(2):
                    for k in range(KD):
                        ins = nc.tensor.matmul(m.psum[0:F, c, 0:HALF], w1T[:, k], xT[:, k, c * HALF:(c + 1) * HALF],
                                               start=(k == 0), stop=(k == KD - 1))
                ins.then_inc(h_ready.sem, 1)
                pe.wait_ge(h_done.sem, h_done.at(2))
                for t in range(T):
                    if t >= 2:
                        pe.wait_ge(s_done.sem, s_done.at(t - 1))
                    for c in range(2):
                        ins = nc.tensor.matmul(m.psum[:, 4 + 2 * (t % 2) + c, 0:384], hq[:, t * P:(t + 1) * P],
                                               w2T[:, c * 384:(c + 1) * 384], start=True, stop=True)
                    ins.then_inc(s_ready.sem, 1)

            @block.scalar
            def _(act):
                act.wait_ge(w_turned.sem, w_turned.at(1))
                nc.scalar.activation(w1T[:, 0:5], m.psum[:, 4, 0:480].rearrange("p (k f) -> p k f", k=5), ACT.Copy)
                nc.scalar.activation(w1T[:, 5], m.psum[:, 5, 0:96], ACT.Copy)
                nc.scalar.activation(w2T[:, 0:512], m.psum[0:F, 6, :], ACT.Copy)
                nc.scalar.activation(w2T[:, 512:D], m.psum[0:F, 7, 0:256], ACT.Copy).then_inc(w_saved.sem, 1)
                save_turned(nc, m, act, xT)
                act.wait_ge(h_ready.sem, h_ready.at(1))
                act.wait_ge(q_ready.sem, q_ready.at(2))
                nc.scalar.activation(hid[:].rearrange("p (c n) -> p c n", c=2), m.psum[0:F, 0:2, 0:HALF], ACT.Gelu,
                                     bias=b1c[:], scale=aw1c[:]).then_inc(h_done.sem, 1)
        params.close(16 * 9), ready.close(T), q_ready.close(2), close_turn(m, 1), w_turned.close(1), w_saved.close(1)
        h_ready.close(1), h_done.close(2), s_ready.close(T), s_done.close(T)


def relation_scores(nc, m, values, q, k, heads, scores, R):
    params, turned, saved, o_ready, o_saved = (m.c[x] for x in ("params", "transposed", "columns_ready", "mixed", "mixed_saved"))
    for r in range(R):
        with ExitStack() as ctx:
            sb = scratch(nc, m, ctx)
            both = sb("both_qk", [P, KD, 2, heads], F32)
            with nc.Block() as block:
                @block.sync
                def _(sp):
                    with nc.allow_non_contiguous_dma("a few thousand numbers"):
                        for n, w in enumerate((k, q)):
                            sp.dma_start(both[:, :, n], w.rearrange("(k p) h -> p k h", p=P)).then_inc(params.sem, 16)

                @block.tensor
                def _(pe):
                    turn_rows(nc, m, pe, values[r], ready_made=True)
                    pe.wait_ge(params.sem, params.at(32))
                    pe.wait_ge(saved.sem, saved.at(T))
                    for t in range(T):
                        for c in range(KD):
                            ins = nc.tensor.matmul(m.psum[:, 4, t * 2 * heads:(t + 1) * 2 * heads], m.HT[:, c, t * P:(t + 1) * P],
                                                   both[:, c].rearrange("p n h -> p (n h)"), start=(c == 0), stop=(c == KD - 1))
                    ins.then_inc(o_ready.sem, 1)

                @block.scalar
                def _(act):
                    save_turned(nc, m, act, m.HT)

                @block.vector
                def _(dve):
                    dve.wait_ge(o_ready.sem, o_ready.at(1))
                    src = m.psum[:, 4, 0:T * 2 * heads].rearrange("p (t n h) -> p t n h", t=T, n=2)
                    for n in range(2):
                        nc.vector.tensor_copy(scores[:, :, n * R * heads + r * heads:n * R * heads + (r + 1) * heads], src[:, :, n])
            params.close(32), close_turn(m, 1), o_ready.close(1)


def rgat_block(nc, m, g):
    R = 3
    for layer, heads in ((1, 4), (2, 1)):
        if layer == 1:
            normalise(nc, m, m.X, m.H, m.eps5, turned=m.HT)
        W, q, k, b = (g[f"L2_gnn_{n}{layer}"] for n in ("W", "q", "k", "b"))
        with ExitStack() as ctx:
            sb = scratch(nc, m, ctx)
            values = [sb(f"values{r}", [P, T, D], F32) for r in range(R)]
            scores = sb("scores", [P, T, 2 * R * heads], F32)
            broad = sb("broad", [P, R * heads, NP], F32)
            project(nc, m, m.HT, [(W[r], None, values[r], None) for r in range(R)])
            relation_scores(nc, m, values, q, k, heads, scores, R)
            spread(nc, m, scores, R * heads, broad)
            attend(nc, m, R, heads, D // heads, values, m.H, broad=broad, near=scores[:, :, R * heads:], logs=(0, 1, 2))
        if layer == 1:
            elu_rows(nc, m, m.H, bias=b)
            with nc.Block() as block:
                @block.tensor
                def _(pe):
                    turn_rows(nc, m, pe, m.H, ready_made=True)

                @block.scalar
                def _(act):
                    save_turned(nc, m, act, m.HT)
            close_turn(m, 1)
        else:
            finish_rows(nc, m, m.H, b, onto=m.X)


def top_two(nc, m, logits, E, eps, gates_dram, mix=None):
    rows = E + (mix is not None)
    e_ready, e_done, ready, t_ready, t_saved, stored = (
        m.c[k] for k in ("elu_ready", "elu_done", "rows_ready", "turned", "turned_saved", "stored"))
    with ExitStack() as ctx:
        sb = scratch(nc, m, ctx)
        shape = [P, T, E]
        work, first, second, prob = (sb(k, shape, F32) for k in ("work", "first", "second", "prob"))
        gates = sb("gates", [P, T, rows], F32)
        gatesT = sb("gatesT", [rows, NP], F32)
        top = sb("top", [P, T, 2], F32)
        share = sb("share", [P, T, 2], F32)
        with nc.Block() as block:
            @block.vector
            def _(dve):
                steps = Steps(dve, m.c["dve_step"])
                steps.then(nc.vector.tensor_reduce(top[:, :, 0], logits[:, :, 0:E], AX_X, ALU.max))
                steps.then(nc.vector.tensor_tensor(prob[:], logits[:, :, 0:E], top[:, :, 0:1].to_broadcast(shape), ALU.subtract))
                dve.sem_inc(e_ready.sem, 1)
                dve.wait_ge(e_done.sem, e_done.at(1))
                steps.then(nc.vector.tensor_reduce(share[:, :, 0], prob[:], AX_X, ALU.add))
                steps.then(nc.vector.reciprocal(share[:, :, 1], share[:, :, 0]))
                steps.then(nc.vector.tensor_tensor(prob[:], prob[:], share[:, :, 1:2].to_broadcast(shape), ALU.mult))
                first_largest(nc, steps, prob[:], work[:], top, first[:], m.rank)
                steps.then(nc.vector.scalar_tensor_tensor(second[:], first[:], -2.0, prob[:], ALU.mult, ALU.add))
                first_largest(nc, steps, second[:], work[:], top, second[:], m.rank)
                steps.then(nc.vector.tensor_tensor(first[:], first[:], second[:], ALU.add))
                steps.then(nc.vector.tensor_tensor(prob[:], prob[:], first[:], ALU.mult))
                steps.then(nc.vector.tensor_reduce(share[:, :, 0], prob[:], AX_X, ALU.add))
                steps.then(nc.vector.tensor_scalar(share[:, :, 0], share[:, :, 0], eps, None, ALU.add))
                steps.then(nc.vector.reciprocal(share[:, :, 1], share[:, :, 0]))
                if mix is not None:
                    steps.then(nc.vector.tensor_scalar(share[:, :, 0], gates[:, :, E], -1.0, 1.0, ALU.mult, ALU.add))
                    steps.then(nc.vector.tensor_tensor(share[:, :, 1], share[:, :, 1], share[:, :, 0], ALU.mult))
                steps.then(nc.vector.tensor_tensor(gates[:, :, 0:E], prob[:], share[:, :, 1:2].to_broadcast(shape), ALU.mult))
                dve.sem_inc(ready.sem, 1)
                steps.done()

            @block.scalar
            def _(act):
                act.wait_ge(e_ready.sem, e_ready.at(1))
                ins = nc.scalar.activation(prob[:], prob[:], ACT.Exp, bias=m.zero[:])
                if mix is not None:
                    ins = nc.scalar.activation(gates[:, :, E], logits[:, :, E], ACT.Sigmoid, bias=mix[:])
                ins.then_inc(e_done.sem, 1)
                act.wait_ge(t_ready.sem, t_ready.at(1))
                nc.scalar.activation(gatesT[:, 0:512], m.psum[0:rows, 0, :], ACT.Copy)
                nc.scalar.activation(gatesT[:, 512:NP], m.psum[0:rows, 1, 0:P], ACT.Copy).then_inc(t_saved.sem, 1)

            @block.tensor
            def _(pe):
                pe.wait_ge(ready.sem, ready.at(1))
                for t in range(T):
                    ins = nc.tensor.transpose(m.psum[0:rows, t // 4, (t % 4) * P:(t % 4 + 1) * P], gates[:, t], m.ident[:])
                ins.then_inc(t_ready.sem, 1)

            @block.sync
            def _(sp):
                sp.wait_ge(t_saved.sem, t_saved.at(1))
                sp.dma_start(gates_dram, gatesT[:]).then_inc(stored.sem, 16)
                sp.wait_ge(stored.sem, stored.at(16))
        e_ready.close(1), e_done.close(1), ready.close(1), t_ready.close(1), t_saved.close(1), stored.close(16)


def deep_experts_block(nc, m, g):
    E, HID, BOT = 32, 64, 256
    PAIRS = E // 2
    normalise(nc, m, m.X, m.H, m.eps5, turned=m.HT)
    gates_dram = m.gates32
    with ExitStack() as ctx:
        logits = scratch(nc, m, ctx)("logits", [P, T, E], F32)
        project(nc, m, m.HT, [(g["L2_ffn_gate_w"], None, logits, None)])
        top_two(nc, m, logits, E, 1e-20, gates_dram)
    with ExitStack() as ctx:
        sb = scratch(nc, m, ctx)
        gated = sb("gated", [P, PAIRS, NP], F32)
        merged = sb("merged", [P, PAIRS, D], F32)
        bias = sb("bias", [E, D], F32)
        bl = sb("bl", [E, D], F32)
        gatesT = sb("gatesT", [E, NP], F32)
        params = m.c["params"]
        with ExitStack() as inner:
            sb1 = scratch(nc, m, inner)
            w1 = sb1("w1", [P, 2, KD, P], F32)
            w2 = sb1("w2", [P, 2, P], F32)
            w3 = sb1("w3", [P, 2, 2, 2, HID + 1], F32)
            wl = sb1("wl", [P, 2, 2, 2, D], F32)
            gate = sb1("gate", [P, 2, NP], F32)
            b1 = sb1("b1", [P, PAIRS], F32)
            b2 = sb1("b2", [P, PAIRS], F32)
            first = sb1("first", [P, 2, NP], F32)
            second = sb1("second", [P, 2, NP], F32)
            row = sb1("row", [HID + 1, 2, D], F32)
            load = (m.c["streamed_a"], m.c["streamed_b"])
            row_out = m.c["bias_out"]
            used, f_ready, f_done, s_ready, s_done, g_done, m_ready, m_done, cleared, c_used = (
                m.c[k] for k in ("stream_used", "hidden_ready", "hidden_done", "second_ready", "second_done", "hidden_used", "mixed",
                                 "mixed_saved", "cleared", "grid_used"))
            LOADS = 6
            with nc.Block() as block:
                @block.sync
                def _(sp):
                    sp.dma_start(b1[:], g["L2_ffn_b1"]).then_inc(params.sem, 16)
                    sp.dma_start(b2[:], g["L2_ffn_b2"]).then_inc(params.sem, 16)
                    sp.dma_start(bl[:], g["L2_ffn_bl"]).then_inc(params.sem, 16)
                    sp.dma_start(gatesT[:], gates_dram).then_inc(params.sem, 16)
                    sp.wait_ge(cleared.sem, cleared.at(1))
                    waited = m.c["waited"]
                    with sp.Fori(0, PAIRS // 2) as i:
                        for s in range(2):
                            p = 2 * i + s
                            sp.wait_ge(used.sem, used.at(p - 1))
                            sp.sem_inc(waited.sem, 1)
                            sp.wait_ge(g_done.sem, g_done.at(p - 1))
                            sp.sem_inc(waited.sem, 1)
                            one_ = bass.ds(p, 1)
                            sp.dma_start(w1[:, s].rearrange("p k f -> p (k f)"), g["L2_ffn_W1"][one_].rearrange("o p f -> (o p) f")).then_inc(load[s].sem, 16)
                            for h in range(2):
                                sp.dma_start(w2[h * HID:(h + 1) * HID, s, h * HID:(h + 1) * HID],
                                             g["L2_ffn_W2"][one_, h * HID:(h + 1) * HID].rearrange("o p f -> (o p) f")).then_inc(load[s].sem, 16)
                            sp.dma_start(w3[:, s].rearrange("p e k f -> p (e k f)"), g["L2_ffn_W3"][one_].rearrange("o p f -> (o p) f")).then_inc(load[s].sem, 16)
                            sp.dma_start(wl[:, s].rearrange("p e k f -> p (e k f)"), g["L2_ffn_Wl"][one_].rearrange("o p f -> (o p) f")).then_inc(load[s].sem, 16)
                            for h in range(2):
                                sp.dma_start(gate[h * HID:(h + 1) * HID, s], gates_dram[bass.ds(2 * p + h, 1)].to_broadcast([HID, NP])).then_inc(load[s].sem, 16)

                @block.tensor
                def _(pe):
                    with pe.Fori(0, PAIRS // 2) as i:
                        for s in range(2):
                            p = 2 * i + s
                            pe.wait_ge(load[s].sem, load[s].at(16 * (LOADS + 1) * (i + 1)))
                            for c in range(2):
                                for k in range(KD):
                                    ins = nc.tensor.matmul(m.psum[:, c, 0:HALF], w1[:, s, k], m.HT[:, k, c * HALF:(c + 1) * HALF],
                                                           start=(k == 0), stop=(k == KD - 1))
                            ins.then_inc(f_ready.sem, 1)
                            for e in range(2):
                                pe.wait_ge(m_done.sem, m_done.at(2 * p + e - 1))
                                for c in range(2):
                                    for k in range(2):
                                        ins = nc.tensor.matmul(m.psum[0:HID + 1, 4 + 2 * e + c, 0:384], w3[:, s, e, k],
                                                               wl[:, s, e, k, c * 384:(c + 1) * 384], start=(k == 0), stop=(k == 1))
                                ins.then_inc(m_ready.sem, 1)
                            pe.wait_ge(f_done.sem, f_done.at(p + 1))
                            pe.wait_ge(s_done.sem, s_done.at(p))
                            for c in range(2):
                                ins = nc.tensor.matmul(m.psum[:, 2 + c, 0:HALF], w2[:, s], first[:, s, c * HALF:(c + 1) * HALF], start=True, stop=True)
                            ins.then_inc(s_ready.sem, 1)
                            pe.wait_ge(s_ready.sem, s_ready.at(p + 1))
                            pe.sem_inc(used.sem, 1)

                @block.scalar
                def _(act):
                    two = lambda v: v.rearrange("p (c n) -> p c n", c=2)
                    act.wait_ge(params.sem, params.at(64))
                    with act.Fori(0, PAIRS // 2) as i:
                        for s in range(2):
                            p = 2 * i + s
                            act.wait_ge(f_ready.sem, f_ready.at(p + 1))
                            nc.scalar.activation(two(first[:, s]), m.psum[:, 0:2, 0:HALF], ACT.Gelu, bias=b1[:, bass.ds(p, 1)]).then_inc(f_done.sem, 1)
                            for e in range(2):
                                act.wait_ge(m_ready.sem, m_ready.at(2 * p + e + 1))
                                if e == 0:
                                    act.wait_ge(row_out.sem, row_out.at(32 * p))
                                nc.scalar.activation(row[HID:HID + 1, e].rearrange("p (c n) -> p c n", c=2), m.psum[HID:HID + 1, 4 + 2 * e:6 + 2 * e, 0:384], ACT.Copy)
                                nc.scalar.activation(merged[e * HID:(e + 1) * HID, bass.ds(p, 1)].rearrange("p o (c n) -> p (o c) n", c=2),
                                                     m.psum[0:HID, 4 + 2 * e:6 + 2 * e, 0:384], ACT.Copy).then_inc(m_done.sem, 1)
                            act.wait_ge(s_ready.sem, s_ready.at(p + 1))
                            act.wait_ge(g_done.sem, g_done.at(p - 1))
                            nc.scalar.activation(two(second[:, s]), m.psum[:, 2:4, 0:HALF], ACT.Gelu, bias=b2[:, bass.ds(p, 1)]).then_inc(s_done.sem, 1)

                @block.vector
                def _(dve):
                    nc.vector.memset(w2[:], 0.0).then_inc(cleared.sem, 1)
                    with dve.Fori(0, PAIRS // 2) as i:
                        for s in range(2):
                            p = 2 * i + s
                            dve.wait_ge(load[s].sem, load[s].at(16 * (LOADS + 1) * (i + 1)))
                            dve.wait_ge(s_done.sem, s_done.at(p + 1))
                            nc.vector.tensor_tensor(gated[:, bass.ds(p, 1)].rearrange("p o n -> p (o n)"), second[:, s], gate[:, s], ALU.mult).then_inc(g_done.sem, 1)

                @block.gpsimd
                def _(pool):
                    with pool.Fori(0, PAIRS // 2) as i:
                        for s in range(2):
                            p = 2 * i + s
                            pool.wait_ge(m_done.sem, m_done.at(2 * p + 2))
                            pool.sem_inc(m.c["waited"].sem, 1)
                            for e in range(2):
                                pool.dma_start(m.bias_rows[bass.ds(2 * p + e, 1)], row[HID:HID + 1, e]).then_inc(row_out.sem, 16)
                    pool.wait_ge(row_out.sem, row_out.at(32 * PAIRS))
            params.close(64), cleared.close(1), m.c["waited"].close(PAIRS)
            for s in range(2):
                load[s].close(16 * (LOADS + 1) * (PAIRS // 2))
            row_out.close(32 * PAIRS)
            used.close(PAIRS), f_ready.close(PAIRS), f_done.close(PAIRS), s_ready.close(PAIRS), s_done.close(PAIRS), g_done.close(PAIRS)
            m_ready.close(E), m_done.close(E)
        ready, o_ready, o_saved = (m.c[k] for k in ("rows_ready", "mixed", "mixed_saved"))
        with nc.Block() as block:
            @block.sync
            def _(sp):
                sp.dma_start(bias[:], m.bias_rows).then_inc(params.sem, 16)

            @block.vector
            def _(dve):
                steps = Steps(dve, m.c["dve_step"])
                dve.wait_ge(params.sem, params.at(16))
                nc.vector.tensor_tensor(bias[:], bias[:], bl[:], ALU.add).then_inc(ready.sem, 1)
                for t in range(T):
                    dve.wait_ge(o_ready.sem, o_ready.at(t + 1))
                    two = m.X[:, t].rearrange("p (c w) -> p c w", c=2)
                    nc.vector.tensor_tensor(two, two, m.psum[:, 2 * (t % 2):2 * (t % 2) + 2, 0:384], ALU.add).then_inc(o_saved.sem, 1)
                steps.done()

            @block.tensor
            def _(pe):
                for t in range(T):
                    if t >= 2:
                        pe.wait_ge(o_saved.sem, o_saved.at(t - 1))
                    cols = slice(t * P, (t + 1) * P)
                    for c in range(2):
                        out, of = m.psum[:, 2 * (t % 2) + c, 0:384], slice(c * 384, (c + 1) * 384)
                        for p in range(PAIRS):
                            nc.tensor.matmul(out, gated[:, p, cols], merged[:, p, of], start=(p == 0), stop=False)
                        if t == 0 and c == 0:
                            pe.wait_ge(ready.sem, ready.at(1))
                        ins = nc.tensor.matmul(out, gatesT[:, cols], bias[:, of], start=False, stop=True)
                    ins.then_inc(o_ready.sem, 1)
        params.close(16), ready.close(1), o_ready.close(T), o_saved.close(T)


def gcn_block(nc, m, g):
    normalise(nc, m, m.X, m.H, m.eps5, turned=m.HT)
    with ExitStack() as ctx:
        sb = scratch(nc, m, ctx)
        count = sb("count", [P, T, NP], F32)
        countT = sb("countT", [P, T, NP], F32)
        root = sb("root", [P, T], F32)
        values = sb("values", [P, T, D], F32)
        row = sb("row", [P, 2, D], F32)
        params, ready, turned, saved, v_ready, d_ready = (
            m.c[k] for k in ("params", "rows_ready", "transposed", "columns_ready", "variance_ready", "deviation_ready"))
        with nc.Block() as block:
            @block.sync
            def _(sp):
                sp.dma_start(count[:], m.counts[3].rearrange("(t p) s -> p t s", p=P)).then_inc(params.sem, 16)
                for k in range(2):
                    sp.dma_start(row[:, k], g[f"L3_gnn_b{k + 1}"].partition_broadcast(P)).then_inc(params.sem, 16)

            @block.vector
            def _(dve):
                steps = Steps(dve, m.c["dve_step"])
                dve.wait_ge(params.sem, params.at(48))
                for t in range(T):
                    own = count[:, t, t * P:(t + 1) * P]
                    ins = nc.vector.tensor_tensor(own, own, m.ident[:], ALU.add)
                    ins.then_inc(ready.sem, 1)
                dve.wait_ge(ready.sem, ready.at(T))
                steps.then(nc.vector.tensor_reduce(root[:], count[:], AX_X, ALU.add))
                dve.sem_inc(v_ready.sem, 1)
                dve.wait_ge(d_ready.sem, d_ready.at(1))
                steps.then(nc.vector.reciprocal(root[:], root[:]))
                steps.done()

            @block.tensor
            def _(pe):
                turn_rows(nc, m, pe, count)

            @block.scalar
            def _(act):
                save_turned(nc, m, act, countT)
                act.wait_ge(v_ready.sem, v_ready.at(1))
                nc.scalar.activation(root[:], root[:], ACT.Sqrt, bias=m.zero[:]).then_inc(d_ready.sem, 1)
        params.close(48), ready.close(T), close_turn(m, 1), v_ready.close(1), d_ready.close(1)
        o_ready, o_saved = m.c["mixed"], m.c["mixed_saved"]
        for layer in (1, 2):
            project(nc, m, m.HT, [(g[f"L3_gnn_W{layer}"], None, values, root)])
            with nc.Block() as block:
                @block.tensor
                def _(pe):
                    for t in range(T):
                        if t >= 2:
                            pe.wait_ge(o_saved.sem, o_saved.at(t - 1))
                        for c in range(2):
                            for k in range(T):
                                ins = nc.tensor.matmul(m.psum[:, 4 + 2 * (t % 2) + c, 0:384], countT[:, k, t * P:(t + 1) * P],
                                                       values[:, k, c * 384:(c + 1) * 384], start=(k == 0), stop=(k == T - 1))
                        ins.then_inc(o_ready.sem, 1)
                    if layer == 1:
                        turn_rows(nc, m, pe, m.H)

                @block.vector
                def _(dve):
                    steps = Steps(dve, m.c["dve_step"])
                    for t in range(T):
                        dve.wait_ge(o_ready.sem, o_ready.at(t + 1))
                        two = lambda r: r.rearrange("p (c w) -> p c w", c=2)
                        b = 4 + 2 * (t % 2)
                        steps.then(nc.vector.scalar_tensor_tensor(two(m.H[:, t]), m.psum[:, b:b + 2, 0:384], root[:, t:t + 1],
                                                                  two(row[:, layer - 1]), ALU.mult, ALU.add))
                        dve.sem_inc(o_saved.sem, 1)
                        if layer == 1:
                            nc.vector.tensor_scalar(m.H[:, t], m.H[:, t], 0.0, None, ALU.max).then_inc(ready.sem, 1)
                        else:
                            nc.vector.tensor_tensor(m.X[:, t], m.X[:, t], m.H[:, t], ALU.add)
                    steps.done()

                if layer == 1:
                    @block.scalar
                    def _(act):
                        save_turned(nc, m, act, m.HT)
            o_ready.close(T), o_saved.close(T)
            if layer == 1:
                ready.close(T), close_turn(m, 1)


ROUND = 12582912.0
PAIRS_OF = 2 * NODES


def tiles_bound(experts):
    return (PAIRS_OF - experts) // P + experts


def route_two(nc, m, logits, E, mix, share1, share2, alpha, send, fetch, plan):
    NT = tiles_bound(E)
    shape = [P, T, E]
    e_ready, e_done, ready, o_ready = (m.c[k] for k in ("elu_ready", "elu_done", "rows_ready", "mixed"))
    with ExitStack() as ctx:
        sb = scratch(nc, m, ctx)
        work, first, second, prob, chosen, place = (sb(k, shape, F32) for k in ("work", "first", "second", "prob", "chosen", "place"))
        top = sb("top", [P, T, 2], F32)
        total = sb("total", [P, T], F32)
        real = sb("real", [P, T], F32)
        trash = sb("trash", [P, T], F32)
        rows = sb("rows", [P, 2, T], F32)
        tiles, ends, base = (sb(k, [P, E], F32) for k in ("tiles", "ends", "base"))
        passed = sb("passed", [P, NT + 1, E], F32)
        expert = sb("expert", [P, NT + 2], F32)
        spread_ = lambda a: a.to_broadcast(shape)
        with nc.Block() as block:
            @block.vector
            def _(dve):
                steps = Steps(dve, m.c["dve_step"])
                do = steps.then
                do(nc.vector.tensor_reduce(top[:, :, 0], logits[:, :, 0:E], AX_X, ALU.max))
                do(nc.vector.tensor_tensor(prob[:], logits[:, :, 0:E], spread_(top[:, :, 0:1]), ALU.subtract))
                dve.sem_inc(e_ready.sem, 1)
                nc.vector.memset(real[:, 0:T - 1], 1.0)
                do(nc.vector.tensor_scalar(real[:, T - 1:T], m.part[:], float(LAST), None, ALU.is_lt))
                do(nc.vector.tensor_scalar(trash[:], real[:], -float(NT * P), float(NT * P), ALU.mult, ALU.add))
                dve.wait_ge(e_done.sem, e_done.at(1))
                do(nc.vector.tensor_reduce(total[:], prob[:], AX_X, ALU.add))
                do(nc.vector.reciprocal(total[:], total[:]))
                do(nc.vector.tensor_tensor(prob[:], prob[:], spread_(total[:].unsqueeze(2)), ALU.mult))
                first_largest(nc, steps, prob[:], work[:], top, first[:], m.rank)
                do(nc.vector.scalar_tensor_tensor(chosen[:], first[:], -2.0, prob[:], ALU.mult, ALU.add))
                first_largest(nc, steps, chosen[:], work[:], top, second[:], m.rank)
                do(nc.vector.tensor_tensor(chosen[:], first[:], second[:], ALU.add))
                do(nc.vector.tensor_tensor(chosen[:], chosen[:], spread_(real[:].unsqueeze(2)), ALU.mult))
                dve.sem_inc(ready.sem, 1)
                for one_hot, share in ((first, share1), (second, share2)):
                    do(nc.vector.tensor_tensor(work[:], prob[:], one_hot[:], ALU.mult))
                    do(nc.vector.tensor_reduce(share[:], work[:], AX_X, ALU.add))
                do(nc.vector.tensor_tensor(total[:], share1[:], share2[:], ALU.add))
                do(nc.vector.reciprocal(total[:], total[:]))
                do(nc.vector.tensor_scalar(top[:, :, 0], alpha[:], -1.0, 1.0, ALU.mult, ALU.add))
                do(nc.vector.tensor_tensor(total[:], total[:], top[:, :, 0], ALU.mult))
                nc.vector.tensor_tensor(share1[:], share1[:], total[:], ALU.mult)
                do(nc.vector.tensor_tensor(share2[:], share2[:], total[:], ALU.mult))
                dve.wait_ge(o_ready.sem, o_ready.at(1))
                do(nc.vector.tensor_scalar(tiles[:], m.psum[:, 1, 0:E], float(P - 1), 1.0 / P, ALU.add, ALU.mult))
                do(nc.vector.tensor_scalar(tiles[:], tiles[:], -(P - 1) / (2.0 * P), ROUND, ALU.add, ALU.add))
                do(nc.vector.tensor_scalar(tiles[:], tiles[:], -ROUND, None, ALU.add))
                do(nc.vector.memset(base[:], 0.0))
                do(nc.vector.tensor_tensor_scan(ends[:], tiles[:], base[:], 0.0, ALU.add, ALU.add))
                do(nc.vector.tensor_tensor(base[:], ends[:], tiles[:], ALU.subtract))
                do(nc.vector.tensor_scalar(base[:], base[:], float(P), -1.0, ALU.mult, ALU.add))
                nth = m.psum[:, 0, 0:T * E].rearrange("p (t e) -> p t e", t=T)
                do(nc.vector.tensor_tensor(place[:], nth, base[:].unsqueeze(1).to_broadcast(shape), ALU.add))
                for k, one_hot in enumerate((first, second)):
                    do(nc.vector.tensor_tensor(work[:], place[:], one_hot[:], ALU.mult))
                    do(nc.vector.tensor_reduce(rows[:, k], work[:], AX_X, ALU.add))
                    do(nc.vector.tensor_tensor(rows[:, k], rows[:, k], real[:], ALU.mult))
                    nc.vector.tensor_copy(fetch[:, k], rows[:, k])
                    do(nc.vector.tensor_tensor(send[:, k], rows[:, k], trash[:], ALU.add))
                whole = [P, NT + 1, E]
                do(nc.vector.tensor_tensor(passed[:], m.rank[:, 0:NT + 1].unsqueeze(2).to_broadcast(whole),
                                           ends[:].unsqueeze(1).to_broadcast(whole), ALU.is_ge))
                nc.vector.memset(expert[:, 0:1], -1.0)
                do(nc.vector.tensor_reduce(expert[:, 1:NT + 2], passed[:], AX_X, ALU.add))
                do(nc.vector.tensor_scalar(expert[:], expert[:], float(E - 1), None, ALU.min))
                nc.vector.tensor_copy(plan[:, :, 0], expert[0:1, 1:NT + 2])
                do(nc.vector.tensor_tensor(plan[:, :, 1], expert[0:1, 1:NT + 2], expert[0:1, 0:NT + 1], ALU.not_equal))
                steps.done()

            @block.scalar
            def _(act):
                act.wait_ge(e_ready.sem, e_ready.at(1))
                nc.scalar.activation(prob[:], prob[:], ACT.Exp, bias=m.zero[:])
                nc.scalar.activation(alpha[:], logits[:, :, E], ACT.Sigmoid, bias=mix[:]).then_inc(e_done.sem, 1)

            @block.tensor
            def _(pe):
                pe.wait_ge(ready.sem, ready.at(1))
                for t in range(T):
                    for k in range(t + 1):
                        nc.tensor.matmul(m.psum[:, 0, t * E:(t + 1) * E], m.after[:] if k == t else m.ones[:], chosen[:, k],
                                         start=(k == 0), stop=(k == t))
                for t in range(T):
                    ins = nc.tensor.matmul(m.psum[:, 1, 0:E], m.ones[:], chosen[:, t], start=(t == 0), stop=(t == T - 1))
                ins.then_inc(o_ready.sem, 1)
        e_ready.close(1), e_done.close(1), ready.close(1), o_ready.close(1)


def gated_experts_block(nc, m, g):
    E, HS = 8, 96
    NT = tiles_bound(E)
    normalise(nc, m, m.X, m.H, m.eps5, turned=m.HT)
    params = m.c["params"]
    with ExitStack() as ctx:
        sb = scratch(nc, m, ctx)
        share1, share2, alpha = (sb(k, [P, T], F32) for k in ("share1", "share2", "alpha"))
        send, fetch = (sb(k, [P, 2, T], U32) for k in ("send", "fetch"))
        plan = sb("plan", [1, NT + 1, 2], I32)
        with ExitStack() as inner:
            sb1 = scratch(nc, m, inner)
            logits = sb1("logits", [P, T, E + 1], F32)
            sg_b = sb1("sg_b", [P, 1], F32)
            with nc.Block() as block:
                @block.sync
                def _(sp):
                    sp.dma_start(sg_b[:], g["L3_ffn_sg_b"].partition_broadcast(P)).then_inc(params.sem, 16)
                    sp.wait_ge(params.sem, params.at(16))
            params.close(16)
            project(nc, m, m.HT, [(g["L3_ffn_router_w"], None, logits, None)])
            route_two(nc, m, logits, E, sg_b, share1, share2, alpha, send, fetch, plan)
        send_and_share(nc, m, g, send, alpha, HS)
        expert_tiles(nc, m, g, plan, NT)
        with ExitStack() as inner:
            got = scratch(nc, m, inner)("got", [P, 2 * T, D], F32)
            fetched = m.c["fetched"]
            with nc.Block() as block:
                @block.gpsimd
                def _(pool):
                    for t in range(T):
                        for k in range(2):
                            nc.gpsimd.indirect_dma_start(
                                out=got[:, 2 * t + k], out_offset=None, in_=m.made,
                                in_offset=bass.IndirectOffsetOnAxis(ap=fetch[:, k, t:t + 1], axis=0)).then_inc(fetched.sem, 16)
                    pool.wait_ge(fetched.sem, fetched.at(16 * 2 * T))
                    pool.sem_inc(m.c["rows_ready"].sem, 1)

                @block.vector
                def _(dve):
                    steps = Steps(dve, m.c["dve_step"])
                    dve.wait_ge(m.c["rows_ready"].sem, m.c["rows_ready"].at(1))
                    for k, share in enumerate((share1, share2)):
                        for t in range(T):
                            ins = nc.vector.scalar_tensor_tensor(m.X[:, t], got[:, 2 * t + k], share[:, t:t + 1], m.X[:, t], ALU.mult, ALU.add)
                        steps.then(ins)
                    steps.done()
            fetched.close(16 * 2 * T), m.c["rows_ready"].close(1)


def send_and_share(nc, m, g, send, alpha, HS):
    params, g_ready, s_ready, p_ready, d_ready, d_done = (
        m.c[k] for k in ("params", "hidden_ready", "hidden_done", "hidden_used", "second_ready", "second_done"))
    sent, waited = m.c["sent"], m.c["waited"]
    with ExitStack() as ctx:
        sb = scratch(nc, m, ctx)
        weights = sb("shared_gate_up", [P, 2, KD, HS], F32)
        down = sb("shared_down", [HS, D], F32)
        silu = sb("silu", [HS, NP], F32)
        hidden = sb("hidden", [HS, NP], F32)
        two = lambda v: v.rearrange("p (c n) -> p c n", c=2)
        with nc.Block() as block:
            @block.gpsimd
            def _(pool):
                for n, (k, t) in enumerate((k, t) for k in range(2) for t in range(T)):
                    if n:
                        pool.wait_ge(sent.sem, sent.at(16 * n))
                    nc.gpsimd.indirect_dma_start(
                        out=m.tokens, out_offset=bass.IndirectOffsetOnAxis(ap=send[:, k, t:t + 1], axis=0),
                        in_=m.H[:, t], in_offset=None).then_inc(sent.sem, 16)
                pool.wait_ge(sent.sem, sent.at(16 * 2 * T))

            @block.sync
            def _(sp):
                sp.dma_start(weights[:, 0], g["L3_ffn_ws_gate"].rearrange("(k p) f -> p k f", p=P)).then_inc(params.sem, 16)
                sp.dma_start(weights[:, 1], g["L3_ffn_ws_up"].rearrange("(k p) f -> p k f", p=P)).then_inc(params.sem, 16)
                sp.dma_start(down[:], g["L3_ffn_ws_down"]).then_inc(params.sem, 16)

            @block.tensor
            def _(pe):
                pe.wait_ge(params.sem, params.at(48))
                for a in range(2):
                    for c in range(2):
                        for k in range(KD):
                            ins = nc.tensor.matmul(m.psum[0:HS, 2 * a + c, 0:HALF], weights[:, a, k], m.HT[:, k, c * HALF:(c + 1) * HALF],
                                                   start=(k == 0), stop=(k == KD - 1))
                    ins.then_inc(g_ready.sem, 1)
                pe.wait_ge(p_ready.sem, p_ready.at(1))
                for t in range(T):
                    if t >= 2:
                        pe.wait_ge(d_done.sem, d_done.at(t - 1))
                    for c in range(2):
                        ins = nc.tensor.matmul(m.psum[:, 4 + 2 * (t % 2) + c, 0:384], hidden[:, t * P:(t + 1) * P],
                                               down[:, c * 384:(c + 1) * 384], start=True, stop=True)
                    ins.then_inc(d_ready.sem, 1)

            @block.scalar
            def _(act):
                act.wait_ge(g_ready.sem, g_ready.at(1))
                nc.scalar.activation(two(silu[:]), m.psum[0:HS, 0:2, 0:HALF], ACT.Silu, bias=m.zero[0:HS]).then_inc(s_ready.sem, 1)

            @block.vector
            def _(dve):
                dve.wait_ge(s_ready.sem, s_ready.at(1))
                dve.wait_ge(g_ready.sem, g_ready.at(2))
                nc.vector.tensor_tensor(two(hidden[:]), two(silu[:]), m.psum[0:HS, 2:4, 0:HALF], ALU.mult).then_inc(p_ready.sem, 1)
                for t in range(T):
                    dve.wait_ge(d_ready.sem, d_ready.at(t + 1))
                    b = 4 + 2 * (t % 2)
                    nc.vector.scalar_tensor_tensor(two(m.X[:, t]), m.psum[:, b:b + 2, 0:384], alpha[:, t:t + 1], two(m.X[:, t]),
                                                   ALU.mult, ALU.add).then_inc(d_done.sem, 1)
        params.close(48), g_ready.close(2), s_ready.close(1), p_ready.close(1), d_ready.close(T), d_done.close(T)
        sent.close(16 * 2 * T)


def expert_tiles(nc, m, g, plan, NT):
    names = ("rows_loaded", "weights_a", "weights_b", "streamed_a", "turned", "turned_saved", "hidden_turned", "hidden_saved",
             "gate_ready", "up_ready", "silu_ready", "hidden_ready", "down_ready", "made_ready")
    x_in, gate_in, up_in, down_in, x_turned, x_saved, h_turned, h_saved, gate_done, up_done, silu_done, h_made, down_done, y_saved = (
        m.c[k] for k in names)
    y_out, waited = m.c["made_out"], m.c["waited"]
    with ExitStack() as ctx:
        sb = scratch(nc, m, ctx)
        gate, up, down = (sb(k, [P, KD, D], F32) for k in ("gate", "up", "down"))
        rows = sb("token_rows", [P, D], F32)
        columns = sb("token_columns", [P, KD, P], F32)
        silu = sb("silu", [P, D], F32)
        hidden = sb("hidden", [P, D], F32)
        hiddenT = sb("hiddenT", [P, KD, P], F32)
        made = sb("made_rows", [P, D], F32)
        two = lambda v: v.rearrange("p (c n) -> p c n", c=2)
        flat = lambda v: v.rearrange("o p f -> (o p) f")
        with nc.Block() as block:
            @block.sync
            def _(sp):
                sp.dma_start(rows[:], m.tokens[0:P]).then_inc(x_in.sem, 16)
                with sp.Fori(0, NT) as i:
                    e = sp.value_load(plan[0:1, bass.ds(i, 1), 0], min_val=0, max_val=7)
                    new = sp.value_load(plan[0:1, bass.ds(i, 1), 1], min_val=0, max_val=1)

                    def weights(to, name, done, sem):
                        sp.wait_ge(done.sem, done.at(i))
                        sp.sem_inc(waited.sem, 1)
                        sp.dma_start(to[:].rearrange("p k f -> p (k f)"), flat(g[name][bass.ds(e, 1)]), cond=new).then_inc(sem.sem, 16)

                    weights(gate, "L3_ffn_w_gate", gate_done, gate_in)
                    weights(up, "L3_ffn_w_up", up_done, up_in)
                    sp.wait_ge(x_turned.sem, x_turned.at(i + 1))
                    sp.sem_inc(waited.sem, 1)
                    sp.dma_start(rows[:], m.tokens[bass.ds((i + 1) * P, P)]).then_inc(x_in.sem, 16)
                    weights(down, "L3_ffn_w_down", down_done, down_in)

            @block.tensor
            def _(pe):
                def turn(source, first_bank):
                    for k in range(KD):
                        ins = nc.tensor.transpose(m.psum[:, first_bank + k // 3, (k % 3) * P:(k % 3 + 1) * P], source[:, k * P:(k + 1) * P], m.ident[:])
                    return ins

                def product(left, right, bank):
                    for c in range(2):
                        for k in range(KD):
                            ins = nc.tensor.matmul(m.psum[:, bank + c, 0:384], left[:, k], right[:, k, c * 384:(c + 1) * 384],
                                                   start=(k == 0), stop=(k == KD - 1))
                    return ins

                def turn_tokens(i):
                    pe.wait_ge(x_in.sem, x_in.at(16 * (i + 1)))
                    pe.wait_ge(h_saved.sem, h_saved.at(i - 1))
                    turn(rows, 6).then_inc(x_turned.sem, 1)

                def down_product(i):
                    pe.wait_ge(down_in.sem, down_in.at(16 * (i + 1)))
                    pe.wait_ge(h_saved.sem, h_saved.at(i + 1))
                    pe.wait_ge(y_saved.sem, y_saved.at(i))
                    product(hiddenT, down, 4).then_inc(down_done.sem, 1)

                def tile(i, first=False):
                    pe.wait_ge(gate_in.sem, gate_in.at(16 * (i + 1)))
                    pe.wait_ge(x_saved.sem, x_saved.at(i + 1))
                    pe.wait_ge(silu_done.sem, silu_done.at(i))
                    product(columns, gate, 0).then_inc(gate_done.sem, 1)
                    pe.wait_ge(up_in.sem, up_in.at(16 * (i + 1)))
                    pe.wait_ge(h_made.sem, h_made.at(i))
                    product(columns, up, 2).then_inc(up_done.sem, 1)
                    turn_tokens(i + 1)
                    if not first:
                        down_product(i - 1)
                    pe.wait_ge(h_made.sem, h_made.at(i + 1))
                    pe.wait_ge(x_saved.sem, x_saved.at(i + 2))
                    turn(hidden, 6).then_inc(h_turned.sem, 1)

                turn_tokens(0)
                tile(0, first=True)
                with pe.Fori(1, NT) as i:
                    tile(i)
                down_product(NT - 1)

            @block.scalar
            def _(act):
                with act.Fori(0, NT) as i:
                    act.wait_ge(gate_done.sem, gate_done.at(i + 1))
                    act.wait_ge(h_made.sem, h_made.at(i))
                    nc.scalar.activation(two(silu[:]), m.psum[:, 0:2, 0:384], ACT.Silu, bias=m.zero[:]).then_inc(silu_done.sem, 1)
                    act.wait_ge(h_turned.sem, h_turned.at(i + 1))
                    nc.scalar.activation(hiddenT[:].rearrange("p (c k) n -> p c (k n)", c=2), m.psum[:, 6:8, 0:384], ACT.Copy).then_inc(h_saved.sem, 1)

            @block.vector
            def _(dve):
                def save_tokens(i):
                    dve.wait_ge(x_turned.sem, x_turned.at(i + 1))
                    nc.vector.tensor_copy(columns[:].rearrange("p (c k) n -> p c (k n)", c=2), m.psum[:, 6:8, 0:384]).then_inc(x_saved.sem, 1)

                def save_made(i):
                    dve.wait_ge(down_done.sem, down_done.at(i + 1))
                    dve.wait_ge(y_out.sem, y_out.at(16 * i))
                    nc.vector.tensor_copy(two(made[:]), m.psum[:, 4:6, 0:384]).then_inc(y_saved.sem, 1)

                def tile(i, first=False):
                    save_tokens(i + 1)
                    dve.wait_ge(silu_done.sem, silu_done.at(i + 1))
                    dve.wait_ge(h_turned.sem, h_turned.at(i))
                    nc.vector.tensor_tensor(two(hidden[:]), two(silu[:]), m.psum[:, 2:4, 0:384], ALU.mult).then_inc(h_made.sem, 1)
                    if not first:
                        save_made(i - 1)

                save_tokens(0)
                tile(0, first=True)
                with dve.Fori(1, NT) as i:
                    tile(i)
                save_made(NT - 1)

            @block.gpsimd
            def _(pool):
                with pool.Fori(0, NT) as i:
                    pool.wait_ge(y_saved.sem, y_saved.at(i + 1))
                    pool.sem_inc(waited.sem, 1)
                    pool.dma_start(m.made[bass.ds(i * P, P)], made[:]).then_inc(y_out.sem, 16)
                pool.wait_ge(y_out.sem, y_out.at(16 * NT))
        for c in (gate_in, up_in, down_in, y_out):
            c.close(16 * NT)
        x_in.close(16 * (NT + 1)), x_turned.close(NT + 1), x_saved.close(NT + 1)
        for c in (h_turned, h_saved, gate_done, up_done, silu_done, h_made, down_done, y_saved):
            c.close(NT)


def finish(nc, m, out):
    stored = m.c["stored"]
    with nc.Block() as block:
        @block.sync
        def _(sp):
            sp.dma_start(out[0:(T - 1) * P].rearrange("(t p) d -> p t d", p=P), m.X[:, 0:T - 1, :]).then_inc(stored.sem, 16)
            sp.dma_start(out[(T - 1) * P:NODES], m.X[0:LAST, T - 1, :]).then_inc(stored.sem, 16)
            sp.wait_ge(stored.sem, stored.at(32))
    stored.close(32)


def gnn_ffn_kernel(nc, g, out, until=(0, 8)):
    m = Memory()
    m.stage = 0
    with ExitStack() as ctx:
        m.c = {name: Counter(ctx.enter_context(nc.semaphore(name))) for name in COUNTERS}
        m.c |= {name: Counter(ctx.enter_context(nc.semaphore(name)), 0) for name in POOL_DMA_COUNTERS}
        m.psum = ctx.enter_context(nc.psum_tensor("psum", [P, 8, 512], F32))
        one = lambda name, shape, dt: ctx.enter_context(nc.sbuf_tensor(name, shape, dt))
        m.grid = nc.dram_tensor("grid", (NP * NP, 8), F32).ap()
        m.grid1 = nc.dram_tensor("grid1", (NP * NP, 1), F32).ap()
        m.logs = nc.dram_tensor("log_counts", (4, NP, NP), F32).ap()
        m.counts = nc.dram_tensor("counts", (4, NP, NP), F32).ap()
        m.from_dram = {h: nc.dram_tensor(f"from_rows_{h}", (NP, D + h), F32).ap() for h in (8, 1)}
        m.to_dram = {h: nc.dram_tensor(f"to_rows_{h}", (NP, D + h), F32).ap() for h in (8, 1)}
        m.gates32 = nc.dram_tensor("gates_32", (32, NP), F32).ap()
        m.tokens = nc.dram_tensor("tokens", ((tiles_bound(8) + 1) * P, D), F32).ap()
        m.made = nc.dram_tensor("made", (tiles_bound(8) * P, D), F32).ap()
        m.bias_rows = nc.dram_tensor("bias_rows", (32, D), F32).ap()
        setup(nc, m, g["x"], g["src"], g["dst"], g["edge_type_3"], one)
        blocks = [gat_v2_block, switch_block, gat_block, quant_block, rgat_block, deep_experts_block, gcn_block,
                  gated_experts_block]
        for b in blocks[until[0]:until[1]]:
            b(nc, m, g)
        finish(nc, m, out)


def host_layout(inputs):
    import numpy as np
    laid = {name: np.asarray(a) for name, a in inputs.items()}
    for name in ("src", "dst", "edge_type_3"):
        padded = np.full((ET * P,), -1, dtype=laid[name].dtype)
        padded[:EDGES] = laid[name]
        laid[name] = padded.reshape(P, ET)
    for name in ("L1_gnn_W1", "L1_gnn_W2", "L2_ffn_gate_w"):
        laid[name] = laid[name].T
    laid["L0_ffn_wi"] = laid["L0_ffn_wi"].transpose(1, 0, 2).reshape(D, -1)
    laid["L2_ffn_W1"] = laid["L2_ffn_W1"].reshape(16, 2, KD, P, 64).transpose(0, 3, 2, 1, 4).reshape(16, P, -1)
    laid["L2_ffn_W2"] = laid["L2_ffn_W2"].reshape(16, P, 64)
    w3 = np.concatenate([laid["L2_ffn_W3"].transpose(0, 2, 1), laid.pop("L2_ffn_b3")[:, :, None]], axis=2)
    laid["L2_ffn_W3"] = w3.reshape(16, 2, 2, P, 65).transpose(0, 3, 1, 2, 4).reshape(16, P, -1)
    laid["L2_ffn_Wl"] = laid["L2_ffn_Wl"].reshape(16, 2, 2, P, D).transpose(0, 3, 1, 2, 4).reshape(16, P, -1)
    for name in ("L2_ffn_b1", "L2_ffn_b2"):
        laid[name] = laid[name].reshape(16, P).T
    laid["L3_ffn_router_w"] = np.concatenate([laid["L3_ffn_router_w"], laid.pop("L3_ffn_sg_w")], axis=1)
    for name in ("L3_ffn_w_gate", "L3_ffn_w_up", "L3_ffn_w_down"):
        laid[name] = laid[name].reshape(8, KD, P, D).transpose(0, 2, 1, 3).reshape(8, P, -1)
    laid = {name: np.ascontiguousarray(a) for name, a in laid.items()}
    return laid


def kernel(**inputs):
    import concourse.bacc as _bacc
    from concourse.bass_utils import run_bass_kernel_spmd as _run

    nc = _bacc.Bacc("TRN2", target_bir_lowering=False, num_devices=1)
    arrays, g = {}, {}
    for name, a in host_layout(inputs).items():
        arrays[f"in_{name}"] = a
        g[name] = nc.dram_tensor(f"in_{name}", a.shape, mybir.dt.from_np(a.dtype), kind="ExternalInput").ap()
    out = nc.dram_tensor("out_x", (NODES, D), F32, kind="ExternalOutput").ap()
    gnn_ffn_kernel(nc, g, out)
    r = _run(nc, [arrays], core_ids=[0])
    return r.results[0]["out_x"]
```

```python
from contextlib import ExitStack, contextmanager

import concourse.bass as bass
from concourse import mybir

ALU = mybir.AluOpType
ACT = mybir.ActivationFunctionType
F32 = mybir.dt.float32
F16 = mybir.dt.float16
BF16 = mybir.dt.bfloat16
I32 = mybir.dt.int32
U32 = mybir.dt.uint32
AX_X = mybir.AxisListType.X

P = 128
NODES = 625
T = (NODES + P - 1) // P
NP = T * P
LAST = NODES - (T - 1) * P
D = 768
KD = D // P
EDGES = 20000
ET = 160
HALF = NP // 2
MASK = -1e30
FLOOR = -1e20
CREDIT = 64


class Counter:

    def __init__(self, sem, credit=CREDIT):
        self.sem, self.base = sem, credit

    def at(self, n):
        return self.base + n

    def close(self, n):
        self.base += n


class Steps:

    def __init__(self, engine, counter):
        self.engine, self.counter, self.first, self.k = engine, counter, counter.base, 0

    def then(self, instruction):
        instruction.then_inc(self.counter.sem, 1)
        self.k += 1
        self.engine.wait_ge(self.counter.sem, self.first + self.k)

    def done(self):
        self.counter.base = self.first + self.k

    @contextmanager
    def loop(self, start, end, per):
        self.done()
        base = self.counter.base
        with self.engine.Fori(start, end) as i:
            self.first, self.k = base + (i - start) * per, 0
            yield i
            assert self.k == per, (self.k, per)
        self.first, self.k = base + (end - start) * per, 0


COUNTERS = [
    "dve_step",
    "loaded", "constants", "params", "weights_a", "weights_b", "rows_loaded",
    "targets_ready", "sources_ready", "onehots_used", "distance_step", "counts_final", "counts_saved", "logs_ready", "logs_done", "log_made", "logs_out", "stored",
    "variance_ready", "deviation_ready", "rows_ready", "transposed", "columns_ready",
    "product_ready", "product_saved", "weights_used",
    "score_ready", "waited", "copied",
    "grid_a", "grid_b", "grid_used", "sum_ready", "last_sum_ready", "sum_used", "max_ready", "probs_ready", "probs_used",
    "turned", "turned_saved", "mixed", "mixed_saved",
    "elu_ready", "elu_done", "streamed_a", "streamed_b", "stream_used", "gate_rows_a", "gate_rows_b",
    "hidden_ready", "hidden_done", "hidden_used", "second_ready", "second_done",
    "cleared", "hidden_turned", "hidden_saved", "gate_ready", "up_ready", "silu_ready", "down_ready", "made_ready",
    "first_expert", "rows_loaded_b",
    "counts_out", "coef_loaded", "turned_loaded", "merged_ready", "merged_placed", "zeros_out",
]
POOL_DMA_COUNTERS = [f"pair_{j}" for j in range(8)] + ["scattered", "bias_out", "sent", "fetched", "made_out", "made_out_b"]


class Memory:
    pass


def scratch(nc, m, ctx):
    m.stage += 1
    stage = m.stage
    return lambda name, shape, dt: ctx.enter_context(nc.sbuf_tensor(f"{name}_{stage}", shape, dt))


def setup(nc, m, g, one):
    x, src, dst, etype = (g[k] for k in ("x", "src", "dst", "edge_type_3"))
    m.zeros = one("zeros", [P, 800], F32)
    m.clearing = 0
    m.merged = {v.key: one(f"merged_{v.key}", [P, len(v.turned), v.kk, v.columns], F32)
                for stage in ("edges_1", "edges_2") for v in score_vectors(g, stage)}
    m.ident = one("ident", [P, P], F32)
    m.after = one("after", [P, P], F32)
    m.iota16 = one("iota16", [P, NP], F16)
    m.X = one("X", [P, T, D], F32)
    m.H = one("H", [P, T, D], F32)
    m.HT = one("HT", [P, KD, NP], F32)
    m.eps5 = one("eps5", [P, 1], F32)
    m.eps6 = one("eps6", [P, 1], F32)
    m.from_row = one("from_row", [P, ET], U32)
    m.to_row = one("to_row", [P, ET], U32)
    m.cell = one("cell", [P, ET], U32)
    m.counted = one("counted", [P, 3, ET], F32)
    m.minus_to = one("minus_to", [P, ET], F32)
    m.ones = one("ones", [P, P], F32)
    m.rank = one("rank", [P, 32], F32)
    m.zero = one("zero", [P, 1], F32)
    m.part = one("part", [P, 1], F32)
    with ExitStack() as ctx:
        sb = scratch(nc, m, ctx)
        iota = sb("iota", [P, NP], I32)
        part = sb("part", [P, 1], I32)
        iota_f = sb("iota_f", [P, NP], F32)
        part_f = sb("part_f", [P, 1], F32)
        ends = sb("ends", [P, 3, ET], I32)
        ends_f = sb("ends_f", [P, 3, ET], F32)
        f0 = sb("f0", [P, ET], F32)
        f1 = sb("f1", [P, ET], F32)
        src_f, dst_f, type_f = (ends_f[:, k] for k in range(3))
        clear, loaded, const = m.c["cleared"], m.c["loaded"], m.c["constants"]
        with nc.Block() as block:
            @block.sync
            def _(sp):
                for name in COUNTERS:
                    sp.sem_inc(m.c[name].sem, CREDIT)
                for k, end in enumerate((src, dst, etype)):
                    sp.dma_start(ends[:, k, :], end).then_inc(loaded.sem, 16)
                sp.dma_start(m.X[:, 0:T - 1, :], x[0:(T - 1) * P].rearrange("(t p) d -> p t d", p=P)).then_inc(loaded.sem, 16)
                sp.wait_ge(clear.sem, clear.at(2))
                sp.dma_start(m.X[0:LAST, T - 1, :], x[(T - 1) * P:NODES]).then_inc(loaded.sem, 16)

            @block.gpsimd
            def _(pool):
                nc.gpsimd.memset(m.X[:, T - 1, :], 0.0).then_inc(clear.sem, 1)
                nc.gpsimd.memset(m.zeros[:], 0.0).then_inc(clear.sem, 1)
                nc.gpsimd.iota(iota[:], pattern=[[1, NP]], base=0, channel_multiplier=0).then_inc(const.sem, 1)
                nc.gpsimd.iota(part[:], pattern=[[0, 1]], base=0, channel_multiplier=1).then_inc(const.sem, 1)

            @block.vector
            def _(dve):
                steps = Steps(dve, m.c["dve_step"])
                nc.vector.memset(m.eps5[:], 1e-5)
                nc.vector.memset(m.eps6[:], 1e-6)
                nc.vector.memset(m.zero[:], 0.0)
                nc.vector.memset(m.ones[:], 1.0)
                dve.wait_ge(const.sem, const.at(2))
                nc.vector.tensor_copy(iota_f[:], iota[:])
                steps.then(nc.vector.tensor_copy(part_f[:], part[:]))
                nc.vector.tensor_copy(m.iota16[:], iota_f[:])
                nc.vector.tensor_copy(m.rank[:], iota_f[:, 0:32])
                nc.vector.tensor_copy(m.part[:], part_f[:])
                nc.vector.tensor_scalar(m.ident[:], iota_f[:, 0:P], part_f[:], None, ALU.is_equal)
                nc.vector.tensor_scalar(m.after[:], iota_f[:, 0:P], part_f[:], None, ALU.is_ge)
                dve.wait_ge(loaded.sem, loaded.at(16 * 5))
                steps.then(nc.vector.tensor_copy(ends_f[:], ends[:]))
                nc.vector.tensor_scalar(m.from_row[:], src_f, 0.0, None, ALU.max)
                nc.vector.tensor_scalar(m.to_row[:], dst_f, 0.0, None, ALU.max)
                nc.vector.tensor_scalar(f0[:], src_f, 0.0, None, ALU.max)
                steps.then(nc.vector.tensor_scalar(f1[:], dst_f, 0.0, float(NP), ALU.max, ALU.mult))
                steps.then(nc.vector.tensor_tensor(m.cell[:], f0[:], f1[:], ALU.add))
                steps.then(nc.vector.tensor_scalar(f0[:], src_f, 1.0, None, ALU.add))
                nc.vector.tensor_copy(m.counted[:, 0], src_f)
                nc.vector.tensor_scalar(m.minus_to[:], dst_f, -1.0, None, ALU.mult)
                for r in range(2):
                    steps.then(nc.vector.scalar_tensor_tensor(m.counted[:, 1 + r], type_f, float(r), f0[:], ALU.is_equal, ALU.mult))
                    steps.then(nc.vector.tensor_scalar(m.counted[:, 1 + r], m.counted[:, 1 + r], -1.0, None, ALU.add))
                steps.done()
        clear.close(2), loaded.close(80), const.close(2)


class LogCounts:

    def __init__(self, nc, m, sb, relations):
        self.nc, self.m, self.relations = nc, m, relations
        slots = min(2, len(relations))
        self.count = sb("count", [P, slots, T, NP], F32)
        self.mask = sb("mask", [P, slots, T, NP], F32)
        self.loads = (m.c["grid_a"], m.c["grid_b"])
        self.logs, self.logged, self.ready, self.stored = (m.c[k] for k in ("logs_ready", "logs_done", "log_made", "logs_out"))

    def sync(self, sp):
        rows = lambda a: a.rearrange("(t p) s -> p t s", p=P)

        def store(n):
            sp.wait_ge(self.ready.sem, self.ready.at(n + 1))
            sp.dma_start(rows(self.m.logs[self.relations[n]]), self.count[:, n % 2]).then_inc(self.stored.sem, 16)

        for n, r in enumerate(self.relations):
            if n >= 2:
                sp.wait_ge(self.stored.sem, self.stored.at(16 * (n - 1)))
            sp.dma_start(self.count[:, n % 2], rows(self.m.counts[r])).then_inc(self.loads[n % 2].sem, 16)
            if n:
                store(n - 1)
        store(len(self.relations) - 1)
        sp.wait_ge(self.stored.sem, self.stored.at(16 * len(self.relations)))

    def vector(self, dve, steps, n):
        vector, s = self.nc.vector, n % 2
        count, mask = self.count[:, s], self.mask[:, s]
        dve.wait_ge(self.loads[s].sem, self.loads[s].at(16 * (n // 2 + 1)))
        vector.tensor_scalar(mask, count, 0.0, MASK, ALU.is_equal, ALU.mult)
        steps.then(vector.tensor_scalar(count, count, 1.0, None, ALU.max))
        dve.sem_inc(self.logs.sem, 1)
        dve.wait_ge(self.logged.sem, self.logged.at(n + 1))
        steps.then(vector.tensor_tensor(count, count, mask, ALU.add))
        dve.sem_inc(self.ready.sem, 1)

    def scalar(self, act):
        for n in range(len(self.relations)):
            act.wait_ge(self.logs.sem, self.logs.at(n + 1))
            self.nc.scalar.activation(self.count[:, n % 2], self.count[:, n % 2], ACT.Ln, bias=self.m.zero[:]).then_inc(self.logged.sem, 1)

    def close(self):
        n = len(self.relations)
        self.loads[0].close(16 * ((n + 1) // 2)), self.loads[1].close(16 * (n // 2))
        self.logs.close(n), self.logged.close(n), self.ready.close(n), self.stored.close(16 * n)


def log_counts(nc, m, relation):
    with ExitStack() as ctx:
        logs = LogCounts(nc, m, scratch(nc, m, ctx), [relation])
        with nc.Block() as block:
            @block.sync
            def _(sp):
                logs.sync(sp)

            @block.vector
            def _(dve):
                steps = Steps(dve, m.c["dve_step"])
                logs.vector(dve, steps, 0)
                steps.done()

            @block.scalar
            def _(act):
                logs.scalar(act)
        logs.close()


def normalise(nc, m, src, dst, eps, scale=None, shift=None, turned=None, ahead=None, clear=False, onto=None):
    with ExitStack() as ctx:
        sb = scratch(nc, m, ctx)
        stats = sb("stats", [P, T, 2, 6], F32)
        mean = sb("mean", [P, T, 2], F32)
        dev = sb("dev", [P, T], F32)
        rdev = sb("rdev", [P, T], F32)
        affine = sb("affine", [P, 2, D], F32) if scale is not None else None
        var_ready, dev_ready, ready, params = (m.c[k] for k in ("variance_ready", "deviation_ready", "rows_ready", "params"))
        with nc.Block() as block:
            @block.sync
            def _(sp):
                if scale is not None:
                    sp.dma_start(affine[:, 0], scale.partition_broadcast(P)).then_inc(params.sem, 16)
                    sp.dma_start(affine[:, 1], shift.partition_broadcast(P)).then_inc(params.sem, 16)
                if ahead is not None:
                    ahead.start(sp)
                if clear:
                    for table in (m.grid, m.grid1, m.tokens):
                        table = table.rearrange("(p r) h -> p (r h)", p=P)
                        n = max(n for n in range(1, m.zeros.shape[1] + 1) if table.shape[1] % n == 0)
                        for k in range(0, table.shape[1], 8 * n):
                            to = table[:, k:min(k + 8 * n, table.shape[1])].rearrange("p (r n) -> p r n", n=n)
                            sp.dma_start(to, m.zeros[:, 0:n].unsqueeze(1).to_broadcast(list(to.shape))).then_inc(m.c["zeros_out"].sem, 16)
                            m.clearing += 1

            @block.vector
            def _(dve):
                steps = Steps(dve, m.c["dve_step"])
                for t in range(T):
                    for h in range(2):
                        ins = nc.vector.bn_stats(stats[:, t, h], src[:, t, h * 384:(h + 1) * 384])
                steps.then(ins)
                for t in range(T):
                    ins = nc.vector.bn_aggr(mean[:, t], stats[:, t].rearrange("p a b -> p (a b)"))
                ins.then_inc(var_ready.sem, 1)
                dve.wait_ge(dev_ready.sem, dev_ready.at(1))
                steps.then(nc.vector.reciprocal(rdev[:], dev[:]))
                if scale is not None:
                    dve.wait_ge(params.sem, params.at(32))
                for t in range(T):
                    ins = nc.vector.tensor_scalar(dst[:, t], src[:, t], mean[:, t, 0:1], rdev[:, t:t + 1],
                                                  ALU.subtract, ALU.mult)
                    if scale is not None:
                        steps.then(ins)
                        steps.then(nc.vector.tensor_tensor(dst[:, t], dst[:, t], affine[:, 0], ALU.mult))
                        ins = nc.vector.tensor_tensor(dst[:, t], dst[:, t], affine[:, 1], ALU.add)
                    if onto is not None:
                        steps.then(ins)
                        ins = nc.vector.tensor_tensor(onto[:, t], onto[:, t], dst[:, t], ALU.add)
                    ins.then_inc(ready.sem, 1)
                steps.done()

            if turned is not None:
                @block.tensor
                def _(pe):
                    turn_rows(nc, m, pe, dst)

            @block.scalar
            def _(act):
                act.wait_ge(var_ready.sem, var_ready.at(1))
                nc.scalar.activation(dev[:], mean[:, :, 1], ACT.Sqrt, bias=eps[:]).then_inc(dev_ready.sem, 1)
                if turned is not None:
                    save_turned(nc, m, act, turned)
        close_turn(m, 1 if turned is not None else 0)
        var_ready.close(1), dev_ready.close(1), ready.close(T)
        if scale is not None:
            params.close(32)


def turn_rows(nc, m, pe, rows):
    ready, turned, saved = m.c["rows_ready"], m.c["transposed"], m.c["columns_ready"]
    nk = rows.shape[2] // P
    for t in range(T):
        pe.wait_ge(ready.sem, ready.at(t + 1))
        pe.wait_ge(saved.sem, saved.at(t - 1))
        for k in range(nk):
            b = 2 * (t % 2) + k // 4
            ins = nc.tensor.transpose(m.psum[:, b, (k % 4) * P:(k % 4 + 1) * P], rows[:, t, k * P:(k + 1) * P], m.ident[:])
        ins.then_inc(turned.sem, 1)


def save_turned(nc, m, act, columns):
    turned, saved = m.c["transposed"], m.c["columns_ready"]
    nk = columns.shape[1]
    for t in range(T):
        act.wait_ge(turned.sem, turned.at(t + 1))
        for k0 in range(0, nk, 4):
            n = min(4, nk - k0)
            src = m.psum[:, 2 * (t % 2) + k0 // 4, 0:n * P].rearrange("p (k c) -> p k c", k=n)
            ins = nc.scalar.activation(columns[:, k0:k0 + n, t * P:(t + 1) * P], src, ACT.Copy)
        ins.then_inc(saved.sem, 1)


def close_turn(m, n):
    m.c["transposed"].close(n * T), m.c["columns_ready"].close(n * T)


class ScoreVectors:

    def __init__(self, key, turned, vectors, r=P, own=False, factor=1.0):
        self.key, self.turned, self.r, self.own, self.factor = key, turned, r, own, factor
        self.vectors = [v if len(v.shape) == 2 else v.rearrange("(f o) -> f o", o=1) for v in vectors]
        self.rows, self.kk = turned[0].shape[0], turned[0].shape[1] // P
        self.chunks, self.n = self.rows // r, sum(v.shape[1] for v in self.vectors)
        self.columns = self.n * self.chunks if own else self.n


def score_vectors(g, stage):
    flat = lambda a: a.rearrange("h c -> (h c)")
    if stage == "edges_1":
        return [ScoreVectors("L0_2", [g["L0_gnn_Wos_turned"], g["L0_gnn_Wod_turned"]], [flat(g["L0_gnn_attno"])], factor=0.2)]
    made = [ScoreVectors(f"L1_{k}", [g[f"L1_gnn_W{k}"]], [flat(g[f"L1_gnn_att_src{k}"]), flat(g[f"L1_gnn_att_dst{k}"])], own=(k == 1))
            for k in (1, 2)]
    return made + [ScoreVectors(f"L2_{k}", [g[f"L2_gnn_W{k}_turned"][r] for r in range(3)], [g[f"L2_gnn_k{k}"], g[f"L2_gnn_q{k}"]])
                   for k in (1, 2)]


class Merger:
    BANK = 7

    def __init__(self, nc, m, sb, groups):
        self.nc, self.m, self.groups = nc, m, groups
        self.items = [(v, k) for v in groups for k in range(len(v.turned))]
        self.buffer = sb("weights_turned", [P, max(v.chunks * v.kk for v in groups) * P], F32)
        self.coef = {v.key: sb(f"vectors_{v.key}", [v.r, v.chunks, v.n], F32) for v in groups}
        self.coef_in, self.ready = m.c["coef_loaded"], m.c["merged_ready"]
        self.turned_in = m.c["turned_loaded"]
        self.loads = sum(len(v.vectors) for v in groups)
        self.chunks_loaded = 0
        self.pieces = [piece for n, (v, _) in enumerate(self.items) for piece in [(n, k) for k in range(v.kk)] + [None] * 3]

    def view(self, v):
        return self.buffer[0:v.r, 0:v.chunks * v.kk * P].rearrange("r (j d) -> r j d", j=v.chunks)

    def load(self, sp):
        for v in self.groups:
            at = 0
            for vector in v.vectors:
                with self.nc.allow_non_contiguous_dma("a few thousand numbers"):
                    sp.dma_start(self.coef[v.key][:, :, at:at + vector.shape[1]], vector.rearrange("(j r) n -> r j n", r=v.r)).then_inc(self.coef_in.sem, 16)
                at += vector.shape[1]
        for n, (v, k) in enumerate(self.items):
            if n:
                sp.wait_ge(self.ready.sem, self.ready.at(n))
            for c in range(v.chunks):
                if self.chunks_loaded:
                    sp.wait_ge(self.turned_in.sem, self.turned_in.at(16 * self.chunks_loaded))
                sp.dma_start(self.view(v)[:, c], v.turned[k][c * v.r:(c + 1) * v.r]).then_inc(self.turned_in.sem, 16)
                self.chunks_loaded += 1

    def product(self, pe, n, k):
        v, _ = self.items[n]
        at = sum(u.kk * u.columns for u, _ in self.items[:n]) + k * v.columns
        if n == 0 and k == 0:
            pe.wait_ge(self.coef_in.sem, self.coef_in.at(16 * self.loads))
        if k == 0:
            pe.wait_ge(self.turned_in.sem, self.turned_in.at(16 * sum(u.chunks for u, _ in self.items[:n + 1])))
        for c in range(v.chunks):
            first = at + (c * v.n if v.own else 0)
            ins = self.nc.tensor.matmul(self.m.psum[:, self.BANK, first:first + v.n], self.view(v)[:, c, k * P:(k + 1) * P], self.coef[v.key][:, c],
                                        start=(v.own or c == 0), stop=(v.own or c == v.chunks - 1))
        if k == v.kk - 1:
            ins.then_inc(self.ready.sem, 1)

    def empty_bank(self, dve):
        dve.wait_ge(self.ready.sem, self.ready.at(len(self.items)))
        at = 0
        for v, k in self.items:
            src = self.m.psum[:, self.BANK, at:at + v.kk * v.columns].rearrange("p (k n) -> p k n", k=v.kk)
            self.nc.vector.tensor_scalar(self.m.merged[v.key][:, k], src, v.factor, None, ALU.mult)
            at += v.kk * v.columns

    def close(self):
        self.coef_in.close(16 * self.loads), self.turned_in.close(16 * self.chunks_loaded), self.ready.close(len(self.items))


class Job:

    def __init__(self, weights, rows, bias=None, scale=None, merged=None, vector=None, heads=0, scores=None, order="p n -> p n", sizes={}, bias_by=None,
                 to_dram=None):
        self.weights, self.rows, self.bias, self.scale, self.merged = weights, rows, bias, scale, merged
        self.scores, self.order, self.sizes, self.vector, self.heads = scores, order, sizes, vector, heads
        self.bias_by, self.to_dram = bias_by, to_dram


class Projection:

    def __init__(self, nc, m, sb, jobs, loads=()):
        self.nc, self.m, self.jobs, self.loads = nc, m, jobs, loads
        rows, self.width = jobs[0].weights.shape
        self.kk = rows // P
        self.slots = min(2, len(jobs))
        job = jobs[0]
        self.extra = job.heads if job.merged is None else job.merged.shape[2]
        self.weights = sb("weights", [P, self.slots, self.kk, self.width + self.extra], F32)
        self.bias = sb("bias", [P, self.slots, self.width], F32) if job.bias is not None else None
        self.counters = (m.c["weights_a"], m.c["weights_b"])
        self.started = False
        if job.bias_by is not None:
            self.bias_work = sb("bias_work", [P, self.width], F32)
            self.bias_score = sb("bias_score", [P, self.extra], F32)

    def load(self, sp, j):
        job, c = self.jobs[j], self.counters[j % 2]
        sp.dma_start(self.weights[:, j % 2, :, 0:self.width], job.weights.rearrange("(k p) f -> p k f", p=P)).then_inc(c.sem, 16)
        if job.bias is not None:
            sp.dma_start(self.bias[:, j % 2], job.bias.partition_broadcast(P)).then_inc(c.sem, 16)

    def start(self, sp):
        for to, source in self.loads:
            sp.dma_start(to, source).then_inc(self.m.c["coef_loaded"].sem, 16)
        for j in range(self.slots):
            self.load(sp, j)
        self.started = True

    def run(self, columns, logs=None):
        nc, m, jobs, weights, bias, load = self.nc, self.m, self.jobs, self.weights, self.bias, self.counters
        kk, width, extra = self.kk, self.width, self.extra
        parts = (width + 511) // 512
        w = width // parts
        ranges = [(c * w, (c + 1) * w) for c in range(parts)]
        if extra == 0:
            score_bank = score_at = None
        elif w + extra <= 512:
            ranges[-1] = (ranges[-1][0], width + extra)
            score_bank, score_at = parts - 1, w
        else:
            ranges.append((width, width + extra))
            score_bank, score_at = parts, 0
        names = ("weights_used", "product_ready", "product_saved", "merged_placed", "coef_loaded", "stored")
        used, ready, saved, placed, coef_in, stored = (m.c[k] for k in names)
        per = 16 if bias is None else 32
        J = len(jobs)
        stores = 0
        with nc.Block() as block:
            @block.sync
            def _(sp):
                nonlocal stores
                if not self.started:
                    self.start(sp)
                for j in range(2, J):
                    sp.wait_ge(used.sem, used.at(j - 1))
                    sp.wait_ge(saved.sem, saved.at((j - 1) * T))
                    self.load(sp, j)
                for j, job in enumerate(jobs):
                    if job.to_dram is not None:
                        for t in range(T):
                            sp.wait_ge(saved.sem, saved.at(j * T + t + 1))
                            sp.dma_start(job.to_dram[t * P:(t + 1) * P], job.rows[:, t]).then_inc(stored.sem, 16)
                            stores += 1
                if stores:
                    sp.wait_ge(stored.sem, stored.at(16 * stores))
                if logs is not None:
                    logs.sync(sp)

            if logs is not None:
                @block.scalar
                def _(act):
                    logs.scalar(act)

            @block.tensor
            def _(pe):
                for j in range(J):
                    pe.wait_ge(load[j % 2].sem, load[j % 2].at(per * (j // 2 + 1)))
                    if extra:
                        pe.wait_ge(placed.sem, placed.at(j + 1))
                    for t in range(T):
                        u = j * T + t
                        pe.wait_ge(saved.sem, saved.at(u - 1))
                        for c, (lo, hi) in enumerate(ranges):
                            for k in range(kk):
                                ins = nc.tensor.matmul(m.psum[:, 3 * (u % 2) + c, 0:hi - lo], columns[:, k, t * P:(t + 1) * P],
                                                       weights[:, j % 2, k, lo:hi], start=(k == 0), stop=(k == kk - 1))
                        ins.then_inc(ready.sem, 1)
                    pe.wait_ge(ready.sem, ready.at((j + 1) * T))
                    pe.sem_inc(used.sem, 1)

            @block.vector
            def _(dve):
                steps = Steps(dve, m.c["dve_step"])

                def place_merged(j):
                    if j >= 2:
                        dve.wait_ge(used.sem, used.at(j - 1))
                    nc.vector.tensor_copy(weights[:, j % 2, :, width:width + extra], jobs[j].merged).then_inc(placed.sem, 1)

                def merge_rows(j, k):
                    dve.wait_ge(load[j % 2].sem, load[j % 2].at(per * (j // 2 + 1)))
                    dve.wait_ge(coef_in.sem, coef_in.at(16 * len(self.loads)))
                    last = weights[:, j % 2, k, width:width + extra]
                    steps.then(nc.vector.tensor_tensor(self.bias_work[:], weights[:, j % 2, k, 0:width], jobs[j].vector[:], ALU.mult))
                    steps.then(nc.vector.tensor_reduce(last, self.bias_work[:].rearrange("p (h c) -> p h c", h=extra), AX_X, ALU.add))
                    steps.then(nc.vector.tensor_scalar(last, last, 0.2, None, ALU.mult))
                    if k == kk - 1:
                        dve.sem_inc(placed.sem, 1)

                by_rows = extra and jobs[0].merged is None
                if by_rows:
                    for k in range(kk):
                        merge_rows(0, k)
                elif extra:
                    place_merged(0)
                for j, job in enumerate(jobs):
                    dve.wait_ge(load[j % 2].sem, load[j % 2].at(per * (j // 2 + 1)))
                    if job.bias_by is not None:
                        if j == 0:
                            dve.wait_ge(coef_in.sem, coef_in.at(16 * len(self.loads)))
                        steps.then(nc.vector.tensor_tensor(self.bias_work[:], bias[:, j % 2], job.bias_by[:], ALU.mult))
                        steps.then(nc.vector.tensor_reduce(self.bias_score[:], self.bias_work[:].rearrange("p (h c) -> p h c", h=extra),
                                                           AX_X, ALU.add))
                        steps.then(nc.vector.tensor_scalar(self.bias_score[:], self.bias_score[:], 0.2, None, ALU.mult))
                    for t in range(T):
                        if extra and not by_rows and t == T - 1 and j + 1 < J:
                            place_merged(j + 1)
                        if by_rows and j + 1 < J:
                            for k in range(kk * t // T, kk * (t + 1) // T):
                                merge_rows(j + 1, k)
                        u = j * T + t
                        dve.wait_ge(ready.sem, ready.at(u + 1))
                        bank = 3 * (u % 2)
                        src = m.psum[:, bank:bank + parts, 0:w]
                        out = job.rows[:, t, 0:width].rearrange("p (c w) -> p c w", c=parts)
                        if job.bias is not None:
                            ins = nc.vector.tensor_tensor(out, src, bias[:, j % 2].rearrange("p (c w) -> p c w", c=parts), ALU.add)
                        elif job.scale is not None:
                            ins = nc.vector.tensor_scalar(out, src, job.scale[:, t:t + 1], None, ALU.mult)
                        else:
                            ins = nc.vector.tensor_copy(out, src)
                        if extra:
                            src = m.psum[:, bank + score_bank, score_at:score_at + extra].rearrange(job.order, **job.sizes)
                            if job.bias_by is not None:
                                ins = nc.vector.tensor_tensor(job.scores(t), src, self.bias_score[:].rearrange(job.order, **job.sizes), ALU.add)
                            else:
                                ins = nc.vector.tensor_copy(job.scores(t), src)
                        ins.then_inc(saved.sem, 1)
                        if logs is not None and u < len(logs.relations):
                            logs.vector(dve, steps, u)
                steps.done()
        for k in range(2):
            n = (J + 1 - k) // 2
            load[k].close(per * n)
        used.close(J), ready.close(J * T), saved.close(J * T), stored.close(16 * stores)
        coef_in.close(16 * len(self.loads))
        if logs is not None:
            logs.close()
        if extra:
            placed.close(J)


def edge_scores(nc, m, coef, heads, grid, passes, saves, vectors):
    W = D + heads
    U = 8
    from_dram = m.from_dram[heads]
    to_dram = m.to_dram[heads]
    with ExitStack() as ctx:
        sb = scratch(nc, m, ctx)
        low = sb("low", [P, D], F32)
        work = sb("work", [P, 2, D], F32)
        params = m.c["params"]
        rows_of = sb("rows_of", [P, 2, 3, U], U32)
        both = sb("both", [P, U, W], F32)
        score = sb("score", [P, U, heads], F32)
        part = sb("part", [P, 2, heads], F32)
        C = len(passes)
        HOTS = 4
        distance = sb("distance", [P, 2, NP], F16)
        to_hot = sb("to_hot", [P, HOTS, NP], BF16)
        from_hot = sb("from_hot", [P, HOTS, NP], BF16)
        counts = sb("counts", [P, T, NP], F32)
        counts2 = sb("counts2", [P, T, NP], F32) if C == 2 else None
        rest = sb("rest", [P, 2, T, NP], F32) if C == 1 else None
        far, counts_out = m.c["distance_step"], m.c["counts_out"]
        merger = Merger(nc, m, sb, vectors)
        landed = [m.c[f"pair_{j}"] for j in range(U)]
        scored, scattered = m.c["score_ready"], m.c["scattered"]
        waited, copied = m.c["waited"], m.c["copied"]
        to_ready, from_ready, hots_used, counted, emptied = (
            m.c[k] for k in ("targets_ready", "sources_ready", "onehots_used", "counts_final", "counts_saved"))
        TURNS = ET // U
        ADD, SCATTER = 2, 5

        def wide(t):
            return m.psum[:, t, :]

        def narrow(t):
            return m.psum[:, T + t // 4, (t % 4) * P:(t % 4 + 1) * P]

        with nc.Block() as block:
            @block.gpsimd
            def _(pool):
                def after(counter, n):
                    pool.wait_ge(counter.sem, n)
                    pool.sem_inc(waited.sem, 1)

                def turn(i, parity, first=False, last=False):
                    if not last:
                        cols = bass.ds(i * U, U)
                        nc.gpsimd.tensor_copy(rows_of[:, parity, 0], m.from_row[:, cols])
                        nc.gpsimd.tensor_copy(rows_of[:, parity, 1], m.to_row[:, cols])
                        nc.gpsimd.tensor_copy(rows_of[:, parity, 2], m.cell[:, cols]).then_inc(copied.sem, 1)
                        after(copied, copied.at(i + 1))
                    for j in range(U):
                        if not last:
                            nc.gpsimd.indirect_dma_start(
                                out=both[:, j], out_offset=None, in_=from_dram,
                                in_offset=bass.IndirectOffsetOnAxis(ap=rows_of[:, parity, 0, j:j + 1], axis=0)).then_inc(landed[j].sem, 16)
                        same = j >= ADD
                        if same and not last or not same and not first:
                            k, q, of = (j - ADD) % U, parity if same else 1 - parity, i if same else i - 1
                            after(landed[k], landed[k].at(32 * of + 16))
                            nc.gpsimd.indirect_dma_start(
                                out=both[:, k], out_offset=None, in_=to_dram,
                                in_offset=bass.IndirectOffsetOnAxis(ap=rows_of[:, q, 1, k:k + 1], axis=0),
                                compute_op=ALU.add).then_inc(landed[k].sem, 16)
                        same = j >= SCATTER
                        if same and not last or not same and not first:
                            k, q, n = (j - SCATTER) % U, parity if same else 1 - parity, i * U + j - SCATTER
                            after(scored, scored.at(n + 1))
                            after(scattered, scattered.at(16 * n))
                            nc.gpsimd.indirect_dma_start(
                                out=grid, out_offset=bass.IndirectOffsetOnAxis(ap=rows_of[:, q, 2, k:k + 1], axis=0),
                                in_=score[:, k], in_offset=None).then_inc(scattered.sem, 16)

                if heads > 1:
                    pool.wait_ge(m.c["zeros_out"].sem, m.c["zeros_out"].at(16 * m.clearing))
                turn(0, 0, first=True)
                with pool.Fori(0, TURNS // 2 - 1) as i:
                    turn(2 * i + 1, 1)
                    turn(2 * i + 2, 0)
                turn(TURNS - 1, 1)
                turn(TURNS, 0, last=True)
                pool.wait_ge(scattered.sem, scattered.at(16 * ET))

            @block.vector
            def _(dve):
                steps = Steps(dve, m.c["dve_step"])

                def turns(start, end, n_pass):
                    with steps.loop(start, end, 2 * U) as i:
                        for j in range(U):
                            for c in range(C):
                                q = C * (U * i + j) + c
                                tile = q - n_pass * ET
                                dve.wait_ge(hots_used.sem, hots_used.at(q - HOTS + 1))
                                nc.vector.tensor_scalar(from_hot[:, (C * j + c) % HOTS], m.iota16[:], m.counted[:, passes[n_pass], bass.ds(tile, 1)],
                                                        None, ALU.is_equal).then_inc(from_ready.sem, 1)
                            dve.wait_ge(landed[j].sem, landed[j].at(32 * i + 32))
                            steps.then(nc.vector.scalar_tensor_tensor(work[:, j % 2], both[:, j, 0:D], 0.0, low[:], ALU.max, ALU.mult))
                            steps.then(nc.vector.tensor_reduce(part[:, j % 2], work[:, j % 2].rearrange("p (h c) -> p h c", h=heads),
                                                               AX_X, ALU.add))
                            nc.vector.tensor_tensor(score[:, j], part[:, j % 2], both[:, j, D:W], ALU.add).then_inc(scored.sem, 1)

                steps.then(nc.vector.tensor_scalar(low[:], coef[:], 0.8, None, ALU.mult))

                def save_counts(n_pass, to):
                    dve.wait_ge(counted.sem, counted.at(n_pass + 1))
                    nc.vector.tensor_copy(to[:, :, 0:512], m.psum[:, 0:T, :])
                    nc.vector.tensor_copy(to[:, 0:4, 512:NP], m.psum[:, T, :].rearrange("p (t c) -> p t c", t=4))
                    nc.vector.tensor_copy(to[:, 4, 512:NP], narrow(4)).then_inc(emptied.sem, 1)

                for k in range(C):
                    turns(k * TURNS // C, (k + 1) * TURNS // C, k)
                    save_counts(k, (counts, counts2)[k])
                merger.empty_bank(dve)
                if C == 1:
                    dve.wait_ge(params.sem, params.at(32))
                    dve.wait_ge(emptied.sem, emptied.at(1))
                    steps.then(nc.vector.tensor_tensor(rest[:, 0], rest[:, 0], rest[:, 1], ALU.subtract))
                    nc.vector.tensor_tensor(rest[:, 0], rest[:, 0], counts[:], ALU.subtract).then_inc(emptied.sem, 1)
                steps.done()

            @block.scalar
            def _(act):
                def turns(start, end, n_pass):
                    with act.Fori(start, end) as i:
                        for j in range(U * C):
                            q = C * U * i + j
                            tile = q - n_pass * ET
                            act.wait_ge(far.sem, far.at(2 * q - 2))
                            nc.scalar.activation(distance[:, j % 2], m.iota16[:], ACT.Abs, bias=m.minus_to[:, bass.ds(tile, 1)]).then_inc(far.sem, 1)
                            act.wait_ge(hots_used.sem, hots_used.at(q - HOTS + 1))
                            act.wait_ge(far.sem, far.at(2 * q + 1))
                            nc.scalar.activation(to_hot[:, j % HOTS], distance[:, j % 2], ACT.Relu, bias=m.ones[:, 0:1], scale=-1.0).then_inc(to_ready.sem, 1)
                            act.sem_inc(far.sem, 1)

                for k in range(C):
                    turns(k * TURNS // C, (k + 1) * TURNS // C, k)

            @block.tensor
            def _(pe):
                def product(q, slot, first=False, last=False):
                    pe.wait_ge(to_ready.sem, to_ready.at(q + 1))
                    pe.wait_ge(from_ready.sem, from_ready.at(q + 1))
                    for t in range(T):
                        rows = to_hot[:, slot, t * P:(t + 1) * P]
                        nc.tensor.matmul(wide(t), rows, from_hot[:, slot, 0:512], start=first, stop=last)
                        ins = nc.tensor.matmul(narrow(t), rows, from_hot[:, slot, 512:NP], start=first and t % 4 == 0,
                                               stop=last and t % 4 == 3 or last and t == T - 1, skip_group_check=True)
                    ins.then_inc(hots_used.sem, 1)

                for n_pass in range(C):
                    if n_pass:
                        pe.wait_ge(emptied.sem, emptied.at(n_pass))
                    q = n_pass * ET
                    for j in range(HOTS):
                        product(q + j, j, first=(j == 0))
                    parts = min((ET // HOTS - 2) // 2, len(merger.pieces))
                    cuts = [1 + (ET // HOTS - 2) * k // parts for k in range(parts + 1)]
                    pieces = merger.pieces[n_pass * len(merger.pieces) // C:(n_pass + 1) * len(merger.pieces) // C]
                    for part, (start, end) in enumerate(zip(cuts, cuts[1:])):
                        with pe.Fori(start, end) as i:
                            for j in range(HOTS):
                                product(q + HOTS * i + j, j)
                        for piece in pieces[part * len(pieces) // parts:(part + 1) * len(pieces) // parts]:
                            if piece is not None:
                                merger.product(pe, *piece)
                    for j in range(HOTS):
                        product(q + ET - HOTS + j, j, last=(j == HOTS - 1))
                    pe.wait_ge(hots_used.sem, hots_used.at(q + ET))
                    pe.sem_inc(counted.sem, 1)

            @block.sync
            def _(sp):
                rows = lambda k: m.counts[k].rearrange("(t p) s -> p t s", p=P)
                if C == 1:
                    sp.dma_start(rest[:, 0], rows(3)).then_inc(params.sem, 16)
                    sp.dma_start(rest[:, 1], rows(0)).then_inc(params.sem, 16)
                merger.load(sp)
                for k, to in enumerate(saves):
                    sp.wait_ge(emptied.sem, emptied.at(k + 1))
                    sp.dma_start(rows(to), (rest[:, 0] if C == 1 else counts2[:]) if k else counts[:]).then_inc(counts_out.sem, 16)
                sp.wait_ge(counts_out.sem, counts_out.at(16 * len(saves)))
        for c in landed:
            c.close(32 * TURNS)
        scored.close(ET), scattered.close(16 * ET), copied.close(TURNS), far.close(2 * C * ET)
        to_ready.close(C * ET), from_ready.close(C * ET), hots_used.close(C * ET), counted.close(C), emptied.close(2)
        counts_out.close(16 * len(saves)), merger.close()
        if heads > 1:
            m.c["zeros_out"].close(16 * m.clearing)
        if C == 1:
            params.close(32)


def attend(nc, m, relations, heads, width, values, out, grid=None, broad=None, near=None, logs=()):
    R, Hn = relations, heads
    parts = (width + 511) // 512
    w = width // parts
    load = (m.c["grid_a"], m.c["grid_b"])
    names = ("grid_used", "sum_ready", "sum_used", "max_ready", "probs_ready", "probs_used", "turned", "turned_saved",
             "mixed", "mixed_saved")
    a_ready = m.c["last_sum_ready"]
    g_used, s_ready, s_used, x_ready, p_ready, p_used, t_ready, t_saved, o_ready, o_saved = (m.c[k] for k in names)
    with ExitStack() as ctx:
        sb = scratch(nc, m, ctx)
        log = sb("log_t", [P, 2, R, NP], F32)
        cells = sb("cells", [P, 2, NP, Hn], F32) if grid is not None else None
        total = sb("sum_t", [P, 2, R, NP], F32)
        score = sb("score_t", [P, 2, R, NP], F32)
        top = sb("top", [P, 2, R + 2], F32)
        probs = sb("probs", [P, 2, R, NP], F32)
        mass = sb("mass", [P, 4, R], F32)
        share = sb("share", [P, 2, 2], F32)
        turned = sb("turned_t", [P, 2, R, NP], F32)
        with nc.Block() as block:
            @block.sync
            def _(sp):
                for t in range(T):
                    if t >= 2:
                        sp.wait_ge(g_used.sem, g_used.at(t - 1))
                    c = load[t % 2]
                    rows = slice(t * P, (t + 1) * P)
                    for r in range(R):
                        sp.dma_start(log[:, t % 2, r], m.logs[logs[r]][rows]).then_inc(c.sem, 16)
                    if grid is not None:
                        sp.dma_start(cells[:, t % 2], grid.rearrange("(d s) h -> d s h", s=NP)[rows]).then_inc(c.sem, 16)

            pool_part = R if R == 1 else R - 1
            if grid is None:
                @block.gpsimd
                def _(pool):
                    for t in range(T):
                        for h in range(Hn):
                            u = t * Hn + h
                            if u >= 2:
                                pool.wait_ge(s_used.sem, s_used.at(u - 1))
                            for r in range(pool_part):
                                ins = nc.gpsimd.tensor_scalar(total[:, u % 2, r], broad[:, r * Hn + h],
                                                              near[:, t, r * Hn + h:r * Hn + h + 1], None, ALU.add)
                            ins.then_inc(s_ready.sem, 1)

            @block.vector
            def _(dve):
                steps = Steps(dve, m.c["dve_step"])

                def scores(t, h):
                    u = t * Hn + h
                    s = u % 2
                    if h == 0:
                        n = (R + (grid is not None)) * 16 * (t // 2 + 1)
                        dve.wait_ge(load[t % 2].sem, load[t % 2].at(n))
                    if u >= 2:
                        dve.wait_ge(p_ready.sem, p_ready.at(u - 1))
                    if grid is None:
                        dve.wait_ge(s_ready.sem, s_ready.at(u + 1))
                        if pool_part < R:
                            dve.wait_ge(a_ready.sem, a_ready.at(u + 1))
                        for r in range(R):
                            ins = nc.vector.scalar_tensor_tensor(total[:, s, r], total[:, s, r], 0.2, total[:, s, r], ALU.mult, ALU.max)
                        steps.then(ins)
                    for r in range(R):
                        part = cells[:, t % 2, :, h] if grid is not None else total[:, s, r]
                        ins = nc.vector.tensor_tensor_reduce(out=score[:, s, r], in0=part, in1=log[:, t % 2, r], scale=1.0,
                                                             scalar=FLOOR, op0=ALU.add, op1=ALU.max,
                                                             accum_out=top[:, s, r:r + 1])
                    steps.then(ins)
                    if grid is None:
                        dve.sem_inc(s_used.sem, 1)
                    if h == Hn - 1:
                        dve.sem_inc(g_used.sem, 1)
                    if R > 1:
                        steps.then(nc.vector.tensor_reduce(top[:, s, R:R + 1], top[:, s, 0:R], AX_X, ALU.max))
                    last = top[:, s, R:R + 1] if R > 1 else top[:, s, 0:1]
                    nc.vector.tensor_scalar(top[:, s, R + 1:R + 2], last, -1.0, None, ALU.mult).then_inc(x_ready.sem, 1)

                def save(t, h):
                    u = t * Hn + h
                    s = u % 2
                    dve.wait_ge(p_ready.sem, p_ready.at(u + 1))
                    if R > 1:
                        steps.then(nc.vector.tensor_reduce(share[:, s, 0:1], mass[:, u % 4, :], AX_X, ALU.add))
                        steps.then(nc.vector.tensor_scalar(share[:, s, 0:1], share[:, s, 0:1], 1e-16, None, ALU.add))
                    else:
                        steps.then(nc.vector.tensor_scalar(share[:, s, 0:1], mass[:, u % 4, 0:1], 1e-16, None, ALU.add))
                    steps.then(nc.vector.reciprocal(share[:, s, 1:2], share[:, s, 0:1]))
                    dve.wait_ge(o_ready.sem, o_ready.at(u + 1))
                    if parts == 1:
                        src, dst = m.psum[:, 4 + 2 * s, 0:w], out[:, t, h * w:(h + 1) * w]
                    else:
                        src = m.psum[:, 4 + 2 * s:6 + 2 * s, 0:w]
                        dst = out[:, t, 0:width].rearrange("p (c w) -> p c w", c=parts)
                    nc.vector.tensor_scalar(dst, src, share[:, s, 1:2], None, ALU.mult).then_inc(o_saved.sem, 1)

                units = [(t, h) for t in range(T) for h in range(Hn)]
                LAG = 3
                for n, unit in enumerate(units):
                    scores(*unit)
                    if n >= LAG:
                        save(*units[n - LAG])
                for unit in units[-LAG:]:
                    save(*unit)
                steps.done()

            @block.scalar
            def _(act):
                def last_sum(u):
                    t, h = divmod(u, Hn)
                    if u >= 2:
                        act.wait_ge(s_used.sem, s_used.at(u - 1))
                    r = R - 1
                    nc.scalar.activation(total[:, u % 2, r], broad[:, r * Hn + h], ACT.Identity,
                                         bias=near[:, t, r * Hn + h:r * Hn + h + 1]).then_inc(a_ready.sem, 1)

                def exponents(u):
                    s = u % 2
                    act.wait_ge(x_ready.sem, x_ready.at(u + 1))
                    if u >= 2:
                        act.wait_ge(p_used.sem, p_used.at(u - 1))
                    if u >= 4:
                        act.wait_ge(o_saved.sem, o_saved.at(u - 3))
                    for r in range(R):
                        ins = nc.scalar.activation(probs[:, s, r], score[:, s, r], ACT.Exp, bias=top[:, s, R + 1:R + 2],
                                                   accum_out=mass[:, u % 4, r:r + 1])
                    ins.then_inc(p_ready.sem, 1)

                def save_turned_probs(u):
                    if u >= 2:
                        act.wait_ge(o_ready.sem, o_ready.at(u - 1))
                    for r in range(R):
                        v = u * R + r
                        act.wait_ge(t_ready.sem, t_ready.at(v + 1))
                        b = 2 * (v % 2)
                        nc.scalar.activation(turned[:, u % 2, r, 0:512], m.psum[:, b, :], ACT.Copy)
                        nc.scalar.activation(turned[:, u % 2, r, 512:NP], m.psum[:, b + 1, 0:P], ACT.Copy).then_inc(t_saved.sem, 1)

                lag = 1 if R == 1 else 0
                if pool_part < R:
                    last_sum(0)
                for u in range(T * Hn):
                    if pool_part < R and u + 1 < T * Hn:
                        last_sum(u + 1)
                    exponents(u)
                    if u >= lag:
                        save_turned_probs(u - lag)
                if lag:
                    save_turned_probs(T * Hn - 1)

            @block.tensor
            def _(pe):
                def turn(u):
                    pe.wait_ge(p_ready.sem, p_ready.at(u + 1))
                    for r in range(R):
                        v = u * R + r
                        if v >= 2:
                            pe.wait_ge(t_saved.sem, t_saved.at(v - 1))
                        for c in range(T):
                            b = 2 * (v % 2) + c // 4
                            ins = nc.tensor.transpose(m.psum[:, b, (c % 4) * P:(c % 4 + 1) * P], probs[:, u % 2, r, c * P:(c + 1) * P],
                                                      m.ident[:])
                        ins.then_inc(t_ready.sem, 1)
                    pe.wait_ge(t_ready.sem, t_ready.at((u + 1) * R))
                    pe.sem_inc(p_used.sem, 1)

                def mix(u):
                    h = u % Hn
                    if u >= 2:
                        pe.wait_ge(o_saved.sem, o_saved.at(u - 1))
                    pe.wait_ge(t_saved.sem, t_saved.at((u + 1) * R))
                    for c in range(parts):
                        for r in range(R):
                            for k in range(T):
                                ins = nc.tensor.matmul(m.psum[:, 4 + 2 * (u % 2) + c, 0:w], turned[:, u % 2, r, k * P:(k + 1) * P],
                                                       values[r][:, k, h * width + c * w:h * width + (c + 1) * w],
                                                       start=(r == 0 and k == 0), stop=(r == R - 1 and k == T - 1))
                    ins.then_inc(o_ready.sem, 1)

                for u in range(T * Hn):
                    turn(u)
                    if u:
                        mix(u - 1)
                mix(T * Hn - 1)
        U = T * Hn
        per = (R + (grid is not None)) * 16
        load[0].close(per * ((T + 1) // 2)), load[1].close(per * (T // 2))
        g_used.close(T), x_ready.close(U), p_ready.close(U), p_used.close(U), t_ready.close(U * R), t_saved.close(U * R)
        o_ready.close(U), o_saved.close(U)
        if grid is None:
            s_ready.close(U), s_used.close(U)
            if R > 1:
                a_ready.close(U)


def elu_rows(nc, m, rows, bias=None, plus=None, turned=None, ahead=None):
    e_ready, e_done, params, ready = (m.c[k] for k in ("elu_ready", "elu_done", "params", "rows_ready"))
    with ExitStack() as ctx:
        sb = scratch(nc, m, ctx)
        low = sb("low_part", [P, T, D], F32)
        row = sb("row", [P, D], F32)
        with nc.Block() as block:
            @block.sync
            def _(sp):
                if bias is not None:
                    sp.dma_start(row[:], bias.partition_broadcast(P)).then_inc(params.sem, 16)
                if ahead is not None:
                    ahead.start(sp)

            @block.vector
            def _(dve):
                steps = Steps(dve, m.c["dve_step"])
                if bias is not None:
                    dve.wait_ge(params.sem, params.at(16))
                    for t in range(T):
                        ins = nc.vector.tensor_tensor(rows[:, t, 0:D], rows[:, t, 0:D], row[:], ALU.add)
                    steps.then(ins)
                for t in range(T):
                    nc.vector.tensor_scalar(low[:, t], rows[:, t, 0:D], 0.0, None, ALU.min).then_inc(e_ready.sem, 1)
                for t in range(T):
                    dve.wait_ge(e_done.sem, e_done.at(t + 1))
                    ins = nc.vector.scalar_tensor_tensor(rows[:, t, 0:D], low[:, t], -1.0, rows[:, t, 0:D], ALU.add, ALU.max)
                    if plus is not None:
                        steps.then(ins)
                        steps.then(nc.vector.tensor_tensor(rows[:, t, 0:D], rows[:, t, 0:D], plus[:, t], ALU.add))
                    if turned is not None:
                        ins.then_inc(ready.sem, 1)
                steps.done()

            @block.scalar
            def _(act):
                for t in range(T):
                    act.wait_ge(e_ready.sem, e_ready.at(t + 1))
                    nc.scalar.activation(low[:, t], low[:, t], ACT.Exp, bias=m.zero[:]).then_inc(e_done.sem, 1)
                if turned is not None:
                    save_turned(nc, m, act, turned)

            if turned is not None:
                @block.tensor
                def _(pe):
                    turn_rows(nc, m, pe, rows)
        e_ready.close(T), e_done.close(T)
        if turned is not None:
            ready.close(T), close_turn(m, 1)
        if bias is not None:
            params.close(16)


def gat_v2_block(nc, m, g):
    with ExitStack() as ctx:
        sb = scratch(nc, m, ctx)
        out = sb("out_rows", [P, T, D], F32)

        def before(projection):
            if projection.jobs[0].rows.shape[2] == D + 8:
                normalise(nc, m, m.X, m.H, m.eps5, turned=m.HT, ahead=projection, clear=True)
            else:
                elu_rows(nc, m, out, plus=m.H)
                normalise(nc, m, out, m.H, m.eps5, g["L0_gnn_ln1_w"], g["L0_gnn_ln1_b"], turned=m.HT, ahead=projection)

        for layer, (heads, names) in enumerate(((8, ("W1s", "b1s", "W1d", "b1d", "attn1")), (1, ("Wos", "bos", "Wod", "bod", "attno")))):
            attn = g["L0_gnn_" + names[4]]
            with ExitStack() as inner:
                sb1 = scratch(nc, m, inner)
                fs = sb1("fs", [P, T, D + heads], F32)
                coef = sb1("attn_row", [P, D], F32)
                loads = ((coef[:], attn.rearrange("h c -> (h c)").partition_broadcast(P)),)
                with ExitStack() as products:
                    sb2 = scratch(nc, m, products)
                    fd = sb2("fd", [P, T, D + heads], F32)
                    jobs = [Job(g["L0_gnn_" + w], rows, bias=g["L0_gnn_" + b], merged=m.merged["L0_2"][:, k] if layer else None, vector=coef, heads=heads,
                                scores=lambda t, rows=rows: rows[:, t, D:D + heads], bias_by=coef, to_dram=dram)
                            for k, (w, b, rows, dram) in enumerate(((names[0], names[1], fs, m.from_dram[heads]), (names[2], names[3], fd, m.to_dram[heads])))]
                    projection = Projection(nc, m, sb2, jobs, loads)
                    before(projection)
                    projection.run(m.HT)
                grid = m.grid if heads == 8 else m.grid1
                passes, saves = ((0, 1), (3, 0)) if layer == 0 else ((2,), (1, 2))
                edge_scores(nc, m, coef, heads, grid, passes, saves, score_vectors(g, f"edges_{layer + 1}"))
                if layer == 0:
                    log_counts(nc, m, 3)
                attend(nc, m, 1, heads, D // heads, [fs], out, grid=grid, logs=(3,))
        elu_rows(nc, m, out)
        normalise(nc, m, out, m.H, m.eps5, g["L0_gnn_lno_w"], g["L0_gnn_lno_b"], onto=m.X)


def first_largest(nc, steps, values, work, top, chosen, rank):
    n = values.shape[2]
    shape = [P, T, n]
    ranks = rank[:, 0:n].unsqueeze(1).to_broadcast(shape)
    steps.then(nc.vector.tensor_reduce(top[:, :, 0], values, AX_X, ALU.max))
    steps.then(nc.vector.tensor_tensor(work, values, top[:, :, 0:1].to_broadcast(shape), ALU.is_lt))
    steps.then(nc.vector.scalar_tensor_tensor(work, work, float(n), ranks, ALU.mult, ALU.add))
    steps.then(nc.vector.tensor_reduce(top[:, :, 1], work, AX_X, ALU.min))
    steps.then(nc.vector.tensor_tensor(chosen, ranks, top[:, :, 1:2].to_broadcast(shape), ALU.is_equal))


def switch_block(nc, m, g):
    E, F, CAP = 16, 96, 64
    normalise(nc, m, m.X, m.H, m.eps5)
    with ExitStack() as ctx:
        sb = scratch(nc, m, ctx)
        N = sb("normed", [P, T, D], F32)
        logits = sb("logits", [P, T, E], F32)
        chance = sb("chance", [P, T], F32)
        passed = sb("passed", [P, T], F32)
        send = sb("send", [P, T], U32)
        fetch = sb("fetch", [P, T], U32)
        wi = sb("wi", [P, KD, E * F], F32)
        wo = sb("wo", [F, E, D], F32)
        router = Projection(nc, m, sb, [Job(g["L0_ffn_w_router"], logits)])
        params, v_ready, d_ready, ready = (m.c[k] for k in ("params", "variance_ready", "deviation_ready", "rows_ready"))
        with ExitStack() as inner:
            sb2 = scratch(nc, m, inner)
            row = sb2("ln_w", [P, D], F32)
            square = sb2("square", [P, T], F32)
            dev = sb2("dev", [P, T], F32)
            junk = sb2("junk", [P, D], F32)
            with nc.Block() as block:
                @block.sync
                def _(sp):
                    sp.dma_start(row[:], g["L0_ffn_ln_w"].partition_broadcast(P)).then_inc(params.sem, 16)
                    router.start(sp)
                    sp.dma_start(wi[:], g["L0_ffn_wi"].rearrange("(k p) f -> p k f", p=P)).then_inc(m.c["streamed_a"].sem, 16)
                    sp.dma_start(wo[:], g["L0_ffn_wo"].rearrange("e f d -> f e d")).then_inc(m.c["streamed_b"].sem, 16)

                @block.vector
                def _(dve):
                    steps = Steps(dve, m.c["dve_step"])
                    for t in range(T):
                        steps.then(nc.vector.tensor_tensor_reduce(out=junk[:], in0=m.H[:, t], in1=m.H[:, t], scale=1.0, scalar=0.0,
                                                                  op0=ALU.mult, op1=ALU.add, accum_out=square[:, t:t + 1]))
                    dve.sem_inc(v_ready.sem, 1)
                    dve.wait_ge(d_ready.sem, d_ready.at(1))
                    steps.then(nc.vector.reciprocal(dev[:], dev[:]))
                    dve.wait_ge(params.sem, params.at(16))
                    for t in range(T):
                        nc.vector.scalar_tensor_tensor(N[:, t], m.H[:, t], dev[:, t:t + 1], row[:], ALU.mult, ALU.mult).then_inc(ready.sem, 1)
                    steps.done()

                @block.tensor
                def _(pe):
                    turn_rows(nc, m, pe, N)

                @block.scalar
                def _(act):
                    act.wait_ge(v_ready.sem, v_ready.at(1))
                    nc.scalar.activation(dev[:], square[:], ACT.Sqrt, bias=m.eps6[:], scale=1.0 / D).then_inc(d_ready.sem, 1)
                    save_turned(nc, m, act, m.HT)
            params.close(16), v_ready.close(1), d_ready.close(1), ready.close(T), close_turn(m, 1)
        router.run(m.HT)
        with ExitStack() as inner:
            sb2 = scratch(nc, m, inner)
            work, chosen, power, kept, place = (sb2(k, [P, T, E], F32) for k in ("work", "chosen", "power", "kept", "place"))
            start = sb2("start", [P, E], F32)
            node = sb2("node", [P, T], F32)
            slot = sb2("slot", [P, T], F32)
            top = sb2("top", [P, T, 2], F32)
            e_ready, e_done, o_ready = m.c["elu_ready"], m.c["elu_done"], m.c["mixed"]
            with nc.Block() as block:
                @block.vector
                def _(dve):
                    steps = Steps(dve, m.c["dve_step"])
                    do = steps.then
                    first_largest(nc, steps, logits[:], work[:], top, chosen[:], m.rank)
                    dve.sem_inc(ready.sem, 1)
                    do(nc.vector.tensor_tensor(power[:], logits[:], top[:, :, 0:1].to_broadcast([P, T, E]), ALU.subtract))
                    dve.sem_inc(e_ready.sem, 1)
                    nc.vector.tensor_scalar(start[:], m.rank[:, 0:E], float(CAP), -1.0, ALU.mult, ALU.add)
                    for t in range(T):
                        ins = nc.vector.tensor_scalar(node[:, t:t + 1], m.part[:], float(t * P), None, ALU.add)
                    do(ins)
                    dve.wait_ge(o_ready.sem, o_ready.at(1))
                    nth = m.psum[:, 0, 0:T * E].rearrange("p (t e) -> p t e", t=T)
                    nc.vector.scalar_tensor_tensor(kept[:], nth, float(CAP), chosen[:], ALU.is_le, ALU.mult)
                    do(nc.vector.tensor_tensor(place[:], nth, start[:].unsqueeze(1).to_broadcast([P, T, E]), ALU.add))
                    do(nc.vector.tensor_reduce(passed[:], kept[:], AX_X, ALU.add))
                    nc.vector.tensor_tensor(place[:], place[:], kept[:], ALU.mult)
                    do(nc.vector.tensor_scalar(passed[:], passed[:], -1.0, 1.0, ALU.mult, ALU.add))
                    do(nc.vector.tensor_reduce(slot[:], place[:], AX_X, ALU.add))
                    nc.vector.tensor_copy(fetch[:], slot[:])
                    do(nc.vector.tensor_scalar(node[:], node[:], float(E * CAP), None, ALU.add))
                    do(nc.vector.tensor_tensor(node[:], node[:], passed[:], ALU.mult))
                    do(nc.vector.tensor_tensor(send[:], slot[:], node[:], ALU.add))
                    dve.wait_ge(e_done.sem, e_done.at(1))
                    do(nc.vector.tensor_reduce(chance[:], power[:], AX_X, ALU.add))
                    do(nc.vector.reciprocal(chance[:], chance[:]))
                    steps.done()

                @block.scalar
                def _(act):
                    act.wait_ge(e_ready.sem, e_ready.at(1))
                    nc.scalar.activation(power[:], power[:], ACT.Exp, bias=m.zero[:]).then_inc(e_done.sem, 1)

                @block.tensor
                def _(pe):
                    pe.wait_ge(ready.sem, ready.at(1))
                    for t in range(T):
                        for k in range(t + 1):
                            ins = nc.tensor.matmul(m.psum[:, 0, t * E:(t + 1) * E], m.after[:] if k == t else m.ones[:],
                                                   chosen[:, k], start=(k == 0), stop=(k == t))
                    ins.then_inc(o_ready.sem, 1)
            ready.close(1), e_ready.close(1), e_done.close(1), o_ready.close(1)
        switch_experts(nc, m, N, chance, passed, send, fetch, wi, wo, E, F, CAP)


def switch_experts(nc, m, N, chance, passed, send, fetch, wi, wo, E, F, CAP):
    assert 2 * CAP == P
    Q = E // 2
    load_in, load_out, sent, fetched = (m.c[k] for k in ("streamed_a", "streamed_b", "sent", "fetched"))
    x_in = (m.c["rows_loaded"], m.c["rows_loaded_b"])
    y_out = (m.c["made_out"], m.c["made_out_b"])
    names = ("copied", "turned", "turned_saved", "hidden_ready", "hidden_done", "second_ready", "second_done", "rows_ready")
    all_sent, x_turned, x_saved, h_ready, h_done, y_ready, y_saved, got_ready = (m.c[k] for k in names)
    with ExitStack() as ctx:
        sb = scratch(nc, m, ctx)
        rows = sb("rows", [P, 2, D], F32)
        columns = sb("columns", [P, 2, KD, P], F32)
        hidden = sb("hidden", [F, E, P], F32)
        made = sb("made_rows", [P, 2, D], F32)
        got = sb("got", [P, T, D], F32)
        weight = sb("weight", [P, 2, T], F32)
        two = lambda v: v.rearrange("p (c n) -> p c n", c=2)
        with nc.Block() as block:
            @block.gpsimd
            def _(pool):
                for t in range(T):
                    nc.gpsimd.indirect_dma_start(
                        out=m.tokens, out_offset=bass.IndirectOffsetOnAxis(ap=send[:, t:t + 1], axis=0),
                        in_=N[:, t], in_offset=None).then_inc(sent.sem, 16)
                pool.wait_ge(sent.sem, sent.at(16 * T))
                pool.sem_inc(all_sent.sem, 1)
                for q in range(Q):
                    pool.wait_ge(y_saved.sem, y_saved.at(q + 1))
                    pool.sem_inc(m.c["waited"].sem, 1)
                    pool.dma_start(m.made[q * P:(q + 1) * P], made[:, q % 2]).then_inc(y_out[q % 2].sem, 16)
                for slot in y_out:
                    pool.wait_ge(slot.sem, slot.at(16 * Q // 2))
                pool.sem_inc(m.c["waited"].sem, 1)
                for t in range(T):
                    nc.gpsimd.indirect_dma_start(
                        out=got[:, t], out_offset=None, in_=m.made[0:E * CAP],
                        in_offset=bass.IndirectOffsetOnAxis(ap=fetch[:, t:t + 1], axis=0)).then_inc(fetched.sem, 16)
                pool.wait_ge(fetched.sem, fetched.at(16 * T))
                pool.sem_inc(got_ready.sem, 1)

            @block.sync
            def _(sp):
                sp.wait_ge(all_sent.sem, all_sent.at(1))
                for q in range(Q):
                    if q >= 2:
                        sp.wait_ge(x_turned.sem, x_turned.at(q - 1))
                    sp.dma_start(rows[:, q % 2], m.tokens[q * P:(q + 1) * P]).then_inc(x_in[q % 2].sem, 16)

            @block.tensor
            def _(pe):
                def turn(q):
                    pe.wait_ge(x_in[q % 2].sem, x_in[q % 2].at(16 * (q // 2 + 1)))
                    if q:
                        pe.wait_ge(x_saved.sem, x_saved.at(q))
                    for k in range(KD):
                        ins = nc.tensor.transpose(m.psum[:, k // 3, (k % 3) * P:(k % 3 + 1) * P], rows[:, q % 2, k * P:(k + 1) * P], m.ident[:])
                    ins.then_inc(x_turned.sem, 1)

                def first(q):
                    pe.wait_ge(x_saved.sem, x_saved.at(q + 1))
                    if q:
                        pe.wait_ge(h_done.sem, h_done.at(q))
                    for side in range(2):
                        e = 2 * q + side
                        own = slice(side * CAP, (side + 1) * CAP)
                        for k in range(KD):
                            ins = nc.tensor.matmul(m.psum[0:F, 2 + side, own], wi[:, k, e * F:(e + 1) * F], columns[:, q % 2, k, own],
                                                   start=(k == 0), stop=(k == KD - 1))
                    ins.then_inc(h_ready.sem, 1)

                def second(q):
                    pe.wait_ge(h_done.sem, h_done.at(q + 1))
                    if q >= 2:
                        pe.wait_ge(y_saved.sem, y_saved.at(q - 1))
                    for c in range(2):
                        for side in range(2):
                            e = 2 * q + side
                            ins = nc.tensor.matmul(m.psum[:, 4 + 2 * (q % 2) + c, 0:384], hidden[:, e], wo[:, e, c * 384:(c + 1) * 384],
                                                   start=(side == 0), stop=(side == 1))
                    ins.then_inc(y_ready.sem, 1)

                turn(0)
                pe.wait_ge(load_in.sem, load_in.at(16))
                for q in range(Q):
                    if q + 1 < Q:
                        turn(q + 1)
                    first(q)
                    if q == 1:
                        pe.wait_ge(load_out.sem, load_out.at(16))
                    if q:
                        second(q - 1)
                second(Q - 1)

            @block.scalar
            def _(act):
                act.wait_ge(m.c["cleared"].sem, m.c["cleared"].at(1))
                for q in range(Q):
                    act.wait_ge(h_ready.sem, h_ready.at(q + 1))
                    for side in range(2):
                        own = slice(side * CAP, (side + 1) * CAP)
                        ins = nc.scalar.activation(hidden[:, 2 * q + side, own], m.psum[0:F, 2 + side, own], ACT.Relu)
                    ins.then_inc(h_done.sem, 1)

            @block.vector
            def _(dve):
                steps = Steps(dve, m.c["dve_step"])

                def save_columns(q):
                    dve.wait_ge(x_turned.sem, x_turned.at(q + 1))
                    if q >= 2:
                        dve.wait_ge(h_ready.sem, h_ready.at(q - 1))
                    nc.vector.tensor_copy(columns[:, q % 2].rearrange("p (c k) n -> p c (k n)", c=2), m.psum[:, 0:2, 0:384]).then_inc(x_saved.sem, 1)

                def save_made(q):
                    dve.wait_ge(y_ready.sem, y_ready.at(q + 1))
                    if q >= 2:
                        dve.wait_ge(y_out[q % 2].sem, y_out[q % 2].at(16 * (q // 2)))
                    b = 4 + 2 * (q % 2)
                    nc.vector.tensor_copy(two(made[:, q % 2]), m.psum[:, b:b + 2, 0:384]).then_inc(y_saved.sem, 1)

                nc.vector.memset(hidden[:], 0.0).then_inc(m.c["cleared"].sem, 1)
                steps.then(nc.vector.tensor_tensor(weight[:, 0], chance[:], passed[:], ALU.mult))
                steps.then(nc.vector.tensor_tensor(weight[:, 1], chance[:], weight[:, 0], ALU.subtract))
                for t in range(T):
                    ins = nc.vector.tensor_tensor(m.X[:, t], m.X[:, t], m.H[:, t], ALU.add)
                steps.then(ins)
                for t in range(T):
                    ins = nc.vector.scalar_tensor_tensor(m.X[:, t], N[:, t], weight[:, 0, t:t + 1], m.X[:, t], ALU.mult, ALU.add)
                steps.then(ins)
                save_columns(0)
                for q in range(Q):
                    if q + 1 < Q:
                        save_columns(q + 1)
                    if q:
                        save_made(q - 1)
                save_made(Q - 1)
                dve.wait_ge(got_ready.sem, got_ready.at(1))
                for t in range(T):
                    ins = nc.vector.scalar_tensor_tensor(m.X[:, t], got[:, t], weight[:, 1, t:t + 1], m.X[:, t], ALU.mult, ALU.add)
                steps.then(ins)
                steps.done()
        load_in.close(16), load_out.close(16), sent.close(16 * T), fetched.close(16 * T), m.c["cleared"].close(1)
        for slot in x_in + y_out:
            slot.close(16 * Q // 2)
        all_sent.close(1), got_ready.close(1)
        for c in (x_turned, x_saved, h_ready, h_done, y_ready, y_saved):
            c.close(Q)


def spread(nc, m, rows, n, broad):
    total = rows.shape[2]
    t_ready, t_saved, o_ready, o_saved, ready = (m.c[k] for k in ("turned", "turned_saved", "mixed", "mixed_saved", "rows_ready"))
    with ExitStack() as ctx:
        sb = scratch(nc, m, ctx)
        pick = sb("pick", [total, n, P], F32)
        turned = sb("turned_s", [total, NP], F32)
        with nc.Block() as block:
            @block.vector
            def _(dve):
                nc.vector.tensor_copy(pick[:], m.ident[0:total, 0:n].unsqueeze(2).to_broadcast([total, n, P])).then_inc(ready.sem, 1)

            @block.tensor
            def _(pe):
                for t in range(T):
                    ins = nc.tensor.transpose(m.psum[0:total, t // 4, (t % 4) * P:(t % 4 + 1) * P], rows[:, t], m.ident[:])
                ins.then_inc(t_ready.sem, 1)
                pe.wait_ge(ready.sem, ready.at(1))
                pe.wait_ge(t_saved.sem, t_saved.at(1))
                for j in range(n):
                    if j >= 2:
                        pe.wait_ge(o_saved.sem, o_saved.at(j - 1))
                    for c in range(2):
                        ins = nc.tensor.matmul(m.psum[:, 4 + 2 * (j % 2) + c, 0:HALF], pick[:, j], turned[:, c * HALF:(c + 1) * HALF],
                                               start=True, stop=True)
                    ins.then_inc(o_ready.sem, 1)

            @block.scalar
            def _(act):
                act.wait_ge(t_ready.sem, t_ready.at(1))
                nc.scalar.activation(turned[:, 0:512], m.psum[0:total, 0, :], ACT.Copy)
                nc.scalar.activation(turned[:, 512:NP], m.psum[0:total, 1, 0:P], ACT.Copy).then_inc(t_saved.sem, 1)
                for j in range(n):
                    act.wait_ge(o_ready.sem, o_ready.at(j + 1))
                    b = 4 + 2 * (j % 2)
                    nc.scalar.activation(broad[:, j].rearrange("p (c n) -> p c n", c=2), m.psum[:, b:b + 2, 0:HALF],
                                         ACT.Copy).then_inc(o_saved.sem, 1)
        ready.close(1), t_ready.close(1), t_saved.close(1), o_ready.close(n), o_saved.close(n)


def finish_rows(nc, m, rows, bias, turned=None, relu=False, onto=None, ahead=None):
    width = rows.shape[2]
    params, ready = m.c["params"], m.c["rows_ready"]
    with ExitStack() as ctx:
        sb = scratch(nc, m, ctx)
        row = sb("row", [P, width], F32)
        with nc.Block() as block:
            @block.sync
            def _(sp):
                sp.dma_start(row[:], bias.partition_broadcast(P)).then_inc(params.sem, 16)
                if ahead is not None:
                    ahead.start(sp)

            @block.vector
            def _(dve):
                steps = Steps(dve, m.c["dve_step"])
                dve.wait_ge(params.sem, params.at(16))
                for t in range(T):
                    ins = nc.vector.tensor_tensor(rows[:, t], rows[:, t], row[:], ALU.add)
                    if relu:
                        steps.then(ins)
                        ins = nc.vector.tensor_scalar(rows[:, t], rows[:, t], 0.0, None, ALU.max)
                    if onto is not None:
                        steps.then(ins)
                        ins = nc.vector.tensor_tensor(onto[:, t], onto[:, t], rows[:, t], ALU.add)
                    ins.then_inc(ready.sem, 1)
                steps.done()

            if turned is not None:
                @block.tensor
                def _(pe):
                    turn_rows(nc, m, pe, rows)

                @block.scalar
                def _(act):
                    save_turned(nc, m, act, turned)
        params.close(16), ready.close(T), close_turn(m, 1 if turned is not None else 0)


def gat_block(nc, m, g):
    def scored(layer, sb, values, scores):
        job = Job(g[f"L1_gnn_W{layer}_turned"], values, merged=m.merged[f"L1_{layer}"][:, 0],
                  scores=lambda t: scores[:, t].rearrange("p (n h) -> p h n", n=2), order="p (h n) -> p h n", sizes={"n": 2})
        return Projection(nc, m, sb, [job])

    with ExitStack() as ctx:
        sb = scratch(nc, m, ctx)
        columns = sb("columns", [P, 8, NP], F32)
        out = sb("out", [P, T, 1024], F32)
        with ExitStack() as inner:
            sb1 = scratch(nc, m, inner)
            values = sb1("values", [P, T, 1024], F32)
            scores = sb1("scores", [P, T, 16], F32)
            with ExitStack() as product:
                projection = scored(1, scratch(nc, m, product), values, scores)
                normalise(nc, m, m.X, m.H, m.eps5, turned=m.HT, ahead=projection)
                projection.run(m.HT, LogCounts(nc, m, scratch(nc, m, product), [0, 1, 2]))
            broad = sb1("broad", [P, 8, NP], F32)
            spread(nc, m, scores, 8, broad)
            attend(nc, m, 1, 8, 128, [values], out, broad=broad, near=scores[:, :, 8:16], logs=(3,))
        values = sb("values", [P, T, D], F32)
        scores = sb("scores", [P, T, 2], F32)
        broad = sb("broad", [P, 1, NP], F32)
        with ExitStack() as product:
            projection = scored(2, scratch(nc, m, product), values, scores)
            finish_rows(nc, m, out, g["L1_gnn_b1"], turned=columns, relu=True, ahead=projection)
            projection.run(columns)
        spread(nc, m, scores, 1, broad)
        attend(nc, m, 1, 1, D, [values], m.H, broad=broad, near=scores[:, :, 1:2], logs=(3,))
        finish_rows(nc, m, m.H, g["L1_gnn_b2"], onto=m.X)


def quantise(nc, steps, out, src, factor):
    steps.then(nc.vector.tensor_scalar(out[0], src, factor, -8.0, ALU.mult, ALU.max))
    steps.then(nc.vector.tensor_scalar(out[0], out[0], 7.0, ROUND, ALU.min, ALU.add))
    ins = nc.vector.tensor_scalar(out[1], out[0], -ROUND, None, ALU.add)
    return ins


def quant_block(nc, m, g):
    F = 96
    normalise(nc, m, m.X, m.H, m.eps5)
    with ExitStack() as ctx:
        sb = scratch(nc, m, ctx)
        a1 = sb("a1", [P, D], F32)
        a2 = sb("a2", [P, F], F32)
        aw2 = sb("aw2", [P, D], F32)
        b2 = sb("b2", [P, D], F32)
        aw1c = sb("aw1c", [F, 1], F32)
        b1c = sb("b1c", [F, 1], F32)
        aw2c = sb("aw2c", [P, KD], F32)
        w1 = sb("w1", [F, D], F32)
        w2 = sb("w2", [P, KD, F], F32)
        mean = sb("mean", [P, 4], F32)
        w1q = sb("w1q", [F, D], F32)
        w2q = sb("w2q", [P, KD, F], F32)
        w1T = sb("w1T", [P, KD, F], BF16)
        w2T = sb("w2T", [F, D], BF16)
        xT = sb("xT", [P, KD, NP], BF16)
        hid = sb("hid", [F, NP], F32)
        hq = sb("hq", [F, NP], BF16)
        rest = sb("rest", [P, T, D], F32)
        params, ready, saved, h_ready, h_done, s_ready, s_done = (
            m.c[k] for k in ("params", "rows_ready", "columns_ready", "hidden_ready", "hidden_done", "second_ready", "second_done"))
        q_ready = m.c["sum_ready"]
        w_turned, w_saved = m.c["turned"], m.c["turned_saved"]
        column = lambda a: a.rearrange("(h o) -> h o", o=1)
        with nc.Block() as block:
            @block.sync
            def _(sp):
                loads = [(a1[:], g["L1_ffn_alpha_a1"].partition_broadcast(P)), (a2[:], g["L1_ffn_alpha_a2"].partition_broadcast(P)),
                         (aw2[:], g["L1_ffn_alpha_w2"].partition_broadcast(P)), (b2[:], g["L1_ffn_b2"].partition_broadcast(P)),
                         (aw1c[:], column(g["L1_ffn_alpha_w1"])), (b1c[:], column(g["L1_ffn_b1"])),
                         (w1[:], g["L1_ffn_w1"]), (w2[:], g["L1_ffn_w2"].rearrange("(k p) h -> p k h", p=P))]
                for to, of in loads:
                    sp.dma_start(to, of).then_inc(params.sem, 16)
                with nc.allow_non_contiguous_dma("768 numbers"):
                    sp.dma_start(aw2c[:], g["L1_ffn_alpha_w2"].rearrange("(k p) -> p k", p=P)).then_inc(params.sem, 16)

            @block.vector
            def _(dve):
                steps = Steps(dve, m.c["dve_step"])
                dve.wait_ge(params.sem, params.at(16 * 9))
                nc.vector.tensor_reduce(mean[:, 0:1], a1[:], AX_X, ALU.add)
                steps.then(nc.vector.tensor_reduce(mean[:, 1:2], a2[:], AX_X, ALU.add))
                nc.vector.tensor_scalar(mean[:, 0:1], mean[:, 0:1], 1.0 / D, None, ALU.mult)
                steps.then(nc.vector.tensor_scalar(mean[:, 1:2], mean[:, 1:2], 1.0 / F, None, ALU.mult))
                nc.vector.reciprocal(mean[:, 2:4], mean[:, 0:2])
                nc.vector.reciprocal(aw2c[:], aw2c[:])
                steps.then(nc.vector.reciprocal(w1q[:, 0:1], aw1c[:]))
                steps.then(nc.vector.tensor_scalar(w1[:], w1[:], w1q[:, 0:1], None, ALU.mult))
                steps.then(nc.vector.tensor_tensor(w2[:], w2[:], aw2c[:].unsqueeze(2).to_broadcast([P, KD, F]), ALU.mult))
                steps.then(quantise(nc, steps, (w1q[:], w1q[:]), w1[:], 1.0))
                steps.then(quantise(nc, steps, (w2q[:], w2q[:]), w2[:], 1.0))
                dve.sem_inc(q_ready.sem, 1)
                for t in range(T):
                    quantise(nc, steps, (rest[:, t], rest[:, t]), m.H[:, t], mean[:, 2:3]).then_inc(ready.sem, 1)
                steps.then(nc.vector.tensor_tensor(aw1c[:], aw1c[:], mean[0:F, 0:1], ALU.mult))
                steps.then(nc.vector.tensor_scalar(aw2[:], aw2[:], mean[:, 1:2], None, ALU.mult))
                dve.sem_inc(q_ready.sem, 1)
                dve.wait_ge(h_done.sem, h_done.at(1))
                steps.then(nc.vector.tensor_scalar(hid[:], hid[:], -10.0, 10.0, ALU.max, ALU.min))
                quantise(nc, steps, (hid[:], hq[:]), hid[:], mean[0:F, 3:4]).then_inc(h_done.sem, 1)
                for t in range(T):
                    dve.wait_ge(s_ready.sem, s_ready.at(t + 1))
                    two = lambda r: r.rearrange("p (c w) -> p c w", c=2)
                    b = 4 + 2 * (t % 2)
                    steps.then(nc.vector.tensor_tensor(two(rest[:, t]), m.psum[:, b:b + 2, 0:384], two(aw2[:]), ALU.mult))
                    dve.sem_inc(s_done.sem, 1)
                    steps.then(nc.vector.tensor_tensor(rest[:, t], rest[:, t], b2[:], ALU.add))
                    steps.then(nc.vector.tensor_tensor(m.X[:, t], m.X[:, t], rest[:, t], ALU.add))
                steps.done()

            @block.tensor
            def _(pe):
                pe.wait_ge(q_ready.sem, q_ready.at(1))
                for k in range(KD):
                    nc.tensor.transpose(m.psum[:, 4, k * 96 % 480:k * 96 % 480 + 96] if k < 5 else m.psum[:, 5, 0:96],
                                        w1q[:, k * P:(k + 1) * P], m.ident[0:F, 0:F])
                for k in range(KD):
                    ins = nc.tensor.transpose(m.psum[0:F, 6 + k // 4, (k % 4) * P:(k % 4 + 1) * P], w2q[:, k], m.ident[:])
                ins.then_inc(w_turned.sem, 1)
                turn_rows(nc, m, pe, rest)
                pe.wait_ge(w_saved.sem, w_saved.at(1))
                pe.wait_ge(saved.sem, saved.at(T))
                for c in range(2):
                    for k in range(KD):
                        ins = nc.tensor.matmul(m.psum[0:F, c, 0:HALF], w1T[:, k], xT[:, k, c * HALF:(c + 1) * HALF],
                                               start=(k == 0), stop=(k == KD - 1))
                ins.then_inc(h_ready.sem, 1)
                pe.wait_ge(h_done.sem, h_done.at(2))
                for t in range(T):
                    if t >= 2:
                        pe.wait_ge(s_done.sem, s_done.at(t - 1))
                    for c in range(2):
                        ins = nc.tensor.matmul(m.psum[:, 4 + 2 * (t % 2) + c, 0:384], hq[:, t * P:(t + 1) * P],
                                               w2T[:, c * 384:(c + 1) * 384], start=True, stop=True)
                    ins.then_inc(s_ready.sem, 1)

            @block.scalar
            def _(act):
                act.wait_ge(w_turned.sem, w_turned.at(1))
                nc.scalar.activation(w1T[:, 0:5], m.psum[:, 4, 0:480].rearrange("p (k f) -> p k f", k=5), ACT.Copy)
                nc.scalar.activation(w1T[:, 5], m.psum[:, 5, 0:96], ACT.Copy)
                nc.scalar.activation(w2T[:, 0:512], m.psum[0:F, 6, :], ACT.Copy)
                nc.scalar.activation(w2T[:, 512:D], m.psum[0:F, 7, 0:256], ACT.Copy).then_inc(w_saved.sem, 1)
                save_turned(nc, m, act, xT)
                act.wait_ge(h_ready.sem, h_ready.at(1))
                act.wait_ge(q_ready.sem, q_ready.at(2))
                nc.scalar.activation(hid[:].rearrange("p (c n) -> p c n", c=2), m.psum[0:F, 0:2, 0:HALF], ACT.Gelu,
                                     bias=b1c[:], scale=aw1c[:]).then_inc(h_done.sem, 1)
        params.close(16 * 9), ready.close(T), q_ready.close(2), close_turn(m, 1), w_turned.close(1), w_saved.close(1)
        h_ready.close(1), h_done.close(2), s_ready.close(T), s_done.close(T)


def rgat_block(nc, m, g):
    R = 3
    for layer, heads in ((1, 4), (2, 1)):
        W = g[f"L2_gnn_W{layer}"]
        with ExitStack() as ctx:
            sb = scratch(nc, m, ctx)
            values = [sb(f"values{r}", [P, T, D], F32) for r in range(R)]
            scores = sb("scores", [P, T, 2 * R * heads], F32)
            with ExitStack() as product:
                sb2 = scratch(nc, m, product)
                jobs = [Job(W[r], values[r], merged=m.merged[f"L2_{layer}"][:, r], order="p (n h) -> p n h", sizes={"n": 2},
                            scores=lambda t, r=r: scores[:, t].rearrange("p (n r h) -> p n r h", n=2, r=R)[:, :, r]) for r in range(R)]
                projection = Projection(nc, m, sb2, jobs)
                if layer == 1:
                    normalise(nc, m, m.X, m.H, m.eps5, turned=m.HT, ahead=projection)
                else:
                    elu_rows(nc, m, m.H, bias=g["L2_gnn_b1"], turned=m.HT, ahead=projection)
                projection.run(m.HT)
            broad = sb("broad", [P, R * heads, NP], F32)
            spread(nc, m, scores, R * heads, broad)
            attend(nc, m, R, heads, D // heads, values, m.H, broad=broad, near=scores[:, :, R * heads:], logs=(0, 1, 2))
    finish_rows(nc, m, m.H, g["L2_gnn_b2"], onto=m.X)


def top_two(nc, m, logits, E, eps, gates_dram, ahead):
    rows = E
    e_ready, e_done, ready, t_ready, t_saved, stored = (
        m.c[k] for k in ("elu_ready", "elu_done", "rows_ready", "turned", "turned_saved", "stored"))
    with ExitStack() as ctx:
        sb = scratch(nc, m, ctx)
        shape = [P, T, E]
        work, first, second, prob = (sb(k, shape, F32) for k in ("work", "first", "second", "prob"))
        gates = sb("gates", [P, T, rows], F32)
        gatesT = sb("gatesT", [rows, NP], F32)
        top = sb("top", [P, T, 2], F32)
        share = sb("share", [P, T, 2], F32)
        with nc.Block() as block:
            @block.vector
            def _(dve):
                steps = Steps(dve, m.c["dve_step"])
                steps.then(nc.vector.tensor_reduce(top[:, :, 0], logits[:, :, 0:E], AX_X, ALU.max))
                steps.then(nc.vector.tensor_tensor(prob[:], logits[:, :, 0:E], top[:, :, 0:1].to_broadcast(shape), ALU.subtract))
                dve.sem_inc(e_ready.sem, 1)
                dve.wait_ge(e_done.sem, e_done.at(1))
                steps.then(nc.vector.tensor_reduce(share[:, :, 0], prob[:], AX_X, ALU.add))
                steps.then(nc.vector.reciprocal(share[:, :, 1], share[:, :, 0]))
                steps.then(nc.vector.tensor_tensor(prob[:], prob[:], share[:, :, 1:2].to_broadcast(shape), ALU.mult))
                first_largest(nc, steps, prob[:], work[:], top, first[:], m.rank)
                steps.then(nc.vector.scalar_tensor_tensor(second[:], first[:], -2.0, prob[:], ALU.mult, ALU.add))
                first_largest(nc, steps, second[:], work[:], top, second[:], m.rank)
                steps.then(nc.vector.tensor_tensor(first[:], first[:], second[:], ALU.add))
                steps.then(nc.vector.tensor_tensor(prob[:], prob[:], first[:], ALU.mult))
                steps.then(nc.vector.tensor_reduce(share[:, :, 0], prob[:], AX_X, ALU.add))
                steps.then(nc.vector.tensor_scalar(share[:, :, 0], share[:, :, 0], eps, None, ALU.add))
                steps.then(nc.vector.reciprocal(share[:, :, 1], share[:, :, 0]))
                steps.then(nc.vector.tensor_tensor(gates[:, :, 0:E], prob[:], share[:, :, 1:2].to_broadcast(shape), ALU.mult))
                dve.sem_inc(ready.sem, 1)
                steps.done()

            @block.scalar
            def _(act):
                act.wait_ge(e_ready.sem, e_ready.at(1))
                nc.scalar.activation(prob[:], prob[:], ACT.Exp, bias=m.zero[:]).then_inc(e_done.sem, 1)
                act.wait_ge(t_ready.sem, t_ready.at(1))
                nc.scalar.activation(gatesT[:, 0:512], m.psum[0:rows, 0, :], ACT.Copy)
                nc.scalar.activation(gatesT[:, 512:NP], m.psum[0:rows, 1, 0:P], ACT.Copy).then_inc(t_saved.sem, 1)

            @block.tensor
            def _(pe):
                pe.wait_ge(ready.sem, ready.at(1))
                for t in range(T):
                    ins = nc.tensor.transpose(m.psum[0:rows, t // 4, (t % 4) * P:(t % 4 + 1) * P], gates[:, t], m.ident[:])
                ins.then_inc(t_ready.sem, 1)

            @block.sync
            def _(sp):
                ahead(sp)
                sp.wait_ge(t_saved.sem, t_saved.at(1))
                sp.dma_start(gates_dram, gatesT[:]).then_inc(stored.sem, 16)
                sp.wait_ge(stored.sem, stored.at(16))
        e_ready.close(1), e_done.close(1), ready.close(1), t_ready.close(1), t_saved.close(1), stored.close(16)


def deep_experts_block(nc, m, g):
    E, HID = 32, 64
    PAIRS = E // 2
    gates_dram = m.gates32
    with ExitStack() as ctx:
        sb = scratch(nc, m, ctx)
        w1 = sb("w1", [P, 2, KD, P], F32)
        w2 = sb("w2", [P, 2, P], F32)
        w3 = sb("w3", [P, 2, 2, 2, HID + 1], F32)
        wl = sb("wl", [P, 2, 2, 2, D], F32)
        load = (m.c["streamed_a"], m.c["streamed_b"])
        row_out = m.c["bias_out"]
        used, f_ready, f_done, s_ready, s_done, g_done, m_ready, m_done, cleared = (
            m.c[k] for k in ("stream_used", "hidden_ready", "hidden_done", "second_ready", "second_done", "hidden_used", "mixed",
                             "mixed_saved", "cleared"))
        gates_in = (m.c["gate_rows_a"], m.c["gate_rows_b"])
        LOADS = 5

        def load_large(sp, p, s):
            for to, name in ((w1[:, s].rearrange("p k f -> p (k f)"), "W1"), (w3[:, s].rearrange("p e k f -> p (e k f)"), "W3"),
                             (wl[:, s].rearrange("p e k f -> p (e k f)"), "Wl")):
                sp.dma_start(to, g["L2_ffn_" + name][bass.ds(p, 1)].rearrange("o p f -> (o p) f")).then_inc(load[s].sem, 16)

        def load_small(sp, p, s):
            for h in range(2):
                half = slice(h * HID, (h + 1) * HID)
                sp.dma_start(w2[half, s, half], g["L2_ffn_W2"][bass.ds(p, 1), half].rearrange("o p f -> (o p) f")).then_inc(load[s].sem, 16)
                sp.dma_start(gate[half, s], gates_dram[bass.ds(2 * p + h, 1)].to_broadcast([HID, NP])).then_inc(gates_in[s].sem, 16)

        def first_pairs(sp):
            load_large(sp, 0, 0)
            load_large(sp, 1, 1)

        with ExitStack() as routing:
            sb2 = scratch(nc, m, routing)
            logits = sb2("logits", [P, T, E], F32)
            router = Projection(nc, m, sb2, [Job(g["L2_ffn_gate_w"], logits)])
            normalise(nc, m, m.X, m.H, m.eps5, turned=m.HT, ahead=router)
            router.run(m.HT)
            top_two(nc, m, logits, E, 1e-20, gates_dram, first_pairs)

        gated = sb("gated", [P, PAIRS, NP], F32)
        merged = sb("merged", [P, PAIRS, D], F32)
        bias = sb("bias", [E, D], F32)
        bl = sb("bl", [E, D], F32)
        gatesT = sb("gatesT", [E, NP], F32)
        params = m.c["params"]
        with ExitStack() as inner:
            sb1 = scratch(nc, m, inner)
            gate = sb1("gate", [P, 2, NP], F32)
            b1 = sb1("b1", [P, PAIRS], F32)
            b2 = sb1("b2", [P, PAIRS], F32)
            first = sb1("first", [P, 2, NP], F32)
            second = sb1("second", [P, 2, NP], F32)
            row = sb1("row", [HID + 1, 2, D], F32)
            with nc.Block() as block:
                @block.sync
                def _(sp):
                    sp.dma_start(b1[:], g["L2_ffn_b1"]).then_inc(params.sem, 16)
                    sp.dma_start(b2[:], g["L2_ffn_b2"]).then_inc(params.sem, 16)
                    sp.dma_start(bl[:], g["L2_ffn_bl"]).then_inc(params.sem, 16)
                    sp.dma_start(gatesT[:], gates_dram).then_inc(params.sem, 16)
                    sp.wait_ge(cleared.sem, cleared.at(1))
                    waited = m.c["waited"]
                    for p in range(2):
                        load_small(sp, p, p)
                    with sp.Fori(1, PAIRS // 2) as i:
                        for s in range(2):
                            p = 2 * i + s
                            sp.wait_ge(used.sem, used.at(p - 1))
                            sp.sem_inc(waited.sem, 1)
                            sp.wait_ge(g_done.sem, g_done.at(p - 1))
                            sp.sem_inc(waited.sem, 1)
                            load_large(sp, p, s)
                            load_small(sp, p, s)

                @block.tensor
                def _(pe):
                    with pe.Fori(0, PAIRS // 2) as i:
                        for s in range(2):
                            p = 2 * i + s
                            pe.wait_ge(load[s].sem, load[s].at(16 * LOADS * (i + 1)))
                            for c in range(2):
                                for k in range(KD):
                                    ins = nc.tensor.matmul(m.psum[:, c, 0:HALF], w1[:, s, k], m.HT[:, k, c * HALF:(c + 1) * HALF],
                                                           start=(k == 0), stop=(k == KD - 1))
                            ins.then_inc(f_ready.sem, 1)
                            for e in range(2):
                                pe.wait_ge(m_done.sem, m_done.at(2 * p + e - 1))
                                for c in range(2):
                                    for k in range(2):
                                        ins = nc.tensor.matmul(m.psum[0:HID + 1, 4 + 2 * e + c, 0:384], w3[:, s, e, k],
                                                               wl[:, s, e, k, c * 384:(c + 1) * 384], start=(k == 0), stop=(k == 1))
                                ins.then_inc(m_ready.sem, 1)
                            pe.wait_ge(f_done.sem, f_done.at(p + 1))
                            pe.wait_ge(s_done.sem, s_done.at(p))
                            for c in range(2):
                                ins = nc.tensor.matmul(m.psum[:, 2 + c, 0:HALF], w2[:, s], first[:, s, c * HALF:(c + 1) * HALF], start=True, stop=True)
                            ins.then_inc(s_ready.sem, 1)
                            pe.wait_ge(s_ready.sem, s_ready.at(p + 1))
                            pe.sem_inc(used.sem, 1)

                @block.scalar
                def _(act):
                    two = lambda v: v.rearrange("p (c n) -> p c n", c=2)
                    act.wait_ge(params.sem, params.at(64))
                    with act.Fori(0, PAIRS // 2) as i:
                        for s in range(2):
                            p = 2 * i + s
                            act.wait_ge(f_ready.sem, f_ready.at(p + 1))
                            nc.scalar.activation(two(first[:, s]), m.psum[:, 0:2, 0:HALF], ACT.Gelu, bias=b1[:, bass.ds(p, 1)]).then_inc(f_done.sem, 1)
                            for e in range(2):
                                act.wait_ge(m_ready.sem, m_ready.at(2 * p + e + 1))
                                if e == 0:
                                    act.wait_ge(row_out.sem, row_out.at(32 * p))
                                nc.scalar.activation(row[HID:HID + 1, e].rearrange("p (c n) -> p c n", c=2), m.psum[HID:HID + 1, 4 + 2 * e:6 + 2 * e, 0:384], ACT.Copy)
                                nc.scalar.activation(merged[e * HID:(e + 1) * HID, bass.ds(p, 1)].rearrange("p o (c n) -> p (o c) n", c=2),
                                                     m.psum[0:HID, 4 + 2 * e:6 + 2 * e, 0:384], ACT.Copy).then_inc(m_done.sem, 1)
                            act.wait_ge(s_ready.sem, s_ready.at(p + 1))
                            act.wait_ge(g_done.sem, g_done.at(p - 1))
                            nc.scalar.activation(two(second[:, s]), m.psum[:, 2:4, 0:HALF], ACT.Gelu, bias=b2[:, bass.ds(p, 1)]).then_inc(s_done.sem, 1)

                @block.vector
                def _(dve):
                    nc.vector.memset(w2[:], 0.0).then_inc(cleared.sem, 1)
                    with dve.Fori(0, PAIRS // 2) as i:
                        for s in range(2):
                            p = 2 * i + s
                            dve.wait_ge(gates_in[s].sem, gates_in[s].at(32 * (i + 1)))
                            dve.wait_ge(s_done.sem, s_done.at(p + 1))
                            nc.vector.tensor_tensor(gated[:, bass.ds(p, 1)].rearrange("p o n -> p (o n)"), second[:, s], gate[:, s], ALU.mult).then_inc(g_done.sem, 1)

                @block.gpsimd
                def _(pool):
                    with pool.Fori(0, PAIRS // 2) as i:
                        for s in range(2):
                            p = 2 * i + s
                            pool.wait_ge(m_done.sem, m_done.at(2 * p + 2))
                            pool.sem_inc(m.c["waited"].sem, 1)
                            for e in range(2):
                                pool.dma_start(m.bias_rows[bass.ds(2 * p + e, 1)], row[HID:HID + 1, e]).then_inc(row_out.sem, 16)
                    pool.wait_ge(row_out.sem, row_out.at(32 * PAIRS))
            params.close(64), cleared.close(1)
            for s in range(2):
                load[s].close(16 * LOADS * (PAIRS // 2)), gates_in[s].close(32 * (PAIRS // 2))
            row_out.close(32 * PAIRS)
            used.close(PAIRS), f_ready.close(PAIRS), f_done.close(PAIRS), s_ready.close(PAIRS), s_done.close(PAIRS), g_done.close(PAIRS)
            m_ready.close(E), m_done.close(E)
        ready, o_ready, o_saved = (m.c[k] for k in ("rows_ready", "mixed", "mixed_saved"))
        with nc.Block() as block:
            @block.sync
            def _(sp):
                sp.dma_start(bias[:], m.bias_rows).then_inc(params.sem, 16)

            @block.vector
            def _(dve):
                steps = Steps(dve, m.c["dve_step"])
                dve.wait_ge(params.sem, params.at(16))
                nc.vector.tensor_tensor(bias[:], bias[:], bl[:], ALU.add).then_inc(ready.sem, 1)
                for t in range(T):
                    dve.wait_ge(o_ready.sem, o_ready.at(t + 1))
                    two = m.X[:, t].rearrange("p (c w) -> p c w", c=2)
                    nc.vector.tensor_tensor(two, two, m.psum[:, 2 * (t % 2):2 * (t % 2) + 2, 0:384], ALU.add).then_inc(o_saved.sem, 1)
                steps.done()

            @block.tensor
            def _(pe):
                for t in range(T):
                    if t >= 2:
                        pe.wait_ge(o_saved.sem, o_saved.at(t - 1))
                    cols = slice(t * P, (t + 1) * P)
                    for c in range(2):
                        out, of = m.psum[:, 2 * (t % 2) + c, 0:384], slice(c * 384, (c + 1) * 384)
                        for p in range(PAIRS):
                            nc.tensor.matmul(out, gated[:, p, cols], merged[:, p, of], start=(p == 0), stop=False)
                        if t == 0 and c == 0:
                            pe.wait_ge(ready.sem, ready.at(1))
                        ins = nc.tensor.matmul(out, gatesT[:, cols], bias[:, of], start=False, stop=True)
                    ins.then_inc(o_ready.sem, 1)
        params.close(16), ready.close(1), o_ready.close(T), o_saved.close(T)


def gcn_block(nc, m, g):
    with ExitStack() as ctx:
        sb = scratch(nc, m, ctx)
        count = sb("count", [P, T, NP], F32)
        countT = sb("countT", [P, T, NP], F32)
        root = sb("root", [P, T], F32)
        values = sb("values", [P, T, D], F32)
        row = sb("row", [P, 2, D], F32)
        params, ready, v_ready, d_ready = (m.c[k] for k in ("params", "rows_ready", "variance_ready", "deviation_ready"))
        projections = [Projection(nc, m, scratch(nc, m, ctx), [Job(g[f"L3_gnn_W{layer}"], values, scale=root)]) for layer in (1, 2)]
        normalise(nc, m, m.X, m.H, m.eps5, turned=m.HT, ahead=projections[0])
        with nc.Block() as block:
            @block.sync
            def _(sp):
                sp.dma_start(count[:], m.counts[3].rearrange("(t p) s -> p t s", p=P)).then_inc(params.sem, 16)
                for k in range(2):
                    sp.dma_start(row[:, k], g[f"L3_gnn_b{k + 1}"].partition_broadcast(P)).then_inc(params.sem, 16)

            @block.vector
            def _(dve):
                steps = Steps(dve, m.c["dve_step"])
                dve.wait_ge(params.sem, params.at(48))
                for t in range(T):
                    own = count[:, t, t * P:(t + 1) * P]
                    ins = nc.vector.tensor_tensor(own, own, m.ident[:], ALU.add)
                    ins.then_inc(ready.sem, 1)
                dve.wait_ge(ready.sem, ready.at(T))
                steps.then(nc.vector.tensor_reduce(root[:], count[:], AX_X, ALU.add))
                dve.sem_inc(v_ready.sem, 1)
                dve.wait_ge(d_ready.sem, d_ready.at(1))
                steps.then(nc.vector.reciprocal(root[:], root[:]))
                steps.done()

            @block.tensor
            def _(pe):
                turn_rows(nc, m, pe, count)

            @block.scalar
            def _(act):
                save_turned(nc, m, act, countT)
                act.wait_ge(v_ready.sem, v_ready.at(1))
                nc.scalar.activation(root[:], root[:], ACT.Sqrt, bias=m.zero[:]).then_inc(d_ready.sem, 1)
        params.close(48), ready.close(T), close_turn(m, 1), v_ready.close(1), d_ready.close(1)
        o_ready, o_saved = m.c["mixed"], m.c["mixed_saved"]
        for layer in (1, 2):
            projections[layer - 1].run(m.HT)
            with nc.Block() as block:
                if layer == 1:
                    @block.sync
                    def _(sp):
                        projections[1].start(sp)

                @block.tensor
                def _(pe):
                    for t in range(T):
                        if t >= 2:
                            pe.wait_ge(o_saved.sem, o_saved.at(t - 1))
                        for c in range(2):
                            for k in range(T):
                                ins = nc.tensor.matmul(m.psum[:, 4 + 2 * (t % 2) + c, 0:384], countT[:, k, t * P:(t + 1) * P],
                                                       values[:, k, c * 384:(c + 1) * 384], start=(k == 0), stop=(k == T - 1))
                        ins.then_inc(o_ready.sem, 1)
                    if layer == 1:
                        turn_rows(nc, m, pe, m.H)

                @block.vector
                def _(dve):
                    steps = Steps(dve, m.c["dve_step"])
                    for t in range(T):
                        dve.wait_ge(o_ready.sem, o_ready.at(t + 1))
                        two = lambda r: r.rearrange("p (c w) -> p c w", c=2)
                        b = 4 + 2 * (t % 2)
                        steps.then(nc.vector.scalar_tensor_tensor(two(m.H[:, t]), m.psum[:, b:b + 2, 0:384], root[:, t:t + 1],
                                                                  two(row[:, layer - 1]), ALU.mult, ALU.add))
                        dve.sem_inc(o_saved.sem, 1)
                        if layer == 1:
                            nc.vector.tensor_scalar(m.H[:, t], m.H[:, t], 0.0, None, ALU.max).then_inc(ready.sem, 1)
                        else:
                            nc.vector.tensor_tensor(m.X[:, t], m.X[:, t], m.H[:, t], ALU.add)
                    steps.done()

                if layer == 1:
                    @block.scalar
                    def _(act):
                        save_turned(nc, m, act, m.HT)
            o_ready.close(T), o_saved.close(T)
            if layer == 1:
                ready.close(T), close_turn(m, 1)


ROUND = 12582912.0
PAIRS_OF = 2 * NODES


def tiles_bound(experts):
    return (PAIRS_OF - experts) // P + experts


def route_two(nc, m, g, logits, E, mix, share1, share2, alpha, send, fetch, plan, weights):
    NT = tiles_bound(E)
    shape = [P, T, E]
    e_ready, e_done, ready, o_ready = (m.c[k] for k in ("elu_ready", "elu_done", "rows_ready", "mixed"))
    with ExitStack() as ctx:
        sb = scratch(nc, m, ctx)
        work, first, second, prob, chosen, place = (sb(k, shape, F32) for k in ("work", "first", "second", "prob", "chosen", "place"))
        top = sb("top", [P, T, 2], F32)
        total = sb("total", [P, T], F32)
        real = sb("real", [P, T], F32)
        trash = sb("trash", [P, 2, T], F32)
        rows = sb("rows", [P, 2, T], F32)
        tiles, ends, base = (sb(k, [P, E], F32) for k in ("tiles", "ends", "base"))
        passed = sb("passed", [P, NT + 1, E], F32)
        expert = sb("expert", [P, NT + 2], F32)
        spread_ = lambda a: a.to_broadcast(shape)
        with nc.Block() as block:
            @block.sync
            def _(sp):
                sp.dma_start(mix[:], g["L3_ffn_sg_b"].partition_broadcast(P)).then_inc(m.c["params"].sem, 16)
                for name, to in zip(EXPERT_WEIGHTS, weights):
                    sp.dma_start(to[:].rearrange("p k f -> p (k f)"), g[name][0]).then_inc(m.c["first_expert"].sem, 16)

            @block.vector
            def _(dve):
                steps = Steps(dve, m.c["dve_step"])
                do = steps.then
                do(nc.vector.tensor_reduce(top[:, :, 0], logits[:, :, 0:E], AX_X, ALU.max))
                do(nc.vector.tensor_tensor(prob[:], logits[:, :, 0:E], spread_(top[:, :, 0:1]), ALU.subtract))
                dve.sem_inc(e_ready.sem, 1)
                nc.vector.memset(real[:, 0:T - 1], 1.0)
                do(nc.vector.tensor_scalar(real[:, T - 1:T], m.part[:], float(LAST), None, ALU.is_lt))
                nc.vector.memset(trash[:, :, 0:T - 1], 0.0)
                for k in range(2):
                    ins = nc.vector.tensor_scalar(trash[:, k, T - 1:T], real[:, T - 1:T], -1.0, 1.0, ALU.mult, ALU.add)
                do(ins)
                for k in range(2):
                    do(nc.vector.tensor_scalar(top[:, 0, 0:1], m.part[:], float(NT * P - 64 * k), None, ALU.add))
                    do(nc.vector.tensor_tensor(trash[:, k, T - 1:T], trash[:, k, T - 1:T], top[:, 0, 0:1], ALU.mult))
                dve.wait_ge(e_done.sem, e_done.at(1))
                do(nc.vector.tensor_reduce(total[:], prob[:], AX_X, ALU.add))
                do(nc.vector.reciprocal(total[:], total[:]))
                do(nc.vector.tensor_tensor(prob[:], prob[:], spread_(total[:].unsqueeze(2)), ALU.mult))
                first_largest(nc, steps, prob[:], work[:], top, first[:], m.rank)
                do(nc.vector.scalar_tensor_tensor(chosen[:], first[:], -2.0, prob[:], ALU.mult, ALU.add))
                first_largest(nc, steps, chosen[:], work[:], top, second[:], m.rank)
                do(nc.vector.tensor_tensor(chosen[:], first[:], second[:], ALU.add))
                do(nc.vector.tensor_tensor(chosen[:], chosen[:], spread_(real[:].unsqueeze(2)), ALU.mult))
                dve.sem_inc(ready.sem, 1)
                for one_hot, share in ((first, share1), (second, share2)):
                    do(nc.vector.tensor_tensor(work[:], prob[:], one_hot[:], ALU.mult))
                    do(nc.vector.tensor_reduce(share[:], work[:], AX_X, ALU.add))
                do(nc.vector.tensor_tensor(total[:], share1[:], share2[:], ALU.add))
                do(nc.vector.reciprocal(total[:], total[:]))
                do(nc.vector.tensor_scalar(top[:, :, 0], alpha[:], -1.0, 1.0, ALU.mult, ALU.add))
                do(nc.vector.tensor_tensor(total[:], total[:], top[:, :, 0], ALU.mult))
                nc.vector.tensor_tensor(share1[:], share1[:], total[:], ALU.mult)
                do(nc.vector.tensor_tensor(share2[:], share2[:], total[:], ALU.mult))
                dve.wait_ge(o_ready.sem, o_ready.at(1))
                do(nc.vector.tensor_scalar(tiles[:], m.psum[:, 1, 0:E], float(P - 1), 1.0 / P, ALU.add, ALU.mult))
                do(nc.vector.tensor_scalar(tiles[:], tiles[:], -(P - 1) / (2.0 * P), ROUND, ALU.add, ALU.add))
                do(nc.vector.tensor_scalar(tiles[:], tiles[:], -ROUND, None, ALU.add))
                do(nc.vector.memset(base[:], 0.0))
                do(nc.vector.tensor_tensor_scan(ends[:], tiles[:], base[:], 0.0, ALU.add, ALU.add))
                do(nc.vector.tensor_tensor(base[:], ends[:], tiles[:], ALU.subtract))
                do(nc.vector.tensor_scalar(base[:], base[:], float(P), -1.0, ALU.mult, ALU.add))
                nth = m.psum[:, 0, 0:T * E].rearrange("p (t e) -> p t e", t=T)
                do(nc.vector.tensor_tensor(place[:], nth, base[:].unsqueeze(1).to_broadcast(shape), ALU.add))
                for k, one_hot in enumerate((first, second)):
                    do(nc.vector.tensor_tensor(work[:], place[:], one_hot[:], ALU.mult))
                    do(nc.vector.tensor_reduce(rows[:, k], work[:], AX_X, ALU.add))
                    do(nc.vector.tensor_tensor(rows[:, k], rows[:, k], real[:], ALU.mult))
                    nc.vector.tensor_copy(fetch[:, k], rows[:, k])
                    do(nc.vector.tensor_tensor(send[:, k], rows[:, k], trash[:, k], ALU.add))
                whole = [P, NT + 1, E]
                do(nc.vector.tensor_tensor(passed[:], m.rank[:, 0:NT + 1].unsqueeze(2).to_broadcast(whole),
                                           ends[:].unsqueeze(1).to_broadcast(whole), ALU.is_ge))
                nc.vector.memset(expert[:, 0:1], 0.0)
                do(nc.vector.tensor_reduce(expert[:, 1:NT + 2], passed[:], AX_X, ALU.add))
                do(nc.vector.tensor_scalar(expert[:], expert[:], float(E - 1), None, ALU.min))
                nc.vector.tensor_copy(plan[:, :, 0], expert[0:1, 1:NT + 2])
                do(nc.vector.tensor_tensor(plan[:, :, 1], expert[0:1, 1:NT + 2], expert[0:1, 0:NT + 1], ALU.not_equal))
                steps.done()

            @block.scalar
            def _(act):
                act.wait_ge(e_ready.sem, e_ready.at(1))
                nc.scalar.activation(prob[:], prob[:], ACT.Exp, bias=m.zero[:])
                act.wait_ge(m.c["params"].sem, m.c["params"].at(16))
                nc.scalar.activation(alpha[:], logits[:, :, E], ACT.Sigmoid, bias=mix[:]).then_inc(e_done.sem, 1)

            @block.tensor
            def _(pe):
                pe.wait_ge(ready.sem, ready.at(1))
                for t in range(T):
                    for k in range(t + 1):
                        nc.tensor.matmul(m.psum[:, 0, t * E:(t + 1) * E], m.after[:] if k == t else m.ones[:], chosen[:, k],
                                         start=(k == 0), stop=(k == t))
                for t in range(T):
                    ins = nc.tensor.matmul(m.psum[:, 1, 0:E], m.ones[:], chosen[:, t], start=(t == 0), stop=(t == T - 1))
                ins.then_inc(o_ready.sem, 1)
        e_ready.close(1), e_done.close(1), ready.close(1), o_ready.close(1), m.c["params"].close(16)


def gated_experts_block(nc, m, g, out):
    E, HS = 8, 96
    NT = tiles_bound(E)
    with ExitStack() as ctx:
        sb = scratch(nc, m, ctx)
        share1, share2, alpha = (sb(k, [P, T], F32) for k in ("share1", "share2", "alpha"))
        send, fetch = (sb(k, [P, 2, T], U32) for k in ("send", "fetch"))
        plan = sb("plan", [1, NT + 1, 2], I32)
        weights = tuple(sb(k, [P, KD, D], F32) for k in ("gate", "up", "down"))
        with ExitStack() as inner:
            sb1 = scratch(nc, m, inner)
            logits = sb1("logits", [P, T, E + 1], F32)
            sg_b = sb1("sg_b", [P, 1], F32)
            router = Projection(nc, m, sb1, [Job(g["L3_ffn_router_w"], logits)])
            normalise(nc, m, m.X, m.H, m.eps5, turned=m.HT, ahead=router)
            router.run(m.HT)
            route_two(nc, m, g, logits, E, sg_b, share1, share2, alpha, send, fetch, plan, weights)
        send_and_share(nc, m, g, send, alpha, HS)
        expert_tiles(nc, m, g, plan, NT, weights)
        with ExitStack() as inner:
            got = scratch(nc, m, inner)("got", [P, T, 2, D], F32)
            fetched, added, stored = ([m.c[f"pair_{t}"] for t in range(T)], m.c["rows_ready"], m.c["stored"])
            with nc.Block() as block:
                @block.gpsimd
                def _(pool):
                    for t in range(T):
                        for k in range(2):
                            nc.gpsimd.indirect_dma_start(
                                out=got[:, t, k], out_offset=None, in_=m.made,
                                in_offset=bass.IndirectOffsetOnAxis(ap=fetch[:, k, t:t + 1], axis=0)).then_inc(fetched[t].sem, 16)

                @block.vector
                def _(dve):
                    steps = Steps(dve, m.c["dve_step"])
                    for t in range(T):
                        dve.wait_ge(fetched[t].sem, fetched[t].at(32))
                        for k, share in enumerate((share1, share2)):
                            steps.then(nc.vector.scalar_tensor_tensor(m.X[:, t], got[:, t, k], share[:, t:t + 1], m.X[:, t], ALU.mult, ALU.add))
                        dve.sem_inc(added.sem, 1)
                    steps.done()

                @block.sync
                def _(sp):
                    for t in range(T):
                        sp.wait_ge(added.sem, added.at(t + 1))
                        n = P if t < T - 1 else LAST
                        sp.dma_start(out[t * P:t * P + n], m.X[0:n, t]).then_inc(stored.sem, 16)
                    sp.wait_ge(stored.sem, stored.at(16 * T))
            added.close(T), stored.close(16 * T)
            for c in fetched:
                c.close(32)


EXPERT_WEIGHTS = ("L3_ffn_w_gate", "L3_ffn_w_up", "L3_ffn_w_down")


def load_expert(sp, g, name, to, plan, i, counter):
    e = sp.value_load(plan[0:1, bass.ds(i, 1), 0], min_val=0, max_val=7)
    new = sp.value_load(plan[0:1, bass.ds(i, 1), 1], min_val=0, max_val=1)
    source = g[name][bass.ds(e, 1)].rearrange("o p f -> (o p) f")
    sp.dma_start(to[:].rearrange("p k f -> p (k f)"), source, cond=new).then_inc(counter.sem, 16)


def send_and_share(nc, m, g, send, alpha, HS):
    params, g_ready, s_ready, p_ready, d_ready, d_done = (
        m.c[k] for k in ("params", "hidden_ready", "hidden_done", "hidden_used", "second_ready", "second_done"))
    sent = m.c["sent"]
    with ExitStack() as ctx:
        sb = scratch(nc, m, ctx)
        weights = sb("shared_gate_up", [P, 2, KD, HS], F32)
        down = sb("shared_down", [HS, D], F32)
        silu = sb("silu", [HS, NP], F32)
        hidden = sb("hidden", [HS, NP], F32)
        two = lambda v: v.rearrange("p (c n) -> p c n", c=2)
        with nc.Block() as block:
            @block.gpsimd
            def _(pool):
                for k, t in ((k, t) for k in range(2) for t in range(T)):
                    nc.gpsimd.indirect_dma_start(
                        out=m.tokens, out_offset=bass.IndirectOffsetOnAxis(ap=send[:, k, t:t + 1], axis=0),
                        in_=m.H[:, t], in_offset=None).then_inc(sent.sem, 16)
                pool.wait_ge(sent.sem, sent.at(16 * 2 * T))

            @block.sync
            def _(sp):
                sp.dma_start(weights[:, 0], g["L3_ffn_ws_gate"].rearrange("(k p) f -> p k f", p=P)).then_inc(params.sem, 16)
                sp.dma_start(weights[:, 1], g["L3_ffn_ws_up"].rearrange("(k p) f -> p k f", p=P)).then_inc(params.sem, 16)
                sp.dma_start(down[:], g["L3_ffn_ws_down"]).then_inc(params.sem, 16)

            @block.tensor
            def _(pe):
                pe.wait_ge(params.sem, params.at(48))
                for a in range(2):
                    for c in range(2):
                        for k in range(KD):
                            ins = nc.tensor.matmul(m.psum[0:HS, 2 * a + c, 0:HALF], weights[:, a, k], m.HT[:, k, c * HALF:(c + 1) * HALF],
                                                   start=(k == 0), stop=(k == KD - 1))
                    ins.then_inc(g_ready.sem, 1)
                pe.wait_ge(p_ready.sem, p_ready.at(1))
                for t in range(T):
                    if t >= 2:
                        pe.wait_ge(d_done.sem, d_done.at(t - 1))
                    for c in range(2):
                        ins = nc.tensor.matmul(m.psum[:, 4 + 2 * (t % 2) + c, 0:384], hidden[:, t * P:(t + 1) * P],
                                               down[:, c * 384:(c + 1) * 384], start=True, stop=True)
                    ins.then_inc(d_ready.sem, 1)

            @block.scalar
            def _(act):
                act.wait_ge(g_ready.sem, g_ready.at(1))
                nc.scalar.activation(two(silu[:]), m.psum[0:HS, 0:2, 0:HALF], ACT.Silu, bias=m.zero[0:HS]).then_inc(s_ready.sem, 1)

            @block.vector
            def _(dve):
                dve.wait_ge(s_ready.sem, s_ready.at(1))
                dve.wait_ge(g_ready.sem, g_ready.at(2))
                nc.vector.tensor_tensor(two(hidden[:]), two(silu[:]), m.psum[0:HS, 2:4, 0:HALF], ALU.mult).then_inc(p_ready.sem, 1)
                for t in range(T):
                    dve.wait_ge(d_ready.sem, d_ready.at(t + 1))
                    b = 4 + 2 * (t % 2)
                    nc.vector.scalar_tensor_tensor(two(m.X[:, t]), m.psum[:, b:b + 2, 0:384], alpha[:, t:t + 1], two(m.X[:, t]),
                                                   ALU.mult, ALU.add).then_inc(d_done.sem, 1)
        params.close(48), g_ready.close(2), s_ready.close(1), p_ready.close(1), d_ready.close(T), d_done.close(T)
        sent.close(16 * 2 * T)


def expert_tiles(nc, m, g, plan, NT, weights_of_tile):
    gate, up, down = weights_of_tile
    names = ("rows_loaded", "weights_a", "weights_b", "streamed_a", "turned", "turned_saved", "hidden_turned", "hidden_saved",
             "gate_ready", "up_ready", "silu_ready", "hidden_ready", "down_ready", "made_ready")
    x_in, gate_in, up_in, down_in, x_turned, x_saved, h_turned, h_saved, gate_done, up_done, silu_done, h_made, down_done, y_saved = (
        m.c[k] for k in names)
    y_out, waited, early = m.c["made_out"], m.c["waited"], m.c["first_expert"]
    with ExitStack() as ctx:
        sb = scratch(nc, m, ctx)
        rows = sb("token_rows", [P, D], F32)
        columns = sb("token_columns", [P, KD, P], F32)
        silu = sb("silu", [P, D], F32)
        hidden = sb("hidden", [P, D], F32)
        hiddenT = sb("hiddenT", [P, KD, P], F32)
        made = sb("made_rows", [P, D], F32)
        two = lambda v: v.rearrange("p (c n) -> p c n", c=2)
        with nc.Block() as block:
            @block.sync
            def _(sp):
                def after(counter, n):
                    sp.wait_ge(counter.sem, n)
                    sp.sem_inc(waited.sem, 1)

                def load_rows(i):
                    sp.dma_start(rows[:], m.tokens[bass.ds(i * P, P)]).then_inc(x_in.sem, 16)

                def load(i):
                    after(gate_done, gate_done.at(i))
                    load_expert(sp, g, EXPERT_WEIGHTS[0], gate, plan, i, gate_in)
                    after(up_done, up_done.at(i))
                    load_expert(sp, g, EXPERT_WEIGHTS[1], up, plan, i, up_in)
                    after(x_turned, x_turned.at(i + 1))
                    load_rows(i + 1)

                def load_down(i):
                    after(down_done, down_done.at(i))
                    load_expert(sp, g, EXPERT_WEIGHTS[2], down, plan, i, down_in)

                load_rows(0)
                sp.wait_ge(early.sem, early.at(48))
                load(0)
                with sp.Fori(1, NT) as i:
                    load(i)
                    load_down(i - 1)
                load_down(NT - 1)

            @block.tensor
            def _(pe):
                def turn(source, first_bank):
                    for k in range(KD):
                        ins = nc.tensor.transpose(m.psum[:, first_bank + k // 3, (k % 3) * P:(k % 3 + 1) * P], source[:, k * P:(k + 1) * P], m.ident[:])
                    return ins

                def product(left, right, bank):
                    for c in range(2):
                        for k in range(KD):
                            ins = nc.tensor.matmul(m.psum[:, bank + c, 0:384], left[:, k], right[:, k, c * 384:(c + 1) * 384],
                                                   start=(k == 0), stop=(k == KD - 1))
                    return ins

                def turn_tokens(i):
                    pe.wait_ge(x_in.sem, x_in.at(16 * (i + 1)))
                    pe.wait_ge(h_saved.sem, h_saved.at(i - 1))
                    turn(rows, 6).then_inc(x_turned.sem, 1)

                def down_product(i):
                    pe.wait_ge(down_in.sem, down_in.at(16 * (i + 1)))
                    pe.wait_ge(h_saved.sem, h_saved.at(i + 1))
                    pe.wait_ge(y_saved.sem, y_saved.at(i))
                    product(hiddenT, down, 4).then_inc(down_done.sem, 1)

                def tile(i, first=False):
                    pe.wait_ge(gate_in.sem, gate_in.at(16 * (i + 1)))
                    pe.wait_ge(x_saved.sem, x_saved.at(i + 1))
                    pe.wait_ge(silu_done.sem, silu_done.at(i))
                    product(columns, gate, 0).then_inc(gate_done.sem, 1)
                    pe.wait_ge(up_in.sem, up_in.at(16 * (i + 1)))
                    pe.wait_ge(h_made.sem, h_made.at(i))
                    product(columns, up, 2).then_inc(up_done.sem, 1)
                    turn_tokens(i + 1)
                    if not first:
                        down_product(i - 1)
                    pe.wait_ge(h_made.sem, h_made.at(i + 1))
                    pe.wait_ge(x_saved.sem, x_saved.at(i + 2))
                    turn(hidden, 6).then_inc(h_turned.sem, 1)

                turn_tokens(0)
                tile(0, first=True)
                with pe.Fori(1, NT) as i:
                    tile(i)
                down_product(NT - 1)

            @block.scalar
            def _(act):
                with act.Fori(0, NT) as i:
                    act.wait_ge(gate_done.sem, gate_done.at(i + 1))
                    act.wait_ge(h_made.sem, h_made.at(i))
                    nc.scalar.activation(two(silu[:]), m.psum[:, 0:2, 0:384], ACT.Silu, bias=m.zero[:]).then_inc(silu_done.sem, 1)
                    act.wait_ge(h_turned.sem, h_turned.at(i + 1))
                    nc.scalar.activation(hiddenT[:].rearrange("p (c k) n -> p c (k n)", c=2), m.psum[:, 6:8, 0:384], ACT.Copy).then_inc(h_saved.sem, 1)

            @block.vector
            def _(dve):
                def save_tokens(i):
                    dve.wait_ge(x_turned.sem, x_turned.at(i + 1))
                    nc.vector.tensor_copy(columns[:].rearrange("p (c k) n -> p c (k n)", c=2), m.psum[:, 6:8, 0:384]).then_inc(x_saved.sem, 1)

                def save_made(i):
                    dve.wait_ge(down_done.sem, down_done.at(i + 1))
                    dve.wait_ge(y_out.sem, y_out.at(16 * i))
                    nc.vector.tensor_copy(two(made[:]), m.psum[:, 4:6, 0:384]).then_inc(y_saved.sem, 1)

                def tile(i, first=False):
                    save_tokens(i + 1)
                    dve.wait_ge(silu_done.sem, silu_done.at(i + 1))
                    dve.wait_ge(h_turned.sem, h_turned.at(i))
                    nc.vector.tensor_tensor(two(hidden[:]), two(silu[:]), m.psum[:, 2:4, 0:384], ALU.mult).then_inc(h_made.sem, 1)
                    if not first:
                        save_made(i - 1)

                save_tokens(0)
                tile(0, first=True)
                with dve.Fori(1, NT) as i:
                    tile(i)
                save_made(NT - 1)

            @block.gpsimd
            def _(pool):
                with pool.Fori(0, NT) as i:
                    pool.wait_ge(y_saved.sem, y_saved.at(i + 1))
                    pool.sem_inc(waited.sem, 1)
                    pool.dma_start(m.made[bass.ds(i * P, P)], made[:]).then_inc(y_out.sem, 16)
                pool.wait_ge(y_out.sem, y_out.at(16 * NT))
        early.close(48)
        for c in (gate_in, up_in, down_in, y_out):
            c.close(16 * NT)
        x_in.close(16 * (NT + 1)), x_turned.close(NT + 1), x_saved.close(NT + 1)
        for c in (h_turned, h_saved, gate_done, up_done, silu_done, h_made, down_done, y_saved):
            c.close(NT)


def gnn_ffn_kernel(nc, g, out):
    m = Memory()
    m.stage = 0
    with ExitStack() as ctx:
        m.c = {name: Counter(ctx.enter_context(nc.semaphore(name))) for name in COUNTERS}
        m.c |= {name: Counter(ctx.enter_context(nc.semaphore(name)), 0) for name in POOL_DMA_COUNTERS}
        m.psum = ctx.enter_context(nc.psum_tensor("psum", [P, 8, 512], F32))
        one = lambda name, shape, dt: ctx.enter_context(nc.sbuf_tensor(name, shape, dt))
        m.grid = nc.dram_tensor("grid", (NP * NP, 8), F32).ap()
        m.grid1 = nc.dram_tensor("grid1", (NP * NP, 1), F32).ap()
        m.logs = nc.dram_tensor("log_counts", (4, NP, NP), F32).ap()
        m.counts = nc.dram_tensor("counts", (4, NP, NP), F32).ap()
        m.from_dram = {h: nc.dram_tensor(f"from_rows_{h}", (NP, D + h), F32).ap() for h in (8, 1)}
        m.to_dram = {h: nc.dram_tensor(f"to_rows_{h}", (NP, D + h), F32).ap() for h in (8, 1)}
        m.gates32 = nc.dram_tensor("gates_32", (32, NP), F32).ap()
        m.tokens = nc.dram_tensor("tokens", ((tiles_bound(8) + 1) * P, D), F32).ap()
        m.made = nc.dram_tensor("made", (tiles_bound(8) * P, D), F32).ap()
        m.bias_rows = nc.dram_tensor("bias_rows", (32, D), F32).ap()
        setup(nc, m, g, one)
        for block in (gat_v2_block, switch_block, gat_block, quant_block, rgat_block, deep_experts_block, gcn_block):
            block(nc, m, g)
        gated_experts_block(nc, m, g, out)


def host_layout(inputs):
    import numpy as np
    laid = {name: np.asarray(a) for name, a in inputs.items()}
    for name in ("src", "dst", "edge_type_3"):
        padded = np.full((ET * P,), -1, dtype=laid[name].dtype)
        padded[:EDGES] = laid[name]
        laid[name] = padded.reshape(P, ET)
    laid["L2_ffn_gate_w"] = laid["L2_ffn_gate_w"].T
    for name in ("L0_gnn_Wos", "L0_gnn_Wod", "L1_gnn_W1", "L1_gnn_W2", "L2_gnn_W1", "L2_gnn_W2"):
        laid[name + "_turned"] = np.swapaxes(laid[name], -1, -2)
    laid["L0_ffn_wi"] = laid["L0_ffn_wi"].transpose(1, 0, 2).reshape(D, -1)
    laid["L2_ffn_W1"] = laid["L2_ffn_W1"].reshape(16, 2, KD, P, 64).transpose(0, 3, 2, 1, 4).reshape(16, P, -1)
    laid["L2_ffn_W2"] = laid["L2_ffn_W2"].reshape(16, P, 64)
    w3 = np.concatenate([laid["L2_ffn_W3"].transpose(0, 2, 1), laid.pop("L2_ffn_b3")[:, :, None]], axis=2)
    laid["L2_ffn_W3"] = w3.reshape(16, 2, 2, P, 65).transpose(0, 3, 1, 2, 4).reshape(16, P, -1)
    laid["L2_ffn_Wl"] = laid["L2_ffn_Wl"].reshape(16, 2, 2, P, D).transpose(0, 3, 1, 2, 4).reshape(16, P, -1)
    for name in ("L2_ffn_b1", "L2_ffn_b2"):
        laid[name] = laid[name].reshape(16, P).T
    laid["L3_ffn_router_w"] = np.concatenate([laid["L3_ffn_router_w"], laid.pop("L3_ffn_sg_w")], axis=1)
    for name in ("L3_ffn_w_gate", "L3_ffn_w_up", "L3_ffn_w_down"):
        laid[name] = laid[name].reshape(8, KD, P, D).transpose(0, 2, 1, 3).reshape(8, P, -1)
    laid = {name: np.ascontiguousarray(a) for name, a in laid.items()}
    return laid


def kernel(**inputs):
    import concourse.bacc as _bacc
    from concourse.bass_utils import run_bass_kernel_spmd as _run

    nc = _bacc.Bacc("TRN2", target_bir_lowering=False, num_devices=1)
    arrays, g = {}, {}
    for name, a in host_layout(inputs).items():
        arrays[f"in_{name}"] = a
        g[name] = nc.dram_tensor(f"in_{name}", a.shape, mybir.dt.from_np(a.dtype), kind="ExternalInput").ap()
    out = nc.dram_tensor("out_x", (NODES, D), F32, kind="ExternalOutput").ap()
    gnn_ffn_kernel(nc, g, out)
    r = _run(nc, [arrays], core_ids=[0])
    return r.results[0]["out_x"]
```
